# Optimizing a Trainium2 kernel written in Bass

```python
import numpy as np
import jax
import jax.numpy as jnp

def _softmax(x, axis=-1):
    return jax.nn.softmax(x, axis=axis)

def _gelu(x):
    return jax.nn.gelu(x, approximate=True)

def _silu(x):
    return jax.nn.silu(x)

def _sigmoid(x):
    return jax.nn.sigmoid(x)

def _layernorm(x, axis=-1, eps=1e-05):
    m = jnp.mean(x, axis=axis, keepdims=True)
    v = jnp.var(x, axis=axis, keepdims=True)
    return (x - m) / jnp.sqrt(v + eps)

def _scatter_add(tgt, idx, src, axis=0):
    return tgt.at[idx].add(src)

def _segment_sum(src, seg, n):
    return jax.ops.segment_sum(src, seg, n)
kernel_name = 'mk_gnn_preln_d4_gnn_r16_a6792f'

def setup_inputs(seed: int=0):
    np.random.seed(seed)
    _w = jnp.asarray

    def _rec_inputs():
        import jax
        import jax.numpy as jnp
        _gk = jax.random.key(seed)
        x = -0.0003713 + 1 * jax.random.normal(jax.random.fold_in(_gk, 1), (6250, 128), jnp.float32)
        src = jax.random.randint(jax.random.fold_in(_gk, 2), (100000,), 0, 6250, jnp.int32)
        dst = jax.random.randint(jax.random.fold_in(_gk, 3), (100000,), 0, 6250, jnp.int32)
        _o = jnp.argsort(dst, stable=True)
        src = src[_o]
        dst = dst[_o]
        edge_attr_32 = 0.000196303 + 1.00016 * jax.random.normal(jax.random.fold_in(_gk, 12), (100000, 32), jnp.float32)
        return (x, src, dst, edge_attr_32)
    x, src, dst, edge_attr_32 = _rec_inputs()

    def _L0_gnn_setup():
        import jax, jax.numpy as jnp
        import numpy as np
        N = 6250
        E_RAND = 100000
        D_IN = 128
        D_H = 128
        NUM_LAYERS = 2
        BN_EPS = 1e-05

        def _batchnorm(x, g, b):
            mean = jnp.mean(x, axis=0)
            var = jnp.mean(jnp.square(x - mean), axis=0)
            return (x - mean) * jax.lax.rsqrt(var + BN_EPS) * g + b

        def _gcn_forward(feats, row, col, params):
            h = feats
            inv_deg = None
            for l in range(NUM_LAYERS):
                pooled = jax.ops.segment_sum(h[col], row, num_segments=N)
                if inv_deg is None:
                    deg = jax.ops.segment_sum(jnp.ones((row.shape[0],), h.dtype), row, num_segments=N)
                    inv_deg = (1.0 / deg)[:, None]
                pooled = pooled * inv_deg
                W0, b0, W1, b1, mg, mb, g, b = params[l]
                x = pooled @ W0 + b0
                x = jax.nn.relu(_batchnorm(x, mg, mb))
                x = x @ W1 + b1
                h = jax.nn.relu(_batchnorm(x, g, b))
            return h
        key = jax.random.key(seed)
        ks = jax.random.split(key, 32)
        feats = jax.random.normal(ks[0], (N, D_IN), dtype=jnp.float32)
        row = jnp.concatenate([jax.random.randint(ks[1], (E_RAND,), 0, N, dtype=jnp.int32), jnp.arange(N, dtype=jnp.int32)])
        col = jnp.concatenate([jax.random.randint(ks[2], (E_RAND,), 0, N, dtype=jnp.int32), jnp.arange(N, dtype=jnp.int32)])
        inp = {'feats': feats, 'row': row, 'col': col}
        k = 3
        for l in range(NUM_LAYERS):
            din = D_IN if l == 0 else D_H
            s = 1.0 / np.sqrt(din)
            inp[f'l{l}_W0'] = jax.random.uniform(ks[k], (din, D_H), jnp.float32, -s, s)
            k += 1
            inp[f'l{l}_b0'] = jnp.zeros((D_H,), jnp.float32)
            sh = 1.0 / np.sqrt(D_H)
            inp[f'l{l}_W1'] = jax.random.uniform(ks[k], (D_H, D_H), jnp.float32, -sh, sh)
            k += 1
            inp[f'l{l}_b1'] = jnp.zeros((D_H,), jnp.float32)
            inp[f'l{l}_mbn_g'] = jnp.ones((D_H,), jnp.float32)
            inp[f'l{l}_mbn_b'] = jnp.zeros((D_H,), jnp.float32)
            inp[f'l{l}_bn_g'] = jnp.ones((D_H,), jnp.float32)
            inp[f'l{l}_bn_b'] = jnp.zeros((D_H,), jnp.float32)
        return inp
    _L0_gnn_all = _L0_gnn_setup()
    _L0_gnn_in = {k: v for k, v in _L0_gnn_all.items() if k in ('l0_W0', 'l0_b0', 'l0_W1', 'l0_b1', 'l0_mbn_g', 'l0_mbn_b', 'l0_bn_g', 'l0_bn_b', 'l1_W0', 'l1_b0', 'l1_W1', 'l1_b1', 'l1_mbn_g', 'l1_mbn_b', 'l1_bn_g', 'l1_bn_b')}
    del _L0_gnn_all

    def _L1_gnn_setup():
        import jax, jax.numpy as jnp
        import numpy as np
        N_NODES = 6250
        N_EDGES = 100000
        D_IN = 128
        D_HID = 128
        N_LAYERS = 4

        def _sage_layer(h, src, dst, Ws, Wn, b):
            deg = jax.ops.segment_sum(jnp.ones_like(dst, dtype=h.dtype), dst, num_segments=N_NODES)
            agg = jax.ops.segment_sum(h[src], dst, num_segments=N_NODES)
            agg = agg / jnp.maximum(deg, 1.0)[:, None]
            return h @ Ws + agg @ Wn + b
        key = jax.random.key(seed)
        ks = jax.random.split(key, 7)
        x = jax.random.normal(ks[0], (N_NODES, D_IN), dtype=jnp.float32)
        src = jax.random.randint(ks[1], (N_EDGES,), 0, N_NODES, dtype=jnp.int32)
        dst = jax.random.randint(ks[2], (N_EDGES,), 0, N_NODES, dtype=jnp.int32)
        scale = 1.0 / np.sqrt(D_IN)
        W_self = jax.random.normal(ks[3], (N_LAYERS, D_IN, D_HID), dtype=jnp.float32) * scale
        W_neigh = jax.random.normal(ks[4], (N_LAYERS, D_IN, D_HID), dtype=jnp.float32) * scale
        bias = jnp.zeros((N_LAYERS, D_HID), dtype=jnp.float32)
        return {'x': x, 'src': src, 'dst': dst, 'W_self': W_self, 'W_neigh': W_neigh, 'bias': bias}
    _L1_gnn_all = _L1_gnn_setup()
    _L1_gnn_in = {k: v for k, v in _L1_gnn_all.items() if k in ('W_self', 'W_neigh', 'bias')}
    del _L1_gnn_all

    def _L2_gnn_setup():
        import jax, jax.numpy as jnp
        import numpy as np
        N_NODES = 6250
        N_EDGES = 50000
        NODE_DIM = 128
        EDGE_DIM = 32
        MSG_DIM = 128
        EPS = 1e-05

        def layer_norm(x, g, b):
            mu = jnp.mean(x, axis=-1, keepdims=True)
            var = jnp.var(x, axis=-1, keepdims=True)
            return (x - mu) * jax.lax.rsqrt(var + EPS) * g + b

        def he_normal(key, shape):
            fan_in = shape[1]
            return jax.random.normal(key, shape, dtype=jnp.float32) * np.sqrt(2.0 / fan_in)
        key = jax.random.key(seed)
        ks = jax.random.split(key, 8)
        nodes = jax.random.normal(ks[0], (N_NODES, NODE_DIM), dtype=jnp.float32)
        edge_index = jax.random.randint(ks[1], (2, N_EDGES), 0, N_NODES, dtype=jnp.int64)
        edge_attr = jax.random.normal(ks[2], (N_EDGES, EDGE_DIM), dtype=jnp.float32)
        W_message = he_normal(ks[3], (MSG_DIM, NODE_DIM + EDGE_DIM))
        W_node = he_normal(ks[4], (NODE_DIM, NODE_DIM))
        W1 = he_normal(ks[5], (NODE_DIM, NODE_DIM + MSG_DIM))
        b1 = jnp.zeros((NODE_DIM,), dtype=jnp.float32)
        ln1_g = jnp.ones((NODE_DIM,), dtype=jnp.float32)
        ln1_b = jnp.zeros((NODE_DIM,), dtype=jnp.float32)
        W2 = he_normal(ks[6], (NODE_DIM, NODE_DIM))
        b2 = jnp.zeros((NODE_DIM,), dtype=jnp.float32)
        ln2_g = jnp.ones((NODE_DIM,), dtype=jnp.float32)
        ln2_b = jnp.zeros((NODE_DIM,), dtype=jnp.float32)
        ln_g = jnp.ones((NODE_DIM,), dtype=jnp.float32)
        ln_b = jnp.zeros((NODE_DIM,), dtype=jnp.float32)
        return {'nodes': nodes, 'edge_index': edge_index, 'edge_attr': edge_attr, 'W_message': W_message, 'W_node': W_node, 'W1': W1, 'b1': b1, 'ln1_g': ln1_g, 'ln1_b': ln1_b, 'W2': W2, 'b2': b2, 'ln2_g': ln2_g, 'ln2_b': ln2_b, 'ln_g': ln_g, 'ln_b': ln_b}
    _L2_gnn_all = _L2_gnn_setup()
    _L2_gnn_in = {k: v for k, v in _L2_gnn_all.items() if k in ('W_message', 'W_node', 'W1', 'b1', 'ln1_g', 'ln1_b', 'W2', 'b2', 'ln2_g', 'ln2_b', 'ln_g', 'ln_b')}
    del _L2_gnn_all

    def _L3_gnn_setup():
        import jax, jax.numpy as jnp
        import numpy as np
        N = 3125
        E = 50000
        D = 128
        key = jax.random.key(seed)
        k0, k1, k2, k3, k4, k5 = jax.random.split(key, 6)
        x = jax.random.normal(k0, (N, D), dtype=jnp.float32)
        edge_index = jax.random.randint(k1, (2, E), 0, N, dtype=jnp.int32)
        scale = 1.0 / np.sqrt(D)
        W1 = jax.random.normal(k2, (D, D), dtype=jnp.float32) * scale
        b1 = jax.random.normal(k3, (D,), dtype=jnp.float32) * 0.01
        W2 = jax.random.normal(k4, (D, D), dtype=jnp.float32) * scale
        b2 = jax.random.normal(k5, (D,), dtype=jnp.float32) * 0.01
        return {'x': x, 'edge_index': edge_index, 'W1': W1, 'b1': b1, 'W2': W2, 'b2': b2}
    _L3_gnn_all = _L3_gnn_setup()
    _L3_gnn_in = {k: v for k, v in _L3_gnn_all.items() if k in ('W1', 'b1', 'W2', 'b2')}
    del _L3_gnn_all
    return {'x': x, 'src': src, 'dst': dst, 'edge_attr_32': edge_attr_32, 'L0_gnn_l0_W0': _L0_gnn_in['l0_W0'], 'L0_gnn_l0_b0': _L0_gnn_in['l0_b0'], 'L0_gnn_l0_W1': _L0_gnn_in['l0_W1'], 'L0_gnn_l0_b1': _L0_gnn_in['l0_b1'], 'L0_gnn_l0_mbn_g': _L0_gnn_in['l0_mbn_g'], 'L0_gnn_l0_mbn_b': _L0_gnn_in['l0_mbn_b'], 'L0_gnn_l0_bn_g': _L0_gnn_in['l0_bn_g'], 'L0_gnn_l0_bn_b': _L0_gnn_in['l0_bn_b'], 'L0_gnn_l1_W0': _L0_gnn_in['l1_W0'], 'L0_gnn_l1_b0': _L0_gnn_in['l1_b0'], 'L0_gnn_l1_W1': _L0_gnn_in['l1_W1'], 'L0_gnn_l1_b1': _L0_gnn_in['l1_b1'], 'L0_gnn_l1_mbn_g': _L0_gnn_in['l1_mbn_g'], 'L0_gnn_l1_mbn_b': _L0_gnn_in['l1_mbn_b'], 'L0_gnn_l1_bn_g': _L0_gnn_in['l1_bn_g'], 'L0_gnn_l1_bn_b': _L0_gnn_in['l1_bn_b'], 'L1_gnn_W_self': _L1_gnn_in['W_self'], 'L1_gnn_W_neigh': _L1_gnn_in['W_neigh'], 'L1_gnn_bias': _L1_gnn_in['bias'], 'L2_gnn_W_message': _L2_gnn_in['W_message'], 'L2_gnn_W_node': _L2_gnn_in['W_node'], 'L2_gnn_W1': _L2_gnn_in['W1'], 'L2_gnn_b1': _L2_gnn_in['b1'], 'L2_gnn_ln1_g': _L2_gnn_in['ln1_g'], 'L2_gnn_ln1_b': _L2_gnn_in['ln1_b'], 'L2_gnn_W2': _L2_gnn_in['W2'], 'L2_gnn_b2': _L2_gnn_in['b2'], 'L2_gnn_ln2_g': _L2_gnn_in['ln2_g'], 'L2_gnn_ln2_b': _L2_gnn_in['ln2_b'], 'L2_gnn_ln_g': _L2_gnn_in['ln_g'], 'L2_gnn_ln_b': _L2_gnn_in['ln_b'], 'L3_gnn_W1': _L3_gnn_in['W1'], 'L3_gnn_b1': _L3_gnn_in['b1'], 'L3_gnn_W2': _L3_gnn_in['W2'], 'L3_gnn_b2': _L3_gnn_in['b2']}

def reference(x, src, dst, edge_attr_32, L0_gnn_l0_W0, L0_gnn_l0_b0, L0_gnn_l0_W1, L0_gnn_l0_b1, L0_gnn_l0_mbn_g, L0_gnn_l0_mbn_b, L0_gnn_l0_bn_g, L0_gnn_l0_bn_b, L0_gnn_l1_W0, L0_gnn_l1_b0, L0_gnn_l1_W1, L0_gnn_l1_b1, L0_gnn_l1_mbn_g, L0_gnn_l1_mbn_b, L0_gnn_l1_bn_g, L0_gnn_l1_bn_b, L1_gnn_W_self, L1_gnn_W_neigh, L1_gnn_bias, L2_gnn_W_message, L2_gnn_W_node, L2_gnn_W1, L2_gnn_b1, L2_gnn_ln1_g, L2_gnn_ln1_b, L2_gnn_W2, L2_gnn_b2, L2_gnn_ln2_g, L2_gnn_ln2_b, L2_gnn_ln_g, L2_gnn_ln_b, L3_gnn_W1, L3_gnn_b1, L3_gnn_W2, L3_gnn_b2):
    import jax
    import jax.numpy as jnp

    def _L0_gnn_ref(feats, row, col, l0_W0, l0_b0, l0_W1, l0_b1, l0_mbn_g, l0_mbn_b, l0_bn_g, l0_bn_b, l1_W0, l1_b0, l1_W1, l1_b1, l1_mbn_g, l1_mbn_b, l1_bn_g, l1_bn_b):
        import jax, jax.numpy as jnp
        import numpy as np
        N = 6250
        E_RAND = 100000
        D_IN = 128
        D_H = 128
        NUM_LAYERS = 2
        BN_EPS = 1e-05

        def _batchnorm(x, g, b):
            mean = jnp.mean(x, axis=0)
            var = jnp.mean(jnp.square(x - mean), axis=0)
            return (x - mean) * jax.lax.rsqrt(var + BN_EPS) * g + b

        def _gcn_forward(feats, row, col, params):
            h = feats
            inv_deg = None
            for l in range(NUM_LAYERS):
                pooled = jax.ops.segment_sum(h[col], row, num_segments=N)
                if inv_deg is None:
                    deg = jax.ops.segment_sum(jnp.ones((row.shape[0],), h.dtype), row, num_segments=N)
                    inv_deg = (1.0 / deg)[:, None]
                pooled = pooled * inv_deg
                W0, b0, W1, b1, mg, mb, g, b = params[l]
                x = pooled @ W0 + b0
                x = jax.nn.relu(_batchnorm(x, mg, mb))
                x = x @ W1 + b1
                h = jax.nn.relu(_batchnorm(x, g, b))
            return h
        params = [(l0_W0, l0_b0, l0_W1, l0_b1, l0_mbn_g, l0_mbn_b, l0_bn_g, l0_bn_b), (l1_W0, l1_b0, l1_W1, l1_b1, l1_mbn_g, l1_mbn_b, l1_bn_g, l1_bn_b)]
        return _gcn_forward(feats, row, col, params)

    def _L1_gnn_ref(x, src, dst, W_self, W_neigh, bias):
        import jax, jax.numpy as jnp
        import numpy as np
        N_NODES = 6250
        N_EDGES = 100000
        D_IN = 128
        D_HID = 128
        N_LAYERS = 4

        def _sage_layer(h, src, dst, Ws, Wn, b):
            deg = jax.ops.segment_sum(jnp.ones_like(dst, dtype=h.dtype), dst, num_segments=N_NODES)
            agg = jax.ops.segment_sum(h[src], dst, num_segments=N_NODES)
            agg = agg / jnp.maximum(deg, 1.0)[:, None]
            return h @ Ws + agg @ Wn + b
        h = x
        for l in range(N_LAYERS):
            h = _sage_layer(h, src, dst, W_self[l], W_neigh[l], bias[l])
            if l != N_LAYERS - 1:
                h = jax.nn.relu(h)
        return h

    def _L2_gnn_ref(nodes, edge_index, edge_attr, W_message, W_node, W1, b1, ln1_g, ln1_b, W2, b2, ln2_g, ln2_b, ln_g, ln_b):
        import jax, jax.numpy as jnp
        import numpy as np
        N_NODES = 6250
        N_EDGES = 50000
        NODE_DIM = 128
        EDGE_DIM = 32
        MSG_DIM = 128
        EPS = 1e-05

        def layer_norm(x, g, b):
            mu = jnp.mean(x, axis=-1, keepdims=True)
            var = jnp.var(x, axis=-1, keepdims=True)
            return (x - mu) * jax.lax.rsqrt(var + EPS) * g + b

        def he_normal(key, shape):
            fan_in = shape[1]
            return jax.random.normal(key, shape, dtype=jnp.float32) * np.sqrt(2.0 / fan_in)
        senders, receivers = (edge_index[0], edge_index[1])
        n_nodes = nodes.shape[0]
        sender_features = nodes[senders]
        message_input = jnp.concatenate([sender_features, edge_attr], -1)
        messages = message_input @ W_message.T
        aggregated = jax.ops.segment_sum(messages, receivers, num_segments=n_nodes)
        node_input = jnp.concatenate([nodes, aggregated], -1)
        h = layer_norm(jax.nn.relu(node_input @ W1.T + b1), ln1_g, ln1_b)
        node_out = layer_norm(jax.nn.relu(h @ W2.T + b2), ln2_g, ln2_b)
        return layer_norm(nodes @ W_node.T + node_out, ln_g, ln_b)

    def _L3_gnn_ref(x, edge_index, W1, b1, W2, b2):
        import jax, jax.numpy as jnp
        import numpy as np
        N = 3125
        E = 50000
        D = 128
        n = x.shape[0]
        src, dst = (edge_index[0], edge_index[1])
        loops = jnp.arange(n, dtype=src.dtype)
        s = jnp.concatenate([src, loops])
        d = jnp.concatenate([dst, loops])
        deg = jax.ops.segment_sum(jnp.ones_like(d, dtype=x.dtype), d, num_segments=n)
        dinv = jnp.where(deg > 0, jax.lax.rsqrt(deg), 0.0)
        ew = dinv[s] * dinv[d]

        def gcn_conv(h, W, b):
            h = h @ W
            msg = ew[:, None] * h[s]
            agg = jax.ops.segment_sum(msg, d, num_segments=n)
            return agg + b
        h = jax.nn.elu(gcn_conv(x, W1, b1))
        out = jax.nn.elu(gcn_conv(h, W2, b2))
        return out
    edge_index = jnp.stack([src, dst])
    h = jnp.maximum(_layernorm(x, axis=-1), 0.0)
    x = x + _L0_gnn_ref(h, src, dst, L0_gnn_l0_W0, L0_gnn_l0_b0, L0_gnn_l0_W1, L0_gnn_l0_b1, L0_gnn_l0_mbn_g, L0_gnn_l0_mbn_b, L0_gnn_l0_bn_g, L0_gnn_l0_bn_b, L0_gnn_l1_W0, L0_gnn_l1_b0, L0_gnn_l1_W1, L0_gnn_l1_b1, L0_gnn_l1_mbn_g, L0_gnn_l1_mbn_b, L0_gnn_l1_bn_g, L0_gnn_l1_bn_b)
    h = jnp.maximum(_layernorm(x, axis=-1), 0.0)
    x = x + _L1_gnn_ref(h, src, dst, L1_gnn_W_self, L1_gnn_W_neigh, L1_gnn_bias)
    h = jnp.maximum(_layernorm(x, axis=-1), 0.0)
    x = x + _L2_gnn_ref(h, edge_index, edge_attr_32, L2_gnn_W_message, L2_gnn_W_node, L2_gnn_W1, L2_gnn_b1, L2_gnn_ln1_g, L2_gnn_ln1_b, L2_gnn_W2, L2_gnn_b2, L2_gnn_ln2_g, L2_gnn_ln2_b, L2_gnn_ln_g, L2_gnn_ln_b)
    h = jnp.maximum(_layernorm(x, axis=-1), 0.0)
    x = x + _L3_gnn_ref(h, edge_index, L3_gnn_W1, L3_gnn_b1, L3_gnn_W2, L3_gnn_b2)
    return x

_drawn_inputs = setup_inputs


def setup_inputs(seed=0):
    import zlib

    import numpy as np

    out = dict(_drawn_inputs(seed))
    spreads = {'L0_gnn_l0_b0': (0.0, 2.0),
     'L0_gnn_l0_b1': (0.0, 2.0),
     'L0_gnn_l0_mbn_g': (1.0, 0.2),
     'L0_gnn_l0_mbn_b': (0.0, 0.1),
     'L0_gnn_l0_bn_g': (1.0, 0.2),
     'L0_gnn_l0_bn_b': (0.0, 0.1),
     'L0_gnn_l1_b0': (0.0, 2.0),
     'L0_gnn_l1_b1': (0.0, 2.0),
     'L0_gnn_l1_mbn_g': (1.0, 0.2),
     'L0_gnn_l1_mbn_b': (0.0, 0.1),
     'L0_gnn_l1_bn_g': (1.0, 0.2),
     'L0_gnn_l1_bn_b': (0.0, 0.1),
     'L1_gnn_bias': (0.0, 0.1),
     'L2_gnn_b1': (0.0, 0.8),
     'L2_gnn_ln1_g': (1.0, 0.2),
     'L2_gnn_ln1_b': (0.0, 0.1),
     'L2_gnn_b2': (0.0, 0.268),
     'L2_gnn_ln2_g': (1.0, 0.2),
     'L2_gnn_ln2_b': (0.0, 0.1),
     'L2_gnn_ln_g': (1.0, 0.2),
     'L2_gnn_ln_b': (0.0, 0.1)}
    factors = {'L3_gnn_b1': 8.0, 'L3_gnn_b2': 8.0}
    for name, (base, spread) in spreads.items():
        noise = np.random.default_rng([zlib.crc32(name.encode()), seed]).standard_normal(out[name].shape)
        drawn = base * np.exp(spread * noise) if base else spread * noise
        out[name] = jnp.asarray(drawn.astype(out[name].dtype))
    for name, factor in factors.items():
        out[name] = (out[name] * factor).astype(out[name].dtype)
    return out
```

```python
from contextlib import ExitStack

import concourse.bass as bass
from concourse import mybir

F32 = mybir.dt.float32
F16 = mybir.dt.float16
BF16 = mybir.dt.bfloat16
I32 = mybir.dt.int32
ALU = mybir.AluOpType
ACT = mybir.ActivationFunctionType
AX = mybir.AxisListType.X

P = 128
D = 128
N = 6250
E = 100000
DE = 32
EPS = 1e-5

SRC_W = 128
DST_W = 224
NS = -(-N // SRC_W)
ND = -(-N // DST_W)
NP = NS * SRC_W
DST_H = DST_W // 2
US = 7
UD = 4
UB = US * UD
STRIP = US * SRC_W
NU = NP // STRIP
HALF = STRIP // 2
NBKT = NS * ND
CAP = 128
assert NP == ND * DST_W and STRIP == UD * DST_W and NP == NU * STRIP

COLS = 784
GR = 8
NG = COLS // GR
LASTP = E // COLS
LASTC = E - LASTP * COLS
FULLP = 112
PW = 2 + DE
FAR = 8000
BIG = float(1 << 20)

LN_SCALE = 12
CH = HALF
NCH = NP // CH
LASTCH = N - (NCH - 1) * CH


class Sem:

    def __init__(self, handle):
        self.h = handle
        self.base = 0

    def at(self, value):
        return self.base + value

    def due(self, value):
        return not isinstance(value, int) or self.base + value > 0


def cols(c, w=CH):
    return bass.ds(c * w, w)


def chunk_pairs(eng, body):
    with eng.Fori(0, NCH // 2) as q:
        for b in range(2):
            body(q * 2 + b, b)


class Core:

    def __init__(self, nc, ctx):
        self.nc = nc
        self.ctx = ctx
        self.sems = {}
        self.n = 0

    def sem(self, name):
        if name not in self.sems:
            self.sems[name] = Sem(self.ctx.enter_context(self.nc.semaphore(name)))
        return self.sems[name]

    def next(self):
        self.n += 1
        return self.n

    def advance(self, **totals):
        for name, n in totals.items():
            self.sems[name].base += n


def constants(k):
    nc = k.nc
    fill = k.sem("fill")
    with nc.Block() as block:
        @block.gpsimd
        def _(pool):
            g = nc.gpsimd
            g.iota(k.iota[:, :], [[1, 256]], base=0, channel_multiplier=0, allow_small_or_imprecise_dtypes=True)
            for m in (k.id16, k.idb, k.idf):
                g.memset(m[:, :], 0.0).then_inc(fill.h, 1)
            g.memset(k.tri[:, :], 1.0).then_inc(fill.h, 1)
            g.memset(k.avg[:, :], 1.0 / D)
            g.memset(k.gather[:, :, :], 1.0 / D).then_inc(fill.h, 1)
            g.memset(k.spread[:, :, :], 1.0).then_inc(fill.h, 1)
            g.memset(k.eps[:, :], EPS)
            g.memset(k.zero[:, :], 0.0)
            pool.wait_ge(fill.h, fill.at(6))
            g.affine_select(out=k.gather[:, :, :], in_=k.gather[:, :, :], compare_op=ALU.is_equal, fill=0.0, base=0,
                            pattern=[[-1, NCH], [1, NCH]], channel_multiplier=0)
            g.affine_select(out=k.spread[:, :, :], in_=k.spread[:, :, :], compare_op=ALU.is_equal, fill=0.0, base=0,
                            pattern=[[-1, NCH], [0, D]], channel_multiplier=1)
            for m in (k.id16, k.idb, k.idf):
                g.affine_select(out=m[:, :], in_=m[:, :], compare_op=ALU.not_equal, fill=1.0, base=0,
                                pattern=[[-1, P]], channel_multiplier=1)
            g.affine_select(out=k.tri[:, :], in_=k.tri[:, :], compare_op=ALU.is_gt, fill=0.0, base=0,
                            pattern=[[-1, P]], channel_multiplier=1)


def rank_edges(k, src, dst, ea):
    nc = k.nc
    with ExitStack() as ctx:
        def sb(name, shape, dt):
            return ctx.enter_context(nc.sbuf_tensor(name, shape, dt))

        def ps(name, shape, dt):
            return ctx.enter_context(nc.psum_tensor(name, shape, dt))

        pay = sb("pay", [P, COLS, PW], F32)
        ring = sb("ring", [P, 2, GR, PW], F32)
        si = sb("si", [P, COLS], I32)
        di = sb("di", [P, COLS], I32)
        ti = sb("ti", [P, COLS], I32)
        tj = sb("tj", [P, COLS], I32)
        srcb = sb("srcb", [P, COLS], F32)
        dstw = sb("dstw", [P, COLS], F32)
        srcl = sb("srcl", [P, COLS], F32)
        dstl = sb("dstl", [P, COLS], F32)
        keyf = sb("keyf", [P, COLS], F32)
        key16 = sb("key16", [P, COLS], F16)
        rowbase = sb("rowbase", [P, COLS], F32)
        row = sb("row", [P, 2 * GR], I32)
        parts = sb("parts", [P, 2, 2, GR], F32)
        rank = sb("rank", [P, GR], F32)
        hot = sb("hot", [P, 4, 64 + ND + SRC_W + DST_W], BF16)
        dneg = sb("dneg", [P, COLS], F32)
        away = sb("away", [P, 2, DST_W], BF16)
        H_DW, H_SL, H_DL, H_END = 64, 64 + ND, 64 + ND + SRC_W, 64 + ND + SRC_W + DST_W
        blockT = sb("blockT", [64, 2, P], BF16)
        before = sb("before", [64, 2, ND], BF16)
        junk = sb("junk", [P, 2 * GR, P], F32)
        over = sb("over", [P, COLS], F32)
        oven = sb("oven", [P, 2], F32)
        oveni = sb("oveni", [1, 1], I32)
        empty = sb("empty", [P, 98, PW], F32)
        zeros = sb("zeros", [P, 256], BF16)
        degs = sb("degs", [NS, SRC_W], F32)
        degd = sb("degd", [ND, DST_W], F32)
        t3 = sb("t3", [ND, DST_W], F32)
        cnt_s = ps("cnt_s", [P, 512], F32)
        cnt_d = ps("cnt_d", [P, 512], F32)
        keys = [ps(f"keys{b}", [P, 512], F32) for b in range(2)]
        look = [ps(f"look{b}", [P, 512], F32) for b in range(2)]
        flip = [ps(f"flip{b}", [P, 1024], BF16) for b in range(2)]

        idx_in, slots_init = k.sem("idx_in"), k.sem("slots_init")
        ea_in = [k.sem(f"ea_in{i}") for i in range(COLS // FULLP)]
        pads_set, empty_set, chain = k.sem("pads_set"), k.sem("empty_set"), k.sem("chain")
        dhot_step = k.sem("dhot_step")
        prepped, hot_ready, keyrow = k.sem("prepped"), k.sem("hot_ready"), k.sem("keyrow")
        flipped, counted, snapped = k.sem("flipped"), k.sem("counted"), k.sem("snapped")
        flip_copied, looked = k.sem("flip_copied"), k.sem("looked")
        within_done, base_done = k.sem("within_done"), k.sem("base_done")
        rows_ready, row_read, ring_full = k.sem("rows_ready"), k.sem("row_read"), k.sem("ring_full")
        scattered = [k.sem("scattered0"), k.sem("scattered1")]
        turn, deg_out, deg_ready, deg_pads = k.sem("turn"), k.sem("deg_out"), k.sem("deg_ready"), k.sem("deg_pads")
        tail, rooted, spill, spill_no = k.sem("tail"), k.sem("rooted"), k.sem("spill"), k.sem("spill_no")

        with nc.Block() as block:
            @block.sync
            def _(sp):
                sp.wait_ge(pads_set.h, pads_set.at(2))
                for a, t in ((src, si), (dst, di)):
                    for p0, p1 in ((0, FULLP), (FULLP, LASTP)):
                        sp.dma_start(t[p0:p1, :], a[p0 * COLS:p1 * COLS].rearrange("(p c) -> p c", c=COLS)
                                     ).then_inc(idx_in.h, 16)
                    sp.dma_start(t[LASTP:P, 0:LASTC], a[LASTP * COLS:E].rearrange("(p c) -> p c", p=1)
                                 ).then_inc(idx_in.h, 16)
                sp.wait_ge(empty_set.h, empty_set.at(2))
                flat = k.slots.rearrange("(p r) w -> p r w", p=P)
                for q in range(NBKT // 98):
                    sp.dma_start(flat[:, q * 98:(q + 1) * 98, :], empty[:, :, :]).then_inc(slots_init.h, 16)
                sp.wait_ge(deg_ready.h, deg_ready.at(3))
                sp.dma_start(k.factors[0].rearrange("(p c) -> p c", c=SRC_W), degs[:, :]).then_inc(deg_out.h, 16)
                sp.dma_start(k.factors[1].rearrange("(p c) -> p c", c=DST_W), degd[:, :]).then_inc(deg_out.h, 16)
                sp.dma_start(k.factors[2].rearrange("(p c) -> p c", c=DST_W), t3[:, :]).then_inc(deg_out.h, 16)
                sp.wait_ge(deg_out.h, deg_out.at(48))
                sp.wait_ge(base_done.h, base_done.at(COLS))
                for p0, p1 in ((0, FULLP), (FULLP, LASTP)):
                    sp.dma_start(si[p0:p1, :], src[p0 * COLS:p1 * COLS].rearrange("(p c) -> p c", c=COLS)
                                 ).then_inc(idx_in.h, 16)
                sp.dma_start(si[LASTP:P, 0:LASTC], src[LASTP * COLS:E].rearrange("(p c) -> p c", p=1)
                             ).then_inc(idx_in.h, 16)
                sp.wait_ge(spill.h, spill.at(6))
                sp.dma_start(k.spill_src, si[:, :]).then_inc(deg_out.h, 16)
                sp.dma_start(k.spill_dst, di[:, :]).then_inc(deg_out.h, 16)
                sp.dma_start(k.spill_edge, ti[:, :]).then_inc(deg_out.h, 16)
                sp.dma_start(k.spill_n, oveni[:, :]).then_inc(deg_out.h, 16)
                sp.wait_ge(deg_out.h, deg_out.at(48 + 64))
                for b in range(2):
                    sp.wait_ge(scattered[b].h, scattered[b].at(16 * COLS // 2))

            @block.gpsimd
            def _(pool):
                g = nc.gpsimd
                bound = pool.to_reg(NBKT * CAP - 1)
                pool.wait_ge(slots_init.h, slots_init.at(16 * (NBKT // 98)))

                with pool.Fori(0, NG // 2) as q:
                    for b in range(2):
                        pool.wait_ge(rows_ready.h, rows_ready.at(q * 2 + b + 1))
                        pool.sem_inc(turn.h, 1)
                        for j in range(GR):
                            g.indirect_dma_start(
                                out=k.slots, in_=ring[:, b, j, :], in_offset=None,
                                out_offset=bass.IndirectOffsetOnAxis(row[:, b * GR + j:b * GR + j + 1], 0),
                                bounds_check=bound, oob_is_err=False, engine_sem=row_read.h,
                            ).then_inc(scattered[b].h, 16)
                pool.wait_ge(deg_pads.h, deg_pads.at(1))
                g.affine_select(out=degs[:, :], in_=degs[:, :], compare_op=ALU.is_ge, fill=1.0, base=N - 1,
                                pattern=[[-1, SRC_W]], channel_multiplier=-SRC_W).then_inc(deg_pads.h, 1)
                pool.wait_ge(prepped.h, prepped.at(1))
                pool.wait_ge(spill.h, spill.at(1))
                g.iota(ti[:, :], [[1, COLS]], base=0, channel_multiplier=COLS).then_inc(spill_no.h, 1)
                g.partition_all_reduce(oven[:, 1:2], oven[:, 0:1], P, bass.bass_isa.ReduceOp.add
                                       ).then_inc(spill_no.h, 1)

            @block.vector
            def _(dve):
                V = nc.vector
                done = [0]

                def link(ins):
                    done[0] += 1
                    ins.then_inc(chain.h, 1)
                    dve.wait_ge(chain.h, chain.at(done[0]))

                V.memset(si[:, :], FAR).then_inc(pads_set.h, 1)
                V.memset(di[:, :], FAR).then_inc(pads_set.h, 1)
                link(V.memset(empty[:, :, :], 0.0))
                V.memset(zeros[:, :], 0.0).then_inc(empty_set.h, 1)
                V.memset(empty[:, :, 0:2], -1.0).then_inc(empty_set.h, 1)
                V.memset(pay[96:P, LASTC:COLS, :], 0.0).then_inc(pads_set.h, 1)
                dve.wait_ge(idx_in.h, idx_in.at(96))
                V.tensor_scalar(ti[:, :], si[:, :], 7, None, ALU.logical_shift_right)
                V.tensor_scalar(si[:, :], si[:, :], SRC_W - 1, None, ALU.bitwise_and)
                link(V.tensor_scalar(tj[:, :], di[:, :], 5, None, ALU.logical_shift_right))
                V.tensor_copy(srcb[:, :], ti[:, :])
                V.tensor_copy(srcl[:, :], si[:, :])
                link(V.tensor_scalar(tj[:, :], tj[:, :], 9363.0, None, ALU.mult))
                link(V.tensor_scalar(tj[:, :], tj[:, :], 16, None, ALU.logical_shift_right))
                link(V.tensor_copy(dstw[:, :], tj[:, :]))
                V.tensor_copy(dstl[:, :], di[:, :])
                link(V.tensor_scalar(tj[:, :], tj[:, :], 2, None, ALU.logical_shift_right))
                link(V.scalar_tensor_tensor(dstl[:, :], dstw[:, :], -float(DST_W), dstl[:, :], ALU.mult, ALU.add))
                link(V.scalar_tensor_tensor(keyf[:, :], tj[:, :], float(UB - UD), dstw[:, :], ALU.mult, ALU.add))
                link(V.scalar_tensor_tensor(keyf[:, :], srcb[:, :], float(UD), keyf[:, :], ALU.mult, ALU.add))
                link(V.tensor_scalar(ti[:, :], ti[:, :], 9363.0, None, ALU.mult))
                link(V.tensor_scalar(ti[:, :], ti[:, :], 16, None, ALU.logical_shift_right))
                link(V.scalar_tensor_tensor(keyf[:, :], ti[:, :], float(NU * UB - US * UD), keyf[:, :],
                                            ALU.mult, ALU.add))
                V.tensor_copy(key16[:, :], keyf[:, :])
                link(V.tensor_scalar(rowbase[:, :], keyf[:, :], float(NBKT), BIG, ALU.is_ge, ALU.mult))
                link(V.tensor_tensor(rowbase[:, :], rowbase[:, :], keyf[:, :], ALU.add))
                dve.wait_ge(pads_set.h, pads_set.at(3))
                link(V.tensor_copy(pay[:, :, 0], srcl[:, :]))
                link(V.tensor_copy(pay[:, :, 1], dstl[:, :]))
                V.tensor_scalar(dneg[:, :], dstl[:, :], -1.0, None, ALU.mult)
                V.memset(degs[:, :], 0.0).then_inc(prepped.h, 1)
                dve.wait_ge(prepped.h, prepped.at(1))

                def one_hots(c, b):
                    if counted.due(c - 2):
                        dve.wait_ge(counted.h, counted.at(c - 2))
                    if base_done.due(c - 3):
                        dve.wait_ge(base_done.h, base_done.at(c - 3))
                    at = bass.ds(c, 1)
                    V.tensor_scalar(hot[:, b, 0:64], k.iota[:, 0:64], srcb[:, at], None, ALU.is_equal)
                    V.tensor_scalar(hot[:, b, H_DW:H_SL], k.iota[:, 0:ND], dstw[:, at], None, ALU.is_equal)
                    V.tensor_scalar(hot[:, b, H_SL:H_DL], k.iota[:, 0:SRC_W], srcl[:, at], None, ALU.is_equal
                                    ).then_inc(hot_ready.h, 1)

                def within(c, b, j):
                    dve.wait_ge(keyrow.h, keyrow.at(c + 1))
                    V.scalar_tensor_tensor(junk[:, j, :], keys[j % 2][:, 0:P], keyf[:, bass.ds(c, 1)],
                                           k.tri[:, :], ALU.is_equal, ALU.mult,
                                           accum_out=parts[:, b, 0, j:j + 1]).then_inc(within_done.h, 1)

                def base(c, b, j):
                    dve.wait_ge(looked.h, looked.at(c + 1))
                    V.scalar_tensor_tensor(junk[:, GR + j, 0:ND], look[j % 2][:, 0:ND], 1.0,
                                           hot[:, j % 4, H_DW:H_SL], ALU.mult, ALU.mult,
                                           accum_out=parts[:, b, 1, j:j + 1]).then_inc(base_done.h, 1)

                def finish(g, b):
                    dve.wait_ge(base_done.h, base_done.at((g + 1) * GR))
                    V.tensor_tensor(rank[:, :], parts[:, b, 0, :], parts[:, b, 1, :], ALU.add).then_inc(chain.h, 1)
                    dve.wait_ge(chain.h, chain.at(g + done[0] + 1))
                    V.tensor_scalar(over[:, bass.ds(g * GR, GR)], rank[:, :], float(CAP) - 0.5, None, ALU.is_gt)
                    if row_read.due((g - 1) * GR):
                        dve.wait_ge(row_read.h, row_read.at((g - 1) * GR))
                    dve.wait_ge(ring_full.h, ring_full.at(g + 1))
                    V.scalar_tensor_tensor(row[:, b * GR:(b + 1) * GR], rank[:, :], float(NBKT),
                                           rowbase[:, bass.ds(g * GR, GR)], ALU.mult, ALU.add
                                           ).then_inc(rows_ready.h, 1)

                def groups(q, first=False, last=False):
                    for b in range(2):
                        g = q * 2 + b
                        for j in range(GR):
                            c = g * GR + j
                            if not (last and b == 1 and j == GR - 1):
                                one_hots(c + 1, (j + 1) % 4)
                            within(c, b, j)
                            if j:
                                base(c - 1, b, j - 1)
                            elif not (first and b == 0):
                                base(c - 1, 1 - b, GR - 1)
                            if j == 1 and not (first and b == 0):
                                finish(g - 1, 1 - b)

                one_hots(0, 0)
                groups(0, first=True)
                with dve.Fori(1, NG // 2 - 1) as q:
                    groups(q)
                groups(NG // 2 - 1, last=True)
                base(COLS - 1, 1, GR - 1)
                finish(NG - 1, 1)
                dve.wait_ge(counted.h, counted.at(COLS + 1))
                V.tensor_copy(degs[:, :], cnt_s[0:NS, ND:ND + SRC_W]).then_inc(deg_pads.h, 1)
                V.tensor_copy(degd[:, :], cnt_d[0:ND, 0:DST_W]).then_inc(tail.h, 1)
                dve.wait_ge(tail.h, tail.at(1))
                V.tensor_scalar(t3[:, :], degd[:, :], 1.0, None, ALU.add).then_inc(tail.h, 1)
                dve.wait_ge(tail.h, tail.at(2))
                V.tensor_scalar(degd[:, :], degd[:, :], 1.0, None, ALU.max).then_inc(tail.h, 1)
                dve.wait_ge(tail.h, tail.at(3))
                V.reciprocal(degd[:, :], degd[:, :]).then_inc(deg_ready.h, 1)
                dve.wait_ge(deg_pads.h, deg_pads.at(2))
                V.reciprocal(degs[:, :], degs[:, :]).then_inc(deg_ready.h, 1)
                dve.wait_ge(rooted.h, rooted.at(1))
                V.reciprocal(t3[:, :], t3[:, :]).then_inc(deg_ready.h, 1)
                V.tensor_reduce(oven[:, 0:1], over[:, :], AX, ALU.add).then_inc(spill.h, 1)
                dve.wait_ge(spill.h, spill.at(1))
                V.tensor_scalar(over[:, :], over[:, :], -BIG, BIG, ALU.mult, ALU.add).then_inc(spill.h, 1)
                dve.wait_ge(spill.h, spill.at(2))
                dve.wait_ge(idx_in.h, idx_in.at(96 + 48))
                V.tensor_tensor(si[:, :], si[:, :], over[:, :], ALU.add).then_inc(spill.h, 1)
                V.tensor_tensor(di[:, :], di[:, :], over[:, :], ALU.add).then_inc(spill.h, 1)
                dve.wait_ge(spill_no.h, spill_no.at(1))
                V.tensor_tensor(ti[:, :], ti[:, :], over[:, :], ALU.add).then_inc(spill.h, 1)
                dve.wait_ge(spill_no.h, spill_no.at(2))
                V.tensor_copy(oveni[:, :], oven[0:1, 1:2]).then_inc(spill.h, 1)

            @block.scalar
            def _(act):
                A = nc.scalar

                def load_features(i):
                    c0, c1 = i * FULLP, (i + 1) * FULLP
                    m = min(c1, LASTC)
                    if m < c1:
                        act.wait_ge(pads_set.h, pads_set.at(3))
                    for p0, p1 in ((0, FULLP), (FULLP, LASTP)):
                        act.dma_start(pay[p0:p1, c0:c1, 2:PW],
                                      ea[p0 * COLS:p1 * COLS, :].rearrange("(p c) f -> p c f", c=COLS)[:, c0:c1, :]
                                      ).then_inc(ea_in[i].h, 16)
                    if m > c0:
                        act.dma_start(pay[LASTP:P, c0:m, 2:PW],
                                      ea[LASTP * COLS + c0:LASTP * COLS + m, :].rearrange("(p c) f -> p c f", p=1)
                                      ).then_inc(ea_in[i].h, 16)

                load_features(0)
                act.wait_ge(prepped.h, prepped.at(1))

                def square(c, b):
                    A.activation(away[:, b % 2, :], k.iota[:, 0:DST_W], ACT.Square, bias=dneg[:, bass.ds(c, 1)]
                                 ).then_inc(dhot_step.h, 1)

                def one_hot(c, b):
                    act.wait_ge(dhot_step.h, dhot_step.at(2 * c + 1))
                    A.activation(hot[:, b, H_DL:H_END], away[:, b % 2, :], ACT.Relu, bias=1.0, scale=-1.0
                                 ).then_inc(dhot_step.h, 1)

                for c in range(2):
                    square(c, c)
                    one_hot(c, c)

                def groups(q, last=False):
                    for b in range(2):
                        g = q * 2 + b
                        for j in range(GR):
                            c = g * GR + j
                            ahead = not (last and b == 1 and j >= GR - 2)
                            act.wait_ge(counted.h, counted.at(c + 1))
                            if looked.due(c - 1):
                                act.wait_ge(looked.h, looked.at(c - 1))
                            A.activation(before[0:NS, j % 2, :], cnt_s[0:NS, 0:ND], ACT.Copy
                                         ).then_inc(snapped.h, 1)
                            if ahead:
                                square(c + 2, (j + 2) % 4)
                            act.wait_ge(flipped.h, flipped.at(c + 1))
                            A.activation(blockT[0:NS, j % 2, :], flip[j % 2][0:NS, 0:P], ACT.Copy
                                         ).then_inc(flip_copied.h, 1)
                            if ahead:
                                one_hot(c + 2, (j + 2) % 4)
                            if j == GR - 2:
                                if scattered[b].due(q * (16 * GR)):
                                    act.wait_ge(scattered[b].h, scattered[b].at(q * (16 * GR)))
                                A.activation(ring[:, b, :, :], pay[:, cols(g, GR), :], ACT.Copy
                                             ).then_inc(ring_full.h, 1)

                turns = FULLP // (2 * GR)
                for i, loaded in enumerate(ea_in):
                    act.wait_ge(loaded.h, loaded.at(48 if LASTC > i * FULLP else 32))
                    groups(i * turns)
                    if i + 1 < len(ea_in):
                        load_features(i + 1)
                    final = i + 1 == len(ea_in)
                    with act.Fori(i * turns + 1, (i + 1) * turns - final) as q:
                        groups(q)
                groups(NG // 2 - 1, last=True)
                act.wait_ge(tail.h, tail.at(2))
                A.activation(t3[:, :], t3[:, :], ACT.Sqrt).then_inc(rooted.h, 1)

            @block.tensor
            def _(pe):
                T = nc.tensor
                pe.wait_ge(prepped.h, prepped.at(1))
                T.matmul(cnt_s[0:NS, 0:ND + SRC_W], zeros[:, 0:NS], zeros[:, 0:ND + SRC_W], start=True, stop=True)
                T.matmul(cnt_d[0:ND, 0:DST_W], zeros[:, 0:ND], zeros[:, 0:DST_W], start=True, stop=True
                         ).then_inc(counted.h, 1)

                def lookup(c, b):
                    pe.wait_ge(flip_copied.h, flip_copied.at(c + 1))
                    if base_done.due(c - 1):
                        pe.wait_ge(base_done.h, base_done.at(c - 1))
                    T.matmul(look[b][:, 0:ND], blockT[0:NS, b, :], before[0:NS, b, :],
                             start=True, stop=True).then_inc(looked.h, 1)

                def groups(g2, first=False):
                    for b in range(2):
                        g = g2 * 2 + b
                        for j in range(GR):
                            c = g * GR + j
                            o = j % 4
                            if within_done.due(c - 1):
                                pe.wait_ge(within_done.h, within_done.at(c - 1))
                            T.matmul(keys[j % 2][:, 0:P], key16[:, bass.ds(c, 1)].to_broadcast([P, P]),
                                     k.id16[:, :], start=True, stop=True).then_inc(keyrow.h, 1)
                            pe.wait_ge(hot_ready.h, hot_ready.at(c + 1))
                            if flip_copied.due(c - 1):
                                pe.wait_ge(flip_copied.h, flip_copied.at(c - 1))
                            T.transpose(flip[j % 2][:, 0:P], hot[:, o, 0:P], k.idb[:, :]).then_inc(flipped.h, 1)
                            if not (first and b == 0 and j == 0):
                                lookup(c - 1, (j + 1) % 2)
                            pe.wait_ge(snapped.h, snapped.at(c + 1))
                            T.matmul(cnt_s[0:NS, 0:ND + SRC_W], hot[:, o, 0:NS], hot[:, o, H_DW:H_DL],
                                     start=False, stop=True, skip_group_check=True)
                            pe.wait_ge(dhot_step.h, dhot_step.at(2 * c + 2))
                            T.matmul(cnt_d[0:ND, 0:DST_W], hot[:, o, H_DW:H_SL], hot[:, o, H_DL:H_END],
                                     start=False, stop=True, skip_group_check=True).then_inc(counted.h, 1)

                groups(0, first=True)
                with pe.Fori(1, NG // 2) as g2:
                    groups(g2)
                lookup(COLS - 1, 1)


def build_adjacency(k):
    nc = k.nc
    with ExitStack() as ctx:
        def sb(name, shape, dt):
            return ctx.enter_context(nc.sbuf_tensor(name, shape, dt))

        slot = sb("slot", [P, 2, UB, PW], F32)
        S = sb("S", [P, 2, UB, SRC_W], BF16)
        Dh = sb("Dh", [P, 2, UB, DST_W], BF16)
        eas = sb("eas", [P, 2, UB, 3 * DE], BF16)
        rest = sb("rest", [P, 2, UB, DE], F32)
        ads = sb("ads", [DST_H, 2, 2 * UD, STRIP], F16)
        asd = sb("asd", [P, 2, US, STRIP], F16)
        easum = sb("easum", [3 * DE, NP], F32)
        bank = [ctx.enter_context(nc.psum_tensor(f"bank{i}", [P, 512], F32)) for i in range(6)]
        eab = [ctx.enter_context(nc.psum_tensor(f"eab{i}", [P, 512], F32)) for i in range(2)]

        slot_in = [k.sem("slot_in0"), k.sem("slot_in1")]
        hots, split, ea_chain = k.sem("hots"), k.sem("split"), k.sem("ea_chain")
        filled, act_out, dve_out = k.sem("filled"), k.sem("act_out"), k.sem("dve_out")
        ea_filled, ea_added, zeroed = k.sem("ea_filled"), k.sem("ea_added"), k.sem("zeroed")
        unit_out = [k.sem("unit_out0"), k.sem("unit_out1")]
        ea_out, turn, turn_sp, turn_act = k.sem("ea_out"), k.sem("turn"), k.sem("turn_sp"), k.sem("turn_act")

        items = []
        for jj in range(UD):
            for h in range(2):
                for lo, hi in ((0, 4), (4, US)):
                    items.append(("ds", 2 * jj + h, lo, hi))
        for ii in range(US):
            for lo, hi in ((0, 2), (2, 4)):
                items.append(("sd", ii, lo, hi))
        NI = len(items)
        assert NI % 6 == 0
        DS_ITEMS = 4 * UD
        on_act = list(range(NI - 4))
        on_dve = list(range(NI - 4, NI))

        def target(item, b):
            kind, r, lo, hi = item
            if kind == "ds":
                return ads[:, b, r, lo * SRC_W:hi * SRC_W]
            return asd[:, b, r, lo * DST_W:hi * DST_W]

        def source(n):
            kind, r, lo, hi = items[n]
            if kind == "ds":
                return bank[n % 6][0:DST_H, 0:(hi - lo) * SRC_W]
            return bank[n % 6][:, 0:(hi - lo) * DST_W]

        def units(eng, body):
            body(0, 0, 0)
            body(1, 1, 0)
            with eng.Fori(1, NU * NU // 2) as q:
                body(q * 2, 0, q)
                body(q * 2 + 1, 1, q)
            body(NU * NU - 1, 0, NU * NU // 2)

        assert NU * NU % 2 == 1

        with nc.Block() as block:
            @block.sync
            def _(sp):
                def body(u, b, n):
                    sp.wait_ge(act_out.h, act_out.at(u * len(on_act) + DS_ITEMS))
                    sp.sem_inc(turn_sp.h, 1)
                    sp.dma_start(k.counts_ds[bass.ds(u, 1)].rearrange("u p r c -> (u p) (r c)"),
                                 ads[:, b, :, :].rearrange("p r c -> p (r c)")).then_inc(unit_out[b].h, 16)
                    sp.wait_ge(act_out.h, act_out.at((u + 1) * len(on_act)))
                    sp.sem_inc(turn_sp.h, 1)
                    sp.wait_ge(dve_out.h, dve_out.at((u + 1) * len(on_dve)))
                    sp.sem_inc(turn_sp.h, 1)
                    sp.dma_start(k.counts_sd[bass.ds(u, 1)].rearrange("u p r c -> (u p) (r c)"),
                                 asd[:, b, :, :].rearrange("p r c -> p (r c)")).then_inc(unit_out[b].h, 16)

                units(sp, body)
                sp.wait_ge(ea_added.h, ea_added.at(2 * NU * NU))
                sp.dma_start(k.ea_sums, easum[:, :]).then_inc(ea_out.h, 16)
                sp.wait_ge(ea_out.h, ea_out.at(16))
                sp.wait_ge(unit_out[0].h, unit_out[0].at(32 * (NU * NU // 2 + 1)))
                sp.wait_ge(unit_out[1].h, unit_out[1].at(32 * (NU * NU // 2)))

            @block.gpsimd
            def _(pool):
                g = nc.gpsimd
                g.memset(easum[:, :], 0.0).then_inc(zeroed.h, 1)

                def body(u, b, n):
                    pool.wait_ge(slot_in[b].h, slot_in[b].at(n * 16 + 16))
                    pool.sem_inc(turn.h, 1)
                    if ea_filled.due(2 * u - 2):
                        pool.wait_ge(ea_filled.h, ea_filled.at(2 * u - 2))
                    pool.sem_inc(turn.h, 1)
                    f = slot[:, b, :, 2:PW]
                    r = rest[:, b, :, :]
                    hi, mid, lo = (eas[:, b, :, i * DE:(i + 1) * DE] for i in range(3))
                    g.tensor_copy(hi, f).then_inc(ea_chain.h, 1)
                    pool.wait_ge(ea_chain.h, ea_chain.at(u * 3 + 1))
                    pool.sem_inc(turn.h, 1)
                    g.tensor_tensor(r, f, hi, ALU.subtract).then_inc(ea_chain.h, 1)
                    pool.wait_ge(ea_chain.h, ea_chain.at(u * 3 + 2))
                    pool.sem_inc(turn.h, 1)
                    g.tensor_copy(mid, r).then_inc(ea_chain.h, 1)
                    pool.wait_ge(ea_chain.h, ea_chain.at(u * 3 + 3))
                    pool.sem_inc(turn.h, 1)
                    g.tensor_tensor(lo, r, mid, ALU.subtract).then_inc(split.h, 1)

                units(pool, body)

            @block.vector
            def _(dve):
                V = nc.vector

                def one_hots(u, b, n):
                    dve.wait_ge(slot_in[b].h, slot_in[b].at(n * 16 + 16))
                    if ea_filled.due(2 * u - 2):
                        dve.wait_ge(ea_filled.h, ea_filled.at(2 * u - 2))
                    for i in range(UB):
                        V.tensor_scalar(S[:, b, i, :], k.iota[:, 0:SRC_W], slot[:, b, i, 0:1], None, ALU.is_equal)
                        last = V.tensor_scalar(Dh[:, b, i, :], k.iota[:, 0:DST_W], slot[:, b, i, 1:2], None,
                                               ALU.is_equal)
                    last.then_inc(hots.h, 1)

                def evacuate(u, b, n):
                    if unit_out[b].due(n * 32):
                        dve.wait_ge(unit_out[b].h, unit_out[b].at(n * 32))
                    for at, i in enumerate(on_dve):
                        dve.wait_ge(filled.h, filled.at(u * NI + i + 1))
                        V.tensor_copy(target(items[i], b), source(i)).then_inc(dve_out.h, 1)

                def add_ea(u):
                    t = u % NU
                    for h in range(2):
                        dve.wait_ge(ea_filled.h, ea_filled.at(u * 2 + h + 1))
                        at = bass.ds(t * STRIP + h * HALF, HALF)
                        V.tensor_tensor(easum[:, at], easum[:, at], eab[h][0:3 * DE, 0:HALF], ALU.add
                                        ).then_inc(ea_added.h, 1)

                def finish(u, b, n):
                    evacuate(u, b, n)
                    add_ea(u)

                dve.wait_ge(zeroed.h, zeroed.at(1))
                one_hots(0, 0, 0)
                one_hots(1, 1, 0)
                finish(0, 0, 0)
                with dve.Fori(1, NU * NU // 2) as q:
                    one_hots(q * 2, 0, q)
                    finish(q * 2 - 1, 1, q - 1)
                    one_hots(q * 2 + 1, 1, q)
                    finish(q * 2, 0, q)
                one_hots(NU * NU - 1, 0, NU * NU // 2)
                finish(NU * NU - 2, 1, NU * NU // 2 - 1)
                finish(NU * NU - 1, 0, NU * NU // 2)

            @block.scalar
            def _(act):
                A = nc.scalar

                def load(u, b):
                    act.dma_start(slot[:, b, :, :].rearrange("p a b -> p (a b)"), rows[:, cols(u, UB * PW)]
                                  ).then_inc(slot_in[b].h, 16)

                def body(u, b, n, ahead=True):
                    if unit_out[b].due(n * 32):
                        act.wait_ge(unit_out[b].h, unit_out[b].at(n * 32))
                    for i in on_act:
                        act.wait_ge(filled.h, filled.at(u * NI + i + 1))
                        A.activation(target(items[i], b), source(i), ACT.Copy).then_inc(act_out.h, 1)
                        if i == 4 and ahead:
                            act.wait_ge(hots.h, hots.at(u + 1))
                            act.wait_ge(ea_chain.h, ea_chain.at(3 * u + 2))
                            act.sem_inc(turn_act.h, 1)
                            load(u + 2, b)

                rows = k.slots.rearrange("(p r) w -> p (r w)", p=P)
                last = NU * NU - 1
                load(0, 0)
                load(1, 1)
                body(0, 0, 0)
                body(1, 1, 0)
                with act.Fori(1, last // 2 - 1) as q:
                    body(q * 2, 0, q)
                    body(q * 2 + 1, 1, q)
                body(last - 2, 0, last // 2 - 1)
                body(last - 1, 1, last // 2 - 1, ahead=False)
                body(last, 0, last // 2, ahead=False)

            @block.tensor
            def _(pe):
                T = nc.tensor

                def body(u, b, n):
                    pe.wait_ge(hots.h, hots.at(u + 1))
                    for i, (kind, r, lo, hi) in enumerate(items):
                        before = (i - 6) % NI
                        v = u if i >= 6 else u - 1
                        if before in on_act:
                            if act_out.due(v * len(on_act) + on_act.index(before) + 1):
                                pe.wait_ge(act_out.h, act_out.at(v * len(on_act) + on_act.index(before) + 1))
                        else:
                            if dve_out.due(v * len(on_dve) + on_dve.index(before) + 1):
                                pe.wait_ge(dve_out.h, dve_out.at(v * len(on_dve) + on_dve.index(before) + 1))
                        for a in range(lo, hi):
                            if kind == "ds":
                                jj, h = r // 2, r % 2
                                kk = a * UD + jj
                                mm = T.matmul(bank[i % 6][0:DST_H, (a - lo) * SRC_W:(a - lo + 1) * SRC_W],
                                              Dh[:, b, kk, h * DST_H:(h + 1) * DST_H], S[:, b, kk, :],
                                              start=True, stop=True)
                            else:
                                kk = r * UD + a
                                mm = T.matmul(bank[i % 6][:, (a - lo) * DST_W:(a - lo + 1) * DST_W],
                                              S[:, b, kk, :], Dh[:, b, kk, :], start=True, stop=True)
                        mm.then_inc(filled.h, 1)
                    pe.wait_ge(split.h, split.at(u + 1))
                    for h in range(2):
                        if ea_added.due(u * 2 + h - 1):
                            pe.wait_ge(ea_added.h, ea_added.at(u * 2 + h - 1))
                        for jj in range(2 * h, 2 * h + 2):
                            for ii in range(US):
                                kk = ii * UD + jj
                                mm = T.matmul(eab[h][0:3 * DE, (jj % 2) * DST_W:(jj % 2 + 1) * DST_W],
                                              eas[:, b, kk, :], Dh[:, b, kk, :],
                                              start=(ii == 0), stop=(ii == US - 1))
                        mm.then_inc(ea_filled.h, 1)

                units(pe, body)



def load_weights(k, w):
    nc = k.nc
    straight = [("a0", w["L0_gnn_l0_W0"]), ("a1", w["L0_gnn_l0_W1"]), ("b0", w["L0_gnn_l1_W0"]),
                ("b1", w["L0_gnn_l1_W1"]), ("g0", w["L3_gnn_W1"]), ("g1", w["L3_gnn_W2"])]
    straight += [(f"self{i}", w["L1_gnn_W_self"][i]) for i in range(4)]
    straight += [(f"neigh{i}", w["L1_gnn_W_neigh"][i]) for i in range(4)]
    turned = [("msg", w["L2_gnn_W_message"][:, 0:D]), ("node", w["L2_gnn_W_node"]),
              ("up_h", w["L2_gnn_W1"][:, 0:D]), ("up_m", w["L2_gnn_W1"][:, D:2 * D]), ("down", w["L2_gnn_W2"])]
    vectors = []
    for i in range(2):
        vectors += [w[f"L0_gnn_l{i}_{n}"] for n in ("b0", "mbn_g", "mbn_b", "b1", "bn_g", "bn_b")]
    vectors += [w["L1_gnn_bias"][i] for i in range(4)]
    vectors += [w[f"L2_gnn_{n}"] for n in ("b1", "ln1_g", "ln1_b", "b2", "ln2_g", "ln2_b", "ln_g", "ln_b")]
    vectors += [w["L3_gnn_b1"], w["L3_gnn_b2"]]
    nv = len(vectors)
    k.W = {name: k.weights[:, i, :] for i, (name, _) in enumerate(straight + turned)}
    k.W["msg_e"] = k.weights[0:3 * DE, len(straight) + len(turned), :]
    k.vec = lambda i: k.vectors[:, i:i + 1]
    w_in, v_in, w_T, w_out = k.sem("w_in"), k.sem("v_in"), k.sem("w_T"), k.sem("w_out")
    with ExitStack() as ctx:
        raw = ctx.enter_context(nc.sbuf_tensor("raw", [P, len(turned), D], F32))
        raw_e = ctx.enter_context(nc.sbuf_tensor("raw_e", [P, 3 * DE], F32))
        rows = ctx.enter_context(nc.sbuf_tensor("rows", [nv, D], F32))
        with nc.Block() as block:
            @block.sync
            def _(sp):
                for i, (_, a) in enumerate(turned):
                    sp.dma_start(raw[:, i, :], a).then_inc(w_in.h, 16)
                for i in range(3):
                    sp.dma_start(raw_e[:, i * DE:(i + 1) * DE], w["L2_gnn_W_message"][:, D:D + DE]
                                 ).then_inc(w_in.h, 16)
                for name, a in straight:
                    sp.dma_start(k.W[name], a).then_inc(w_in.h, 16)

            @block.scalar
            def _(act):
                for i, a in enumerate(vectors):
                    act.dma_start(rows[i:i + 1, :], a.rearrange("(a f) -> a f", a=1)).then_inc(v_in.h, 16)
                for i, (name, _) in enumerate(turned):
                    act.wait_ge(w_T.h, w_T.at(i + 1))
                    nc.scalar.activation(k.W[name], k.bank[i][:, 0:D], ACT.Copy).then_inc(w_out.h, 1)
                i = len(turned)
                act.wait_ge(w_T.h, w_T.at(i + 1))
                nc.scalar.activation(k.W["msg_e"], k.bank[i][0:3 * DE, 0:D], ACT.Copy).then_inc(w_out.h, 1)
                act.wait_ge(w_T.h, w_T.at(i + 2))
                nc.scalar.activation(k.vectors[:, 0:nv], k.bank[i + 1][:, 0:nv], ACT.Copy).then_inc(w_out.h, 1)

            @block.tensor
            def _(pe):
                pe.wait_ge(w_in.h, w_in.at(16 * (len(turned) + 3 + len(straight))))
                for i in range(len(turned)):
                    nc.tensor.transpose(k.bank[i][:, 0:D], raw[:, i, :], k.idf[:, :]).then_inc(w_T.h, 1)
                i = len(turned)
                nc.tensor.transpose(k.bank[i][0:3 * DE, 0:D], raw_e[:, :], k.idf[:, :]).then_inc(w_T.h, 1)
                pe.wait_ge(v_in.h, v_in.at(16 * nv))
                nc.tensor.transpose(k.bank[i + 1][:, 0:nv], rows[:, :], k.idf[0:nv, 0:nv]).then_inc(w_T.h, 1)


def load_x(k, x):
    nc = k.nc
    x_in, x_T, x_copied, x_kept, x_pad = k.sem("x_in"), k.sem("x_T"), k.sem("x_copied"), k.sem("x_kept"), k.sem("x_pad")
    full = NS - 1
    rowsn = k.B[:, :].rearrange("p (b f) -> p b f", f=D)
    with nc.Block() as block:
        @block.vector
        def _(dve):
            nc.vector.memset(k.B[:, full * D:NP], 0.0).then_inc(x_pad.h, 1)

        @block.sync
        def _(sp):
            sp.dma_start(rowsn[:, 0:full, :], x[0:full * P, :].rearrange("(b p) f -> p b f", p=P)).then_inc(x_in.h, 16)
            sp.wait_ge(x_pad.h, x_pad.at(1))
            sp.dma_start(rowsn[0:N - full * P, full, :], x[full * P:N, :]).then_inc(x_in.h, 16)
            sp.wait_ge(x_copied.h, x_copied.at(-(-NS // 4)))
            sp.dma_start(k.x_kept, k.A[:, :]).then_inc(x_kept.h, 16)
            sp.wait_ge(x_kept.h, x_kept.at(16))

        @block.tensor
        def _(pe):
            pe.wait_ge(x_in.h, x_in.at(32))
            for g in range(-(-NS // 4)):
                if x_copied.due(g - 3):
                    pe.wait_ge(x_copied.h, x_copied.at(g - 3))
                for i in range(4 * g, min(4 * g + 4, NS)):
                    mm = nc.tensor.transpose(k.bank[g % 4][:, (i % 4) * P:(i % 4 + 1) * P], rowsn[:, i, :], k.idf[:, :])
                mm.then_inc(x_T.h, 1)

        @block.scalar
        def _(act):
            for g in range(-(-NS // 4)):
                act.wait_ge(x_T.h, x_T.at(g + 1))
                n = min(4, NS - 4 * g) * P
                nc.scalar.activation(k.A[:, g * 512:g * 512 + n], k.bank[g % 4][:, 0:n], ACT.Copy
                                     ).then_inc(x_copied.h, 1)


def residual(k, y):
    nc = k.nc
    got, added, kept = k.sem("res_in"), k.sem("res_added"), k.sem("res_kept")
    with nc.Block() as block:
        @block.sync
        def _(sp):
            sp.dma_start(k.A[:, :], k.x_kept).then_inc(got.h, 16)
            sp.wait_ge(added.h, added.at(NU))
            sp.dma_start(k.x_kept, k.A[:, :]).then_inc(kept.h, 16)
            sp.wait_ge(kept.h, kept.at(16))

        @block.vector
        def _(dve):
            dve.wait_ge(got.h, got.at(16))
            with dve.Fori(0, NU) as s:
                at = cols(s, STRIP)
                nc.vector.tensor_tensor(k.A[:, at], k.A[:, at], y[:, at], ALU.add).then_inc(added.h, 1)
    k.advance(res_in=16, res_added=NU, res_kept=16)


def store_out(k, out):
    nc = k.nc
    o_T, o_copied, o_out = k.sem("o_T"), k.sem("o_copied"), k.sem("o_out")
    full = NS - 1
    rowsn = k.B[:, :].rearrange("p (b f) -> p b f", f=D)
    NGRP = -(-NS // 4)
    with nc.Block() as block:
        @block.tensor
        def _(pe):
            for g in range(NGRP):
                if o_copied.due(g - 3):
                    pe.wait_ge(o_copied.h, o_copied.at(g - 3))
                for i in range(4 * g, min(4 * g + 4, NS)):
                    mm = nc.tensor.transpose(k.bank[g % 4][:, (i % 4) * P:(i % 4 + 1) * P],
                                             k.A[:, i * P:(i + 1) * P], k.idf[:, :])
                mm.then_inc(o_T.h, 1)

        @block.scalar
        def _(act):
            for g in range(NGRP):
                act.wait_ge(o_T.h, o_T.at(g + 1))
                n = min(4, NS - 4 * g) * P
                nc.scalar.activation(k.B[:, g * 512:g * 512 + n], k.bank[g % 4][:, 0:n], ACT.Copy
                                     ).then_inc(o_copied.h, 1)

        @block.sync
        def _(sp):
            for g in range(NGRP - 1):
                sp.wait_ge(o_copied.h, o_copied.at(g + 1))
                sp.dma_start(out[g * 512:(g + 1) * 512, :].rearrange("(b p) f -> p b f", p=P),
                             rowsn[:, 4 * g:4 * g + 4, :]).then_inc(o_out.h, 16)
            sp.wait_ge(o_copied.h, o_copied.at(NGRP))
            sp.dma_start(out[full * P:N, :], rowsn[0:N - full * P, full, :]).then_inc(o_out.h, 16)
            sp.wait_ge(o_out.h, o_out.at(16 * NGRP))


def layer_norm(k, src, dst, gain=None, shift=None):
    nc = k.nc
    mean, centred, squared = k.sem("ln_mean"), k.sem("ln_centred"), k.sem("ln_squared")
    var, rooted, inverse = k.sem("ln_var"), k.sem("ln_rooted"), k.sem("ln_inverse")
    spread, final = k.sem("ln_spread"), k.sem("ln_final")
    with nc.Block() as block:
        @block.tensor
        def _(pe):
            def means(c, b):
                pe.wait_ge(centred.h, centred.at(c + 1))
                nc.tensor.matmul(k.bank[b][:, 0:CH], k.avg[:, :], src[:, cols(c)], start=True, stop=True
                                 ).then_inc(mean.h, 1)

            chunk_pairs(pe, means)
            for c in range(NCH):
                pe.wait_ge(squared.h, squared.at(c + 1))
                nc.tensor.matmul(k.bank[2][0:NCH, 0:CH], k.gather[:, c, :], dst[:, c * CH:(c + 1) * CH],
                                 start=(c == 0), stop=(c == NCH - 1)).then_inc(var.h, 1)
            pe.wait_ge(inverse.h, inverse.at(1))
            for c in range(NCH):
                if c >= 2:
                    pe.wait_ge(final.h, final.at(c - 1))
                nc.tensor.matmul(k.bank[3 + c % 2][:, 0:CH], k.spread[:, c, :], k.rstd[:, :], start=True, stop=True
                                 ).then_inc(spread.h, 1)

        @block.vector
        def _(dve):
            V = nc.vector
            dve.sem_inc(centred.h, 2)

            def centre(c, b):
                dve.wait_ge(mean.h, mean.at(c + 1))
                V.tensor_tensor(src[:, cols(c)], src[:, cols(c)], k.bank[b][:, 0:CH], ALU.subtract
                                ).then_inc(centred.h, 1)

            def scale(c, b):
                dve.wait_ge(spread.h, spread.at(c + 1))
                at = cols(c)
                if gain is None:
                    V.scalar_tensor_tensor(dst[:, at], src[:, at], 0.0, k.bank[3 + b][:, 0:CH], ALU.max, ALU.mult
                                           ).then_inc(final.h, 1)
                else:
                    V.scalar_tensor_tensor(dst[:, at], src[:, at], gain, k.bank[3 + b][:, 0:CH], ALU.mult, ALU.mult
                                           ).then_inc(final.h, 1)

            chunk_pairs(dve, centre)
            dve.wait_ge(rooted.h, rooted.at(1))
            V.reciprocal(k.rstd[:, :], k.rstd[:, :]).then_inc(inverse.h, 1)
            chunk_pairs(dve, scale)

        @block.scalar
        def _(act):
            A = nc.scalar

            def square(c, b):
                act.wait_ge(centred.h, centred.at(2 + c + 1))
                A.activation(dst[:, cols(c)], src[:, cols(c)], ACT.Square).then_inc(squared.h, 1)

            def shift_in(c, b):
                act.wait_ge(final.h, final.at(c + 1))
                A.activation(dst[:, cols(c)], dst[:, cols(c)], ACT.Identity, bias=shift)

            chunk_pairs(act, square)
            act.wait_ge(var.h, var.at(NCH))
            A.activation(k.rstd[:, :], k.bank[2][0:NCH, 0:CH], ACT.Sqrt, bias=k.eps[0:NCH, 0:1]
                         ).then_inc(rooted.h, 1)
            if shift is not None:
                chunk_pairs(act, shift_in)
    k.advance(ln_mean=NCH, ln_centred=NCH + 2, ln_squared=NCH, ln_var=NCH, ln_rooted=1, ln_inverse=1,
              ln_spread=NCH, ln_final=NCH)


def product(k, terms, dst, func, bias):
    nc = k.nc
    summed, moved = k.sem("summed"), k.sem("moved")
    with nc.Block() as block:
        @block.tensor
        def _(pe):
            def body(c, b):
                pe.wait_ge(moved.h, moved.at(c + 1))
                for i, (w, v) in enumerate(terms):
                    mm = nc.tensor.matmul(k.bank[b][:, 0:CH], w, v[:, cols(c)], start=(i == 0),
                                          stop=(i == len(terms) - 1))
                mm.then_inc(summed.h, 1)

            chunk_pairs(pe, body)

        @block.scalar
        def _(act):
            act.sem_inc(moved.h, 2)

            def body(c, b):
                act.wait_ge(summed.h, summed.at(c + 1))
                nc.scalar.activation(dst[:, cols(c)], k.bank[b][:, 0:CH], func, bias=bias).then_inc(moved.h, 1)

            chunk_pairs(act, body)
    k.advance(summed=NCH, moved=NCH + 2)


def batch_norm_relu(k, v, gain, shift):
    nc = k.nc
    stat, bn_root, bn_scaled = k.sem("bn_stat"), k.sem("bn_root"), k.sem("bn_scaled")
    st, mv = k.bn_stats, k.bn_mv
    with nc.Block() as block:
        @block.vector
        def _(dve):
            V = nc.vector
            for c in range(NCH):
                n = CH if c < NCH - 1 else LASTCH
                V.bn_stats(st[:, c, :], v[:, c * CH:c * CH + n]).then_inc(stat.h, 1)
            dve.wait_ge(stat.h, stat.at(NCH))
            V.bn_aggr(mv[:, 0:2], st[:, :, :].rearrange("p a b -> p (a b)")).then_inc(stat.h, 1)
            dve.wait_ge(bn_root.h, bn_root.at(1))
            V.reciprocal(mv[:, 3:4], mv[:, 2:3]).then_inc(stat.h, 1)
            dve.wait_ge(stat.h, stat.at(NCH + 2))
            V.tensor_tensor(mv[:, 4:5], mv[:, 3:4], gain, ALU.mult).then_inc(stat.h, 1)
            dve.wait_ge(stat.h, stat.at(NCH + 3))
            with dve.Fori(0, NU) as s:
                at = cols(s, STRIP)
                V.tensor_scalar(v[:, at], v[:, at], mv[:, 0:1], mv[:, 4:5], ALU.subtract, ALU.mult
                                ).then_inc(bn_scaled.h, 1)

        @block.scalar
        def _(act):
            act.wait_ge(stat.h, stat.at(NCH + 1))
            nc.scalar.activation(mv[:, 2:3], mv[:, 1:2], ACT.Sqrt, bias=k.eps[:, 0:1]).then_inc(bn_root.h, 1)
            with act.Fori(0, NU) as s:
                act.wait_ge(bn_scaled.h, bn_scaled.at(s + 1))
                at = cols(s, STRIP)
                nc.scalar.activation(v[:, at], v[:, at], ACT.Relu, bias=shift)
    k.advance(bn_stat=NCH + 3, bn_root=1, bn_scaled=NU)


def split_rows(k, v, rows, signed, scaled):
    nc = k.nc
    nb = NP // rows
    top, scaled_ok, turned, hi_ok, lo_ok = k.sem("top"), k.sem("scaled"), k.sem("turned"), k.sem("hi_ok"), k.sem("lo_ok")
    m = k.span
    ng = -(-nb // 4)
    EXP1 = 1 << 23
    from_ = v if scaled is None else scaled
    unit = 2.0 ** LN_SCALE if scaled is None else 1.0
    with nc.Block() as block:
        @block.vector
        def _(dve):
            V = nc.vector
            n = [0]
            k.tops = 0

            def link(ins):
                n[0] += 1
                ins.then_inc(top.h, 1)
                dve.wait_ge(top.h, top.at(n[0]))

            def exponents():
                V.tensor_reduce(m[:, 0:1], v[:, :], AX, ALU.max).then_inc(top.h, 1)
                n[0] += 1
                if signed:
                    link(V.tensor_reduce(m[:, 1:2], v[:, :], AX, ALU.min))
                    link(V.scalar_tensor_tensor(m[:, 0:1], m[:, 1:2], -1.0, m[:, 0:1], ALU.mult, ALU.max))
                else:
                    dve.wait_ge(top.h, top.at(n[0]))
                link(V.tensor_scalar(m[:, 0:1], m[:, 0:1], 2.0 ** -60, None, ALU.max))
                mi = m[:, :].bitcast(I32)
                link(V.tensor_scalar(mi[:, 1:2], mi[:, 0:1], 0x7F800000, None, ALU.bitwise_and))
                V.tensor_scalar(mi[:, 2:3], mi[:, 1:2], -1.0, float((2 * 127 + 14) * EXP1), ALU.mult, ALU.add
                                ).then_inc(top.h, 1)
                V.tensor_scalar(mi[:, 3:4], mi[:, 1:2], float(-14 * EXP1), None, ALU.add).then_inc(top.h, 1)
                n[0] += 2
                k.tops = n[0]

            if scaled is None:
                V.memset(m[:, 3:4], 2.0 ** -LN_SCALE)
            else:
                exponents()
            for g in range(ng):
                w = min(4, nb - 4 * g)
                dve.wait_ge(hi_ok.h, hi_ok.at(g + 1))
                V.scalar_tensor_tensor(k.hs[0:rows, 4 * g:4 * g + w, 1, :],
                                       k.bank[g % 4][0:rows, 0:w * P].rearrange("p (a f) -> p a f", f=P), unit,
                                       k.hs[0:rows, 4 * g:4 * g + w, 0, :], ALU.mult, ALU.subtract
                                       ).then_inc(lo_ok.h, 1)

        tops = k.tops

        @block.scalar
        def _(act):
            if scaled is not None:
                act.wait_ge(top.h, top.at(tops))
                with act.Fori(0, NU) as s:
                    at = cols(s, STRIP)
                    nc.scalar.activation(scaled[:, at], v[:, at], ACT.Copy, scale=m[:, 2:3]).then_inc(scaled_ok.h, 1)
            for g in range(ng):
                w = min(4, nb - 4 * g)
                act.wait_ge(turned.h, turned.at(g + 1))
                nc.scalar.activation(k.hs[0:rows, 4 * g:4 * g + w, 0, :],
                                     k.bank[g % 4][0:rows, 0:w * P].rearrange("p (a f) -> p a f", f=P), ACT.Copy,
                                     scale=unit).then_inc(hi_ok.h, 1)

        @block.tensor
        def _(pe):
            for g in range(ng):
                w = min(4, nb - 4 * g)
                if scaled is not None:
                    pe.wait_ge(scaled_ok.h, scaled_ok.at(min(NU, -(-(4 * g + w) * rows // STRIP))))
                if lo_ok.due(g - 3):
                    pe.wait_ge(lo_ok.h, lo_ok.at(g - 3))
                for i in range(w):
                    j = 4 * g + i
                    mm = nc.tensor.transpose(k.bank[g % 4][0:rows, i * P:(i + 1) * P],
                                             from_[:, j * rows:(j + 1) * rows], k.idf[:, :])
                mm.then_inc(turned.h, 1)
    k.advance(top=tops, scaled=NU if scaled is not None else 0, turned=ng, hi_ok=ng, lo_ok=ng)


def pool_neighbours(k, over_src, dst, factor):
    nc = k.nc
    table = k.counts_sd if over_src else k.counts_ds
    rows, per = (SRC_W, US) if over_src else (DST_H, 2 * UD)
    halves = [(t, lo, hi) for t in range(NU) for lo, hi in ((0, 4), (4, per))]
    NH = len(halves)
    NBUF = 7
    assert NH % NBUF == 0
    a_in = [k.sem(f"table_in{b}") for b in range(NBUF)]
    used, acc_full, acc_read, fac_in = k.sem("table_used"), k.sem("acc_full"), k.sem("acc_read"), k.sem("fac_in")
    turn = k.sem("turn_pool")
    acc = [k.bank[h] for h in range(2)]
    with nc.sbuf_tensor(f"tbuf{k.next()}", [P, NBUF, 4, STRIP], F16) as tbuf, nc.Block() as block:
        @block.sync
        def _(sp):
            with sp.Fori(0, NU) as s:
                for i, (t, lo, hi) in enumerate(halves):
                    sp.wait_ge(used.h, used.at(s * NH + i + 1))
                    sp.sem_inc(turn.h, 1)
                    u = s + t * NU if over_src else s * NU + t
                    sp.dma_start(tbuf[0:rows, i % NBUF, 0:hi - lo, :],
                                 table[bass.ds(u, 1), :, lo:hi, :].rearrange("u p r c -> (u p) r c")
                                 ).then_inc(a_in[i % NBUF].h, 16)

        @block.tensor
        def _(pe):
            pe.sem_inc(used.h, NBUF)
            with pe.Fori(0, NU) as s:
                for i, (t, lo, hi) in enumerate(halves):
                    b = i % NBUF
                    pe.wait_ge(a_in[b].h, a_in[b].at(s * (16 * NH // NBUF) + 16 * (i // NBUF + 1)))
                    for h in range(2):
                        if i == 0:
                            pe.wait_ge(acc_read.h, acc_read.at(s * 2 + h + 1))
                        for r in range(lo, hi):
                            kb = t * per + r
                            for part in range(2):
                                mm = nc.tensor.matmul(
                                    acc[h][:, 0:HALF], k.hs[0:rows, kb, part, :],
                                    tbuf[0:rows, b, r - lo, h * HALF:(h + 1) * HALF],
                                    start=(i == 0 and r == lo and part == 0),
                                    stop=(i == NH - 1 and r == hi - 1 and part == 1))
                        if h == 1:
                            mm.then_inc(used.h, 1)
                        elif i == NH - 1:
                            mm.then_inc(acc_full.h, 1)

        @block.scalar
        def _(act):
            if factor is not None:
                act.dma_start(k.C[:, :], k.factors[factor:factor + 1, :].to_broadcast([P, NP])).then_inc(fac_in.h, 16)

        @block.vector
        def _(dve):
            dve.sem_inc(acc_read.h, 2)
            if factor is not None:
                dve.wait_ge(fac_in.h, fac_in.at(16))
            with dve.Fori(0, NU) as s:
                for h in range(2):
                    if h == 0:
                        dve.wait_ge(acc_full.h, acc_full.at(s + 1))
                    else:
                        dve.wait_ge(used.h, used.at(s * NH + NH + NBUF))
                    at = bass.ds(s * STRIP + h * HALF, HALF)
                    if factor is None:
                        ins = nc.vector.tensor_scalar(dst[:, at], acc[h][:, 0:HALF], k.span[:, 3:4], None, ALU.mult)
                    else:
                        ins = nc.vector.scalar_tensor_tensor(dst[:, at], acc[h][:, 0:HALF], k.span[:, 3:4],
                                                             k.C[:, at], ALU.mult, ALU.mult)
                    ins.then_inc(acc_read.h, 1)
    for b in range(NBUF):
        a_in[b].base += 16 * NU * NH // NBUF
    k.advance(table_used=NU * NH + NBUF, acc_full=NU, acc_read=2 * NU + 2)
    if factor is not None:
        k.advance(fac_in=16)


def overflow(k, table, gather_at, scatter_at, width, values=None, dst=None, factor=False):
    nc = k.nc
    i = k.next()
    sums = k.spill_sums if width == D else k.spill_sums_e
    nrows = NP if values is not None else E
    with ExitStack() as ctx:
        def sb(name, shape, dt):
            return ctx.enter_context(nc.sbuf_tensor(f"{name}{i}", shape, dt))

        gidx = sb("gidx", [P, COLS], I32)
        sidx = sb("sidx", [P, COLS], I32)
        gcol = sb("gcol", [P, 1], I32)
        scol = sb("scol", [P, 1], I32)
        put = sb("put", [P, 1], I32)
        scolf = sb("scolf", [P, 1], F32)
        dup = sb("dup", [P, 2], F32)
        rows = sb("rows_g", [P, width], F32)
        old = sb("old", [P, width], F32)
        new = sb("new", [P, width], F32)
        diag = sb("diag", [P, P], F32)
        same = sb("same", [P, P], F32)
        junk = sb("junk_o", [P, P], F32)
        ones = sb("ones", [P, P], F32)
        turnb = sb("turnb", [P, 4, P], F32)
        bank = k.bank

        o_in, o_zero, o_dve, o_pe = k.sem("o_in"), k.sem("o_zero"), k.sem("o_dve"), k.sem("o_pe")
        o_got, o_put = k.sem(f"o_got{i}"), k.sem(f"o_put{i}")
        o_col, o_rows = k.sem("o_col"), k.sem("o_rows")
        o_kept, o_set, o_back, o_T, o_add = (k.sem(n) for n in ("o_kept", "o_set", "o_back", "o_T2", "o_add"))
        NV = 5
        NKEEP = NS if values is not None else 0

        with nc.Block() as block:
            @block.sync
            def _(sp):
                n = sp.value_load(k.spill_n[0:1, 0:1], min_val=0, max_val=E)
                with sp.If(n > 0):
                    sp.dma_start(gidx[:, :], gather_at).then_inc(o_in.h, 16)
                    sp.dma_start(sidx[:, :], scatter_at).then_inc(o_in.h, 16)
                    sp.wait_ge(o_set.h, o_set.at(1))
                    for b in range(NS):
                        sp.dma_start(sums[b * P:(b + 1) * P, :], old[:, :]).then_inc(o_zero.h, 16)
                    for b in range(NKEEP):
                        sp.wait_ge(o_rows.h, o_rows.at(b + 1))
                        sp.dma_start(table[b * P:(b + 1) * P, :], turnb[:, b % 4, :]).then_inc(o_kept.h, 16)
                        sp.wait_ge(o_kept.h, o_kept.at(16 * (b + 1)))
                    sp.wait_ge(o_col.h, o_col.at(COLS + 1))
                    for b in range(NS):
                        if o_add.due(b - 1):
                            sp.wait_ge(o_add.h, o_add.at(b - 1))
                        sp.dma_start(turnb[:, b % 2, 0:width], sums[b * P:(b + 1) * P, :]).then_inc(o_back.h, 16)
                        sp.wait_ge(o_back.h, o_back.at(16 * (b + 1)))
                        sp.sem_inc(o_rows.h, 1)
                    sp.wait_ge(o_add.h, o_add.at(NS))
                    if dst is None:
                        sp.dma_start(k.ea_sums[0:DE, :], k.A[0:DE, :]).then_inc(o_back.h, 16)
                        sp.wait_ge(o_back.h, o_back.at(16 * NS + 16))

            @block.gpsimd
            def _(pool):
                n = pool.value_load(k.spill_n[0:1, 0:1], min_val=0, max_val=E)
                with pool.If(n > 0):
                    g = nc.gpsimd
                    gbound = pool.to_reg(nrows - 1)
                    sbound = pool.to_reg(NP - 1)
                    pool.wait_ge(o_zero.h, o_zero.at(16 * NS))
                    if o_kept.due(16 * NKEEP):
                        pool.wait_ge(o_kept.h, o_kept.at(16 * NKEEP))
                    pool.sem_inc(o_col.h, 1)
                    with pool.Fori(0, COLS) as c:
                        pool.wait_ge(o_dve.h, o_dve.at(c * NV + 1))
                        pool.sem_inc(k.sem("turn_o").h, 1)
                        g.indirect_dma_start(out=rows[:, :], out_offset=None, in_=table,
                                             in_offset=bass.IndirectOffsetOnAxis(gcol[:, 0:1], 0),
                                             bounds_check=gbound, oob_is_err=False).then_inc(o_got.h, 16)
                        g.indirect_dma_start(out=old[:, :], out_offset=None, in_=sums,
                                             in_offset=bass.IndirectOffsetOnAxis(scol[:, 0:1], 0),
                                             bounds_check=sbound, oob_is_err=False).then_inc(o_got.h, 16)
                        pool.wait_ge(o_dve.h, o_dve.at(c * NV + NV))
                        pool.sem_inc(k.sem("turn_o").h, 1)
                        g.indirect_dma_start(out=sums, in_=new[:, :], in_offset=None,
                                             out_offset=bass.IndirectOffsetOnAxis(put[:, 0:1], 0),
                                             bounds_check=sbound, oob_is_err=False).then_inc(o_put.h, 16)
                        pool.wait_ge(o_put.h, o_put.at(c * 16 + 16))
                        pool.sem_inc(k.sem("turn_o").h, 1)
                        pool.sem_inc(o_col.h, 1)

            @block.vector
            def _(dve):
                n = dve.value_load(k.spill_n[0:1, 0:1], min_val=0, max_val=E)
                with dve.If(n > 0):
                    V = nc.vector
                    chain, step = k.sem("o_chain"), [0]
                    V.memset(rows[:, :], 0.0)
                    V.memset(ones[:, :], 1.0)
                    V.memset(old[:, :], 0.0).then_inc(o_set.h, 1)
                    dve.wait_ge(o_in.h, o_in.at(32))
                    dve.wait_ge(o_zero.h, o_zero.at(16 * NS))
                    for b in range(NKEEP):
                        dve.wait_ge(o_T.h, o_T.at(b + 1))
                        if o_kept.due(16 * (b - 3)):
                            dve.wait_ge(o_kept.h, o_kept.at(16 * (b - 3)))
                        V.tensor_copy(turnb[:, b % 4, :], bank[b % 2][:, 0:P]).then_inc(o_rows.h, 1)
                    with dve.Fori(0, COLS) as c:
                        at = bass.ds(c, 1)
                        dve.wait_ge(o_col.h, o_col.at(c + 1))
                        V.tensor_copy(gcol[:, :], gidx[:, at])
                        V.tensor_copy(scolf[:, :], sidx[:, at])
                        V.tensor_copy(scol[:, :], sidx[:, at]).then_inc(o_dve.h, 1)
                        dve.wait_ge(o_dve.h, o_dve.at(c * NV + 1))
                        V.tensor_scalar(diag[:, :], k.idf[:, :], scolf[:, 0:1], None, ALU.mult).then_inc(o_dve.h, 1)
                        dve.wait_ge(o_pe.h, o_pe.at(c * 2 + 1))
                        V.tensor_scalar(same[:, :], bank[2][:, 0:P], scolf[:, 0:1], None, ALU.is_equal
                                        ).then_inc(o_dve.h, 1)
                        dve.wait_ge(o_dve.h, o_dve.at(c * NV + 3))
                        V.scalar_tensor_tensor(junk[:, :], same[:, :], 1.0, k.tri[:, :], ALU.mult, ALU.mult,
                                               accum_out=dup[:, 0:1]).then_inc(chain.h, 1)
                        dve.wait_ge(chain.h, chain.at(c * 2 + 1))
                        V.tensor_scalar(dup[:, 1:2], dup[:, 0:1], 0.5, BIG, ALU.is_gt, ALU.mult).then_inc(chain.h, 1)
                        dve.wait_ge(chain.h, chain.at(c * 2 + 2))
                        V.tensor_tensor(put[:, :], dup[:, 1:2], scolf[:, :], ALU.add).then_inc(o_dve.h, 1)
                        dve.wait_ge(o_pe.h, o_pe.at(c * 2 + 2))
                        V.tensor_tensor(new[:, :], bank[3][:, 0:width], old[:, :], ALU.add).then_inc(o_dve.h, 1)
                    for b in range(NS):
                        dve.wait_ge(o_T.h, o_T.at(NKEEP + b + 1))
                        at = slice(b * P, (b + 1) * P)
                        t = bank[b % 2][0:width, 0:P]
                        if dst is None:
                            V.tensor_tensor(k.A[0:width, at], k.A[0:width, at], t, ALU.add).then_inc(o_add.h, 1)
                            continue
                        if factor:
                            V.tensor_tensor(junk[:, :], t, k.C[:, at], ALU.mult).then_inc(chain.h, 1)
                        else:
                            V.tensor_copy(junk[:, :], t).then_inc(chain.h, 1)
                        dve.wait_ge(chain.h, chain.at(2 * COLS + b + 1))
                        V.tensor_tensor(dst[:, at], dst[:, at], junk[:, :], ALU.add).then_inc(o_add.h, 1)
                        dve.wait_ge(o_add.h, o_add.at(b + 1))

            @block.tensor
            def _(pe):
                n = pe.value_load(k.spill_n[0:1, 0:1], min_val=0, max_val=E)
                with pe.If(n > 0):
                    T = nc.tensor
                    for b in range(NKEEP):
                        pe.wait_ge(o_rows.h, o_rows.at(b - 1))
                        T.transpose(bank[b % 2][:, 0:P], values[:, b * P:(b + 1) * P], k.idf[:, :]).then_inc(o_T.h, 1)
                    with pe.Fori(0, COLS) as c:
                        pe.wait_ge(o_dve.h, o_dve.at(c * NV + 2))
                        T.matmul(bank[2][:, 0:P], ones[:, :], diag[:, :], start=True, stop=True).then_inc(o_pe.h, 1)
                        pe.wait_ge(o_dve.h, o_dve.at(c * NV + 3))
                        pe.wait_ge(o_got.h, o_got.at(c * 32 + 32))
                        T.matmul(bank[3][:, 0:width], same[:, :], rows[:, :], start=True, stop=True
                                 ).then_inc(o_pe.h, 1)
                    for b in range(NS):
                        pe.wait_ge(o_rows.h, o_rows.at(NKEEP + b + 1))
                        if o_add.due(b - 1):
                            pe.wait_ge(o_add.h, o_add.at(b - 1))
                        T.transpose(bank[b % 2][0:width, 0:P], turnb[:, b % 2, 0:width], k.idf[:, :]
                                    ).then_inc(o_T.h, 1)
    k.sem("turn_o")
    k.advance(o_in=32, o_zero=16 * NS, o_dve=NV * COLS, o_pe=2 * COLS,
              o_col=COLS + 1, o_rows=NKEEP + NS, o_kept=16 * NKEEP, o_set=1,
              o_back=16 * NS + (16 if dst is None else 0), o_T2=NKEEP + NS, o_add=NS, o_chain=2 * COLS +
              (0 if dst is None else NS))


def elu_stage(k, pooled, own, factor, bias, dst):
    nc = k.nc
    step, exped = k.sem("elu_step"), k.sem("elu_exp")
    with nc.Block() as block:
        @block.vector
        def _(dve):
            V = nc.vector
            passes = [
                lambda at: V.tensor_tensor(pooled[:, at], pooled[:, at], own[:, at], ALU.add),
                lambda at: V.tensor_tensor(pooled[:, at], pooled[:, at], factor[:, at], ALU.mult),
                lambda at: V.tensor_scalar(pooled[:, at], pooled[:, at], bias, None, ALU.add),
                lambda at: V.tensor_scalar(dst[:, at], pooled[:, at], 0.0, None, ALU.min),
                lambda at: V.scalar_tensor_tensor(dst[:, at], pooled[:, at], 0.0, dst[:, at], ALU.max, ALU.add),
                lambda at: V.tensor_scalar(dst[:, at], dst[:, at], -1.0, None, ALU.add),
            ]
            for i, f in enumerate(passes):
                with dve.Fori(0, NU) as s:
                    if i == 4:
                        dve.wait_ge(exped.h, exped.at(s + 1))
                    elif i:
                        dve.wait_ge(step.h, step.at((i - 1) * NU + s + 1))
                    f(cols(s, STRIP)).then_inc(step.h, 1)

        @block.scalar
        def _(act):
            with act.Fori(0, NU) as s:
                act.wait_ge(step.h, step.at(3 * NU + s + 1))
                at = cols(s, STRIP)
                nc.scalar.activation(dst[:, at], dst[:, at], ACT.Exp).then_inc(exped.h, 1)
    k.advance(elu_step=6 * NU, elu_exp=NU)


def times(k, v, factor_row):
    nc = k.nc
    f_in, multiplied = k.sem("times_in"), k.sem("multiplied")
    with nc.Block() as block:
        @block.sync
        def _(sp):
            sp.dma_start(k.C[:, :], k.factors[factor_row:factor_row + 1, :].to_broadcast([P, NP])).then_inc(f_in.h, 16)

        @block.vector
        def _(dve):
            dve.wait_ge(f_in.h, f_in.at(16))
            with dve.Fori(0, NU) as s:
                at = cols(s, STRIP)
                nc.vector.tensor_tensor(v[:, at], v[:, at], k.C[:, at], ALU.mult).then_inc(multiplied.h, 1)
    k.advance(times_in=16, multiplied=NU)


def load_ea(k, into):
    nc = k.nc
    got = k.sem("easum_in")
    with nc.Block() as block:
        @block.sync
        def _(sp):
            sp.dma_start(into[0:3 * DE, :], k.ea_sums).then_inc(got.h, 16)
            sp.wait_ge(got.h, got.at(16))
    k.advance(easum_in=16)


def program(nc, w, out):
    with ExitStack() as ctx:
        k = Core(nc, ctx)

        def sb(name, shape, dt):
            return ctx.enter_context(nc.sbuf_tensor(name, shape, dt))

        k.iota = sb("iota", [P, 256], BF16)
        k.id16 = sb("id16", [P, P], F16)
        k.idb = sb("idb", [P, P], BF16)
        k.idf = sb("idf", [P, P], F32)
        k.tri = sb("tri", [P, P], F32)
        k.avg = sb("avg", [P, P], F32)
        k.eps = sb("eps", [P, 1], F32)
        k.gather = sb("gather", [P, NCH, NCH], F32)
        k.spread = sb("spread", [NCH, NCH, D], F32)
        k.zero = sb("zero", [P, 1], F32)
        k.slots = nc.dram_tensor("slots", [NBKT * CAP, PW], F32).ap()
        k.factors = nc.dram_tensor("factors", [3, NP], F32).ap()
        k.counts_ds = nc.dram_tensor("counts_ds", [NU * NU, DST_H, 2 * UD, STRIP], F16).ap()
        k.counts_sd = nc.dram_tensor("counts_sd", [NU * NU, P, US, STRIP], F16).ap()
        k.ea_sums = nc.dram_tensor("ea_sums", [3 * DE, NP], F32).ap()
        k.spill_src = nc.dram_tensor("spill_src", [P, COLS], I32).ap()
        k.spill_dst = nc.dram_tensor("spill_dst", [P, COLS], I32).ap()
        k.spill_edge = nc.dram_tensor("spill_edge", [P, COLS], I32).ap()
        k.spill_n = nc.dram_tensor("spill_n", [1, 1], I32).ap()
        k.spill_rows = nc.dram_tensor("spill_rows", [NP, D], F32).ap()
        k.spill_sums = nc.dram_tensor("spill_sums", [NP, D], F32).ap()
        k.spill_sums_e = nc.dram_tensor("spill_sums_e", [NP, DE], F32).ap()
        k.x_kept = nc.dram_tensor("x_kept", [P, NP], F32).ap()
        constants(k)
        rank_edges(k, w["src"], w["dst"], w["edge_attr_32"])
        build_adjacency(k)

        k.A = sb("A", [P, NP], F32)
        k.B = sb("B", [P, NP], F32)
        k.C = sb("C", [P, NP], F32)
        k.H = sb("H", [P, NP], F32)
        k.hs = sb("hs", [P, NP // DST_H, 2, P], F16)
        k.weights = sb("weights", [P, 20, D], F32)
        k.vectors = sb("vectors", [P, 32], F32)
        k.bn_stats = sb("bn_stats", [P, NCH, 6], F32)
        k.bn_mv = sb("bn_mv", [P, 8], F32)
        k.span = sb("span", [P, 4], F32)
        k.rstd = sb("rstd", [NCH, CH], F32)
        k.bank = [ctx.enter_context(nc.psum_tensor(f"acc{i}", [P, 512], F32)) for i in range(8)]
        load_weights(k, w)
        A, B, C, H, W, vec = k.A, k.B, k.C, k.H, k.W, k.vec
        load_ea(k, A)
        overflow(k, w["edge_attr_32"], k.spill_edge, k.spill_dst, DE)
        load_x(k, w["x"])

        layer_norm(k, A, H)
        for l in range(2):
            v0 = 6 * l
            split_rows(k, H, DST_H, False, B if l else None)
            pool_neighbours(k, False, B, 0)
            overflow(k, k.spill_rows, k.spill_dst, k.spill_src, D, H, B, True)
            product(k, [(W["ab"[l] + "0"], B)], B, ACT.Identity, vec(v0))
            batch_norm_relu(k, B, vec(v0 + 1), vec(v0 + 2))
            product(k, [(W["ab"[l] + "1"], B)], H, ACT.Identity, vec(v0 + 3))
            batch_norm_relu(k, H, vec(v0 + 4), vec(v0 + 5))
        residual(k, H)

        layer_norm(k, A, H)
        for l in range(4):
            split_rows(k, H, SRC_W, False, B if l else None)
            pool_neighbours(k, True, B, 1)
            overflow(k, k.spill_rows, k.spill_src, k.spill_dst, D, H, B, True)
            product(k, [(W[f"self{l}"], H), (W[f"neigh{l}"], B)], H, ACT.Relu if l < 3 else ACT.Identity, vec(12 + l))
        residual(k, H)

        layer_norm(k, A, H)
        split_rows(k, H, SRC_W, False, None)
        pool_neighbours(k, True, B, None)
        overflow(k, k.spill_rows, k.spill_src, k.spill_dst, D, H, B)
        load_ea(k, C)
        product(k, [(W["msg"], B), (W["msg_e"], C[0:3 * DE])], B, ACT.Identity, k.zero[:, 0:1])
        product(k, [(W["up_h"], H), (W["up_m"], B)], A, ACT.Relu, vec(16))
        layer_norm(k, A, B, vec(17), vec(18))
        product(k, [(W["down"], B)], A, ACT.Relu, vec(19))
        layer_norm(k, A, B, vec(20), vec(21))
        product(k, [(W["node"], H), (k.idf[:, :], B)], A, ACT.Identity, k.zero[:, 0:1])
        layer_norm(k, A, H, vec(22), vec(23))
        residual(k, H)

        layer_norm(k, A, H)
        for l in range(2):
            product(k, [(W[f"g{l}"], H)], A, ACT.Identity, k.zero[:, 0:1])
            times(k, A, 2)
            split_rows(k, A, SRC_W, True, B)
            pool_neighbours(k, True, B, None)
            overflow(k, k.spill_rows, k.spill_src, k.spill_dst, D, A, B)
            elu_stage(k, B, A, C, vec(24 + l), H)
        residual(k, H)
        store_out(k, out)


_INS = ['x', 'src', 'dst', 'edge_attr_32',
        'L0_gnn_l0_W0', 'L0_gnn_l0_b0', 'L0_gnn_l0_W1', 'L0_gnn_l0_b1',
        'L0_gnn_l0_mbn_g', 'L0_gnn_l0_mbn_b', 'L0_gnn_l0_bn_g', 'L0_gnn_l0_bn_b',
        'L0_gnn_l1_W0', 'L0_gnn_l1_b0', 'L0_gnn_l1_W1', 'L0_gnn_l1_b1',
        'L0_gnn_l1_mbn_g', 'L0_gnn_l1_mbn_b', 'L0_gnn_l1_bn_g', 'L0_gnn_l1_bn_b',
        'L1_gnn_W_self', 'L1_gnn_W_neigh', 'L1_gnn_bias',
        'L2_gnn_W_message', 'L2_gnn_W_node', 'L2_gnn_W1', 'L2_gnn_b1', 'L2_gnn_ln1_g', 'L2_gnn_ln1_b',
        'L2_gnn_W2', 'L2_gnn_b2', 'L2_gnn_ln2_g', 'L2_gnn_ln2_b', 'L2_gnn_ln_g', 'L2_gnn_ln_b',
        'L3_gnn_W1', 'L3_gnn_b1', 'L3_gnn_W2', 'L3_gnn_b2']


def kernel(**inputs):
    import numpy as _np
    import concourse.bacc as _bacc
    from concourse import mybir as _mybir
    from concourse.bass_utils import run_bass_kernel_spmd as _run

    nc = _bacc.Bacc("TRN2", target_bir_lowering=False, num_devices=1)
    arrays, args = {}, {}
    for name in _INS:
        a = _np.ascontiguousarray(inputs[name])
        arrays[f"in_{name}_dram"] = a
        args[name] = nc.dram_tensor(f"in_{name}_dram", a.shape, _mybir.dt.from_np(a.dtype), kind="ExternalInput").ap()
    out = nc.dram_tensor("out_0_dram", (N, D), _mybir.dt.float32, kind="ExternalOutput").ap()
    program(nc, args, out)
    r = _run(nc, [arrays], core_ids=[0])
    return r.results[0]["out_0_dram"]
```

```python
from contextlib import ExitStack

import concourse.bass as bass
from concourse import mybir

F32 = mybir.dt.float32
F16 = mybir.dt.float16
BF16 = mybir.dt.bfloat16
I32 = mybir.dt.int32
ALU = mybir.AluOpType
ACT = mybir.ActivationFunctionType
AX = mybir.AxisListType.X

P = 128
D = 128
N = 6250
E = 100000
DE = 32
EPS = 1e-5

SRC_W = 128
DST_W = 224
NS = -(-N // SRC_W)
ND = -(-N // DST_W)
NP = NS * SRC_W
DST_H = DST_W // 2
US = 7
UD = 4
UB = US * UD
STRIP = US * SRC_W
NU = NP // STRIP
HALF = STRIP // 2
NBKT = NS * ND
CAP = 128
assert NP == ND * DST_W and STRIP == UD * DST_W and NP == NU * STRIP

COLS = 784
GR = 8
NG = COLS // GR
LASTP = E // COLS
LASTC = E - LASTP * COLS
FULLP = 112
PW = 2 + DE
FAR = 8000
BIG = float(1 << 20)

LN_SCALE = 12
CH = HALF
NCH = NP // CH
LASTCH = N - (NCH - 1) * CH


class Sem:

    def __init__(self, handle):
        self.h = handle
        self.base = 0

    def at(self, value):
        return self.base + value

    def due(self, value):
        return not isinstance(value, int) or self.base + value > 0


def cols(c, w=CH):
    return bass.ds(c * w, w)


def chunk_pairs(eng, body):
    with eng.Fori(0, NCH // 2) as q:
        for b in range(2):
            body(q * 2 + b, b)


class Core:

    def __init__(self, nc, ctx):
        self.nc = nc
        self.ctx = ctx
        self.sems = {}
        self.n = 0

    def sem(self, name):
        if name not in self.sems:
            self.sems[name] = Sem(self.ctx.enter_context(self.nc.semaphore(name)))
        return self.sems[name]

    def next(self):
        self.n += 1
        return self.n

    def advance(self, **totals):
        for name, n in totals.items():
            self.sems[name].base += n


def constants(k):
    nc = k.nc
    fill = k.sem("fill")
    with nc.Block() as block:
        @block.gpsimd
        def _(pool):
            g = nc.gpsimd
            g.iota(k.iota[:, :], [[1, 256]], base=0, channel_multiplier=0, allow_small_or_imprecise_dtypes=True)
            for m in (k.id16, k.idb, k.idf):
                g.memset(m[:, :], 0.0).then_inc(fill.h, 1)
            g.memset(k.tri[:, :], 1.0).then_inc(fill.h, 1)
            g.memset(k.avg[:, :], 1.0 / D)
            g.memset(k.gather[:, :, :], 1.0 / D).then_inc(fill.h, 1)
            g.memset(k.spread[:, :, :], 1.0).then_inc(fill.h, 1)
            g.memset(k.eps[:, :], EPS)
            g.memset(k.zero[:, :], 0.0)
            pool.wait_ge(fill.h, fill.at(6))
            g.affine_select(out=k.gather[:, :, :], in_=k.gather[:, :, :], compare_op=ALU.is_equal, fill=0.0, base=0,
                            pattern=[[-1, NCH], [1, NCH]], channel_multiplier=0)
            g.affine_select(out=k.spread[:, :, :], in_=k.spread[:, :, :], compare_op=ALU.is_equal, fill=0.0, base=0,
                            pattern=[[-1, NCH], [0, D]], channel_multiplier=1)
            for m in (k.id16, k.idb, k.idf):
                g.affine_select(out=m[:, :], in_=m[:, :], compare_op=ALU.not_equal, fill=1.0, base=0,
                                pattern=[[-1, P]], channel_multiplier=1)
            g.affine_select(out=k.tri[:, :], in_=k.tri[:, :], compare_op=ALU.is_gt, fill=0.0, base=0,
                            pattern=[[-1, P]], channel_multiplier=1)


def rank_edges(k, src, dst, ea):
    nc = k.nc
    with ExitStack() as ctx:
        def sb(name, shape, dt):
            return ctx.enter_context(nc.sbuf_tensor(name, shape, dt))

        def ps(name, shape, dt):
            return ctx.enter_context(nc.psum_tensor(name, shape, dt))

        pay = sb("pay", [P, COLS, PW], F32)
        ring = sb("ring", [P, 2, GR, PW], F32)
        si = sb("si", [P, COLS], I32)
        di = sb("di", [P, COLS], I32)
        ti = sb("ti", [P, COLS], I32)
        tj = sb("tj", [P, COLS], I32)
        srcb = sb("srcb", [P, COLS], F32)
        dstw = sb("dstw", [P, COLS], F32)
        srcl = sb("srcl", [P, COLS], F32)
        dstl = sb("dstl", [P, COLS], F32)
        keyf = sb("keyf", [P, COLS], F32)
        key16 = sb("key16", [P, COLS], F16)
        rowbase = sb("rowbase", [P, COLS], F32)
        row = sb("row", [P, 2 * GR], I32)
        parts = sb("parts", [P, 2, 2, GR], F32)
        rank = sb("rank", [P, GR], F32)
        hot = sb("hot", [P, 4, 64 + ND + SRC_W + DST_W], BF16)
        dneg = sb("dneg", [P, COLS], F32)
        away = sb("away", [P, 2, DST_W], BF16)
        H_DW, H_SL, H_DL, H_END = 64, 64 + ND, 64 + ND + SRC_W, 64 + ND + SRC_W + DST_W
        blockT = sb("blockT", [64, 2, P], BF16)
        before = sb("before", [64, 2, ND], BF16)
        junk = sb("junk", [P, 2 * GR, P], F32)
        over = sb("over", [P, COLS], F32)
        oven = sb("oven", [P, 2], F32)
        oveni = sb("oveni", [1, 1], I32)
        empty = sb("empty", [P, 98, PW], F32)
        zeros = sb("zeros", [P, 256], BF16)
        degs = sb("degs", [NS, SRC_W], F32)
        degd = sb("degd", [ND, DST_W], F32)
        t3 = sb("t3", [ND, DST_W], F32)
        cnt_s = ps("cnt_s", [P, 512], F32)
        cnt_d = ps("cnt_d", [P, 512], F32)
        keys = [ps(f"keys{b}", [P, 512], F32) for b in range(2)]
        look = [ps(f"look{b}", [P, 512], F32) for b in range(2)]
        flip = [ps(f"flip{b}", [P, 1024], BF16) for b in range(2)]

        idx_in, slots_init = k.sem("idx_in"), k.sem("slots_init")
        ea_in = [k.sem(f"ea_in{i}") for i in range(COLS // FULLP)]
        pads_set, empty_set, chain = k.sem("pads_set"), k.sem("empty_set"), k.sem("chain")
        dhot_step = k.sem("dhot_step")
        prepped, hot_ready, keyrow = k.sem("prepped"), k.sem("hot_ready"), k.sem("keyrow")
        flipped, counted, snapped = k.sem("flipped"), k.sem("counted"), k.sem("snapped")
        flip_copied, looked = k.sem("flip_copied"), k.sem("looked")
        within_done, base_done = k.sem("within_done"), k.sem("base_done")
        rows_ready, row_read, ring_full = k.sem("rows_ready"), k.sem("row_read"), k.sem("ring_full")
        scattered = [k.sem("scattered0"), k.sem("scattered1")]
        turn, deg_out, deg_ready, deg_pads = k.sem("turn"), k.sem("deg_out"), k.sem("deg_ready"), k.sem("deg_pads")
        tail, rooted, spill, spill_no = k.sem("tail"), k.sem("rooted"), k.sem("spill"), k.sem("spill_no")

        with nc.Block() as block:
            @block.sync
            def _(sp):
                sp.wait_ge(pads_set.h, pads_set.at(2))
                for a, t in ((src, si), (dst, di)):
                    for p0, p1 in ((0, FULLP), (FULLP, LASTP)):
                        sp.dma_start(t[p0:p1, :], a[p0 * COLS:p1 * COLS].rearrange("(p c) -> p c", c=COLS)
                                     ).then_inc(idx_in.h, 16)
                    sp.dma_start(t[LASTP:P, 0:LASTC], a[LASTP * COLS:E].rearrange("(p c) -> p c", p=1)
                                 ).then_inc(idx_in.h, 16)
                sp.wait_ge(empty_set.h, empty_set.at(2))
                flat = k.slots.rearrange("(p r) w -> p r w", p=P)
                for q in range(NBKT // 98):
                    sp.dma_start(flat[:, q * 98:(q + 1) * 98, :], empty[:, :, :]).then_inc(slots_init.h, 16)
                sp.wait_ge(deg_ready.h, deg_ready.at(3))
                sp.dma_start(k.factors[0].rearrange("(p c) -> p c", c=SRC_W), degs[:, :]).then_inc(deg_out.h, 16)
                sp.dma_start(k.factors[1].rearrange("(p c) -> p c", c=DST_W), degd[:, :]).then_inc(deg_out.h, 16)
                sp.dma_start(k.factors[2].rearrange("(p c) -> p c", c=DST_W), t3[:, :]).then_inc(deg_out.h, 16)
                sp.wait_ge(deg_out.h, deg_out.at(48))
                sp.wait_ge(base_done.h, base_done.at(COLS))
                for p0, p1 in ((0, FULLP), (FULLP, LASTP)):
                    sp.dma_start(si[p0:p1, :], src[p0 * COLS:p1 * COLS].rearrange("(p c) -> p c", c=COLS)
                                 ).then_inc(idx_in.h, 16)
                sp.dma_start(si[LASTP:P, 0:LASTC], src[LASTP * COLS:E].rearrange("(p c) -> p c", p=1)
                             ).then_inc(idx_in.h, 16)
                sp.wait_ge(spill.h, spill.at(6))
                sp.dma_start(k.spill_src, si[:, :]).then_inc(deg_out.h, 16)
                sp.dma_start(k.spill_dst, di[:, :]).then_inc(deg_out.h, 16)
                sp.dma_start(k.spill_edge, ti[:, :]).then_inc(deg_out.h, 16)
                sp.dma_start(k.spill_n, oveni[:, :]).then_inc(deg_out.h, 16)
                sp.wait_ge(deg_out.h, deg_out.at(48 + 64))
                for b in range(2):
                    sp.wait_ge(scattered[b].h, scattered[b].at(16 * COLS // 2))

            @block.gpsimd
            def _(pool):
                g = nc.gpsimd
                bound = pool.to_reg(NBKT * CAP - 1)
                pool.wait_ge(slots_init.h, slots_init.at(16 * (NBKT // 98)))

                with pool.Fori(0, NG // 2) as q:
                    for b in range(2):
                        pool.wait_ge(rows_ready.h, rows_ready.at(q * 2 + b + 1))
                        pool.sem_inc(turn.h, 1)
                        for j in range(GR):
                            g.indirect_dma_start(
                                out=k.slots, in_=ring[:, b, j, :], in_offset=None,
                                out_offset=bass.IndirectOffsetOnAxis(row[:, b * GR + j:b * GR + j + 1], 0),
                                bounds_check=bound, oob_is_err=False, engine_sem=row_read.h,
                            ).then_inc(scattered[b].h, 16)
                pool.wait_ge(deg_pads.h, deg_pads.at(1))
                g.affine_select(out=degs[:, :], in_=degs[:, :], compare_op=ALU.is_ge, fill=1.0, base=N - 1,
                                pattern=[[-1, SRC_W]], channel_multiplier=-SRC_W).then_inc(deg_pads.h, 1)
                pool.wait_ge(prepped.h, prepped.at(1))
                pool.wait_ge(spill.h, spill.at(1))
                g.iota(ti[:, :], [[1, COLS]], base=0, channel_multiplier=COLS).then_inc(spill_no.h, 1)
                g.partition_all_reduce(oven[:, 1:2], oven[:, 0:1], P, bass.bass_isa.ReduceOp.add
                                       ).then_inc(spill_no.h, 1)

            @block.vector
            def _(dve):
                V = nc.vector
                done = [0]

                def link(ins):
                    done[0] += 1
                    ins.then_inc(chain.h, 1)
                    dve.wait_ge(chain.h, chain.at(done[0]))

                V.memset(si[:, :], FAR).then_inc(pads_set.h, 1)
                V.memset(di[:, :], FAR).then_inc(pads_set.h, 1)
                link(V.memset(empty[:, :, :], 0.0))
                V.memset(zeros[:, :], 0.0).then_inc(empty_set.h, 1)
                V.memset(empty[:, :, 0:2], -1.0).then_inc(empty_set.h, 1)
                V.memset(pay[96:P, LASTC:COLS, :], 0.0).then_inc(pads_set.h, 1)
                dve.wait_ge(idx_in.h, idx_in.at(96))
                V.tensor_scalar(ti[:, :], si[:, :], 7, None, ALU.logical_shift_right)
                V.tensor_scalar(si[:, :], si[:, :], SRC_W - 1, None, ALU.bitwise_and)
                link(V.tensor_scalar(tj[:, :], di[:, :], 5, None, ALU.logical_shift_right))
                V.tensor_copy(srcb[:, :], ti[:, :])
                V.tensor_copy(srcl[:, :], si[:, :])
                link(V.tensor_scalar(tj[:, :], tj[:, :], 9363.0, None, ALU.mult))
                link(V.tensor_scalar(tj[:, :], tj[:, :], 16, None, ALU.logical_shift_right))
                link(V.tensor_copy(dstw[:, :], tj[:, :]))
                V.tensor_copy(dstl[:, :], di[:, :])
                link(V.tensor_scalar(tj[:, :], tj[:, :], 2, None, ALU.logical_shift_right))
                link(V.scalar_tensor_tensor(dstl[:, :], dstw[:, :], -float(DST_W), dstl[:, :], ALU.mult, ALU.add))
                link(V.scalar_tensor_tensor(keyf[:, :], tj[:, :], float(UB - UD), dstw[:, :], ALU.mult, ALU.add))
                link(V.scalar_tensor_tensor(keyf[:, :], srcb[:, :], float(UD), keyf[:, :], ALU.mult, ALU.add))
                link(V.tensor_scalar(ti[:, :], ti[:, :], 9363.0, None, ALU.mult))
                link(V.tensor_scalar(ti[:, :], ti[:, :], 16, None, ALU.logical_shift_right))
                link(V.scalar_tensor_tensor(keyf[:, :], ti[:, :], float(NU * UB - US * UD), keyf[:, :],
                                            ALU.mult, ALU.add))
                V.tensor_copy(key16[:, :], keyf[:, :])
                link(V.tensor_scalar(rowbase[:, :], keyf[:, :], float(NBKT), BIG, ALU.is_ge, ALU.mult))
                link(V.tensor_tensor(rowbase[:, :], rowbase[:, :], keyf[:, :], ALU.add))
                dve.wait_ge(pads_set.h, pads_set.at(3))
                link(V.tensor_copy(pay[:, :, 0], srcl[:, :]))
                link(V.tensor_copy(pay[:, :, 1], dstl[:, :]))
                V.tensor_scalar(dneg[:, :], dstl[:, :], -1.0, None, ALU.mult)
                V.memset(degs[:, :], 0.0).then_inc(prepped.h, 1)
                dve.wait_ge(prepped.h, prepped.at(1))

                def one_hots(c, b):
                    if counted.due(c - 2):
                        dve.wait_ge(counted.h, counted.at(c - 2))
                    if base_done.due(c - 3):
                        dve.wait_ge(base_done.h, base_done.at(c - 3))
                    at = bass.ds(c, 1)
                    V.tensor_scalar(hot[:, b, 0:64], k.iota[:, 0:64], srcb[:, at], None, ALU.is_equal)
                    V.tensor_scalar(hot[:, b, H_DW:H_SL], k.iota[:, 0:ND], dstw[:, at], None, ALU.is_equal)
                    V.tensor_scalar(hot[:, b, H_SL:H_DL], k.iota[:, 0:SRC_W], srcl[:, at], None, ALU.is_equal
                                    ).then_inc(hot_ready.h, 1)

                def within(c, b, j):
                    dve.wait_ge(keyrow.h, keyrow.at(c + 1))
                    V.scalar_tensor_tensor(junk[:, j, :], keys[j % 2][:, 0:P], keyf[:, bass.ds(c, 1)],
                                           k.tri[:, :], ALU.is_equal, ALU.mult,
                                           accum_out=parts[:, b, 0, j:j + 1]).then_inc(within_done.h, 1)

                def base(c, b, j):
                    dve.wait_ge(looked.h, looked.at(c + 1))
                    V.scalar_tensor_tensor(junk[:, GR + j, 0:ND], look[j % 2][:, 0:ND], 1.0,
                                           hot[:, j % 4, H_DW:H_SL], ALU.mult, ALU.mult,
                                           accum_out=parts[:, b, 1, j:j + 1]).then_inc(base_done.h, 1)

                def finish(g, b):
                    dve.wait_ge(base_done.h, base_done.at((g + 1) * GR))
                    V.tensor_tensor(rank[:, :], parts[:, b, 0, :], parts[:, b, 1, :], ALU.add).then_inc(chain.h, 1)
                    dve.wait_ge(chain.h, chain.at(g + done[0] + 1))
                    V.tensor_scalar(over[:, bass.ds(g * GR, GR)], rank[:, :], float(CAP) - 0.5, None, ALU.is_gt)
                    if row_read.due((g - 1) * GR):
                        dve.wait_ge(row_read.h, row_read.at((g - 1) * GR))
                    dve.wait_ge(ring_full.h, ring_full.at(g + 1))
                    V.scalar_tensor_tensor(row[:, b * GR:(b + 1) * GR], rank[:, :], float(NBKT),
                                           rowbase[:, bass.ds(g * GR, GR)], ALU.mult, ALU.add
                                           ).then_inc(rows_ready.h, 1)

                def groups(q, first=False, last=False):
                    for b in range(2):
                        g = q * 2 + b
                        for j in range(GR):
                            c = g * GR + j
                            if not (last and b == 1 and j == GR - 1):
                                one_hots(c + 1, (j + 1) % 4)
                            within(c, b, j)
                            if j:
                                base(c - 1, b, j - 1)
                            elif not (first and b == 0):
                                base(c - 1, 1 - b, GR - 1)
                            if j == 1 and not (first and b == 0):
                                finish(g - 1, 1 - b)

                one_hots(0, 0)
                groups(0, first=True)
                with dve.Fori(1, NG // 2 - 1) as q:
                    groups(q)
                groups(NG // 2 - 1, last=True)
                base(COLS - 1, 1, GR - 1)
                finish(NG - 1, 1)
                dve.wait_ge(counted.h, counted.at(COLS + 1))
                V.tensor_copy(degs[:, :], cnt_s[0:NS, ND:ND + SRC_W]).then_inc(deg_pads.h, 1)
                V.tensor_copy(degd[:, :], cnt_d[0:ND, 0:DST_W]).then_inc(tail.h, 1)
                dve.wait_ge(tail.h, tail.at(1))
                V.tensor_scalar(t3[:, :], degd[:, :], 1.0, None, ALU.add).then_inc(tail.h, 1)
                dve.wait_ge(tail.h, tail.at(2))
                V.tensor_scalar(degd[:, :], degd[:, :], 1.0, None, ALU.max).then_inc(tail.h, 1)
                dve.wait_ge(tail.h, tail.at(3))
                V.reciprocal(degd[:, :], degd[:, :]).then_inc(deg_ready.h, 1)
                dve.wait_ge(deg_pads.h, deg_pads.at(2))
                V.reciprocal(degs[:, :], degs[:, :]).then_inc(deg_ready.h, 1)
                dve.wait_ge(rooted.h, rooted.at(1))
                V.reciprocal(t3[:, :], t3[:, :]).then_inc(deg_ready.h, 1)
                V.tensor_reduce(oven[:, 0:1], over[:, :], AX, ALU.add).then_inc(spill.h, 1)
                dve.wait_ge(spill.h, spill.at(1))
                V.tensor_scalar(over[:, :], over[:, :], -BIG, BIG, ALU.mult, ALU.add).then_inc(spill.h, 1)
                dve.wait_ge(spill.h, spill.at(2))
                dve.wait_ge(idx_in.h, idx_in.at(96 + 48))
                V.tensor_tensor(si[:, :], si[:, :], over[:, :], ALU.add).then_inc(spill.h, 1)
                V.tensor_tensor(di[:, :], di[:, :], over[:, :], ALU.add).then_inc(spill.h, 1)
                dve.wait_ge(spill_no.h, spill_no.at(1))
                V.tensor_tensor(ti[:, :], ti[:, :], over[:, :], ALU.add).then_inc(spill.h, 1)
                dve.wait_ge(spill_no.h, spill_no.at(2))
                V.tensor_copy(oveni[:, :], oven[0:1, 1:2]).then_inc(spill.h, 1)

            @block.scalar
            def _(act):
                A = nc.scalar

                def load_features(i):
                    c0, c1 = i * FULLP, (i + 1) * FULLP
                    m = min(c1, LASTC)
                    if m < c1:
                        act.wait_ge(pads_set.h, pads_set.at(3))
                    for p0, p1 in ((0, FULLP), (FULLP, LASTP)):
                        act.dma_start(pay[p0:p1, c0:c1, 2:PW],
                                      ea[p0 * COLS:p1 * COLS, :].rearrange("(p c) f -> p c f", c=COLS)[:, c0:c1, :]
                                      ).then_inc(ea_in[i].h, 16)
                    if m > c0:
                        act.dma_start(pay[LASTP:P, c0:m, 2:PW],
                                      ea[LASTP * COLS + c0:LASTP * COLS + m, :].rearrange("(p c) f -> p c f", p=1)
                                      ).then_inc(ea_in[i].h, 16)

                load_features(0)
                act.wait_ge(prepped.h, prepped.at(1))

                def square(c, b):
                    A.activation(away[:, b % 2, :], k.iota[:, 0:DST_W], ACT.Square, bias=dneg[:, bass.ds(c, 1)]
                                 ).then_inc(dhot_step.h, 1)

                def one_hot(c, b):
                    act.wait_ge(dhot_step.h, dhot_step.at(2 * c + 1))
                    A.activation(hot[:, b, H_DL:H_END], away[:, b % 2, :], ACT.Relu, bias=1.0, scale=-1.0
                                 ).then_inc(dhot_step.h, 1)

                for c in range(2):
                    square(c, c)
                    one_hot(c, c)

                def groups(q, last=False):
                    for b in range(2):
                        g = q * 2 + b
                        for j in range(GR):
                            c = g * GR + j
                            ahead = not (last and b == 1 and j >= GR - 2)
                            act.wait_ge(counted.h, counted.at(c + 1))
                            if looked.due(c - 1):
                                act.wait_ge(looked.h, looked.at(c - 1))
                            A.activation(before[0:NS, j % 2, :], cnt_s[0:NS, 0:ND], ACT.Copy
                                         ).then_inc(snapped.h, 1)
                            if ahead:
                                square(c + 2, (j + 2) % 4)
                            act.wait_ge(flipped.h, flipped.at(c + 1))
                            A.activation(blockT[0:NS, j % 2, :], flip[j % 2][0:NS, 0:P], ACT.Copy
                                         ).then_inc(flip_copied.h, 1)
                            if ahead:
                                one_hot(c + 2, (j + 2) % 4)
                            if j == GR - 2:
                                if scattered[b].due(q * (16 * GR)):
                                    act.wait_ge(scattered[b].h, scattered[b].at(q * (16 * GR)))
                                A.activation(ring[:, b, :, :], pay[:, cols(g, GR), :], ACT.Copy
                                             ).then_inc(ring_full.h, 1)

                turns = FULLP // (2 * GR)
                for i, loaded in enumerate(ea_in):
                    act.wait_ge(loaded.h, loaded.at(48 if LASTC > i * FULLP else 32))
                    groups(i * turns)
                    if i + 1 < len(ea_in):
                        load_features(i + 1)
                    final = i + 1 == len(ea_in)
                    with act.Fori(i * turns + 1, (i + 1) * turns - final) as q:
                        groups(q)
                groups(NG // 2 - 1, last=True)
                act.wait_ge(tail.h, tail.at(2))
                A.activation(t3[:, :], t3[:, :], ACT.Sqrt).then_inc(rooted.h, 1)

            @block.tensor
            def _(pe):
                T = nc.tensor
                pe.wait_ge(prepped.h, prepped.at(1))
                T.matmul(cnt_s[0:NS, 0:ND + SRC_W], zeros[:, 0:NS], zeros[:, 0:ND + SRC_W], start=True, stop=True)
                T.matmul(cnt_d[0:ND, 0:DST_W], zeros[:, 0:ND], zeros[:, 0:DST_W], start=True, stop=True
                         ).then_inc(counted.h, 1)

                def lookup(c, b):
                    pe.wait_ge(flip_copied.h, flip_copied.at(c + 1))
                    if base_done.due(c - 1):
                        pe.wait_ge(base_done.h, base_done.at(c - 1))
                    T.matmul(look[b][:, 0:ND], blockT[0:NS, b, :], before[0:NS, b, :],
                             start=True, stop=True).then_inc(looked.h, 1)

                def groups(g2, first=False):
                    for b in range(2):
                        g = g2 * 2 + b
                        for j in range(GR):
                            c = g * GR + j
                            o = j % 4
                            if within_done.due(c - 1):
                                pe.wait_ge(within_done.h, within_done.at(c - 1))
                            T.matmul(keys[j % 2][:, 0:P], key16[:, bass.ds(c, 1)].to_broadcast([P, P]),
                                     k.id16[:, :], start=True, stop=True).then_inc(keyrow.h, 1)
                            pe.wait_ge(hot_ready.h, hot_ready.at(c + 1))
                            if flip_copied.due(c - 1):
                                pe.wait_ge(flip_copied.h, flip_copied.at(c - 1))
                            T.transpose(flip[j % 2][:, 0:P], hot[:, o, 0:P], k.idb[:, :]).then_inc(flipped.h, 1)
                            if not (first and b == 0 and j == 0):
                                lookup(c - 1, (j + 1) % 2)
                            pe.wait_ge(snapped.h, snapped.at(c + 1))
                            T.matmul(cnt_s[0:NS, 0:ND + SRC_W], hot[:, o, 0:NS], hot[:, o, H_DW:H_DL],
                                     start=False, stop=True, skip_group_check=True)
                            pe.wait_ge(dhot_step.h, dhot_step.at(2 * c + 2))
                            T.matmul(cnt_d[0:ND, 0:DST_W], hot[:, o, H_DW:H_SL], hot[:, o, H_DL:H_END],
                                     start=False, stop=True, skip_group_check=True).then_inc(counted.h, 1)

                groups(0, first=True)
                with pe.Fori(1, NG // 2) as g2:
                    groups(g2)
                lookup(COLS - 1, 1)


def build_adjacency(k):
    nc = k.nc
    NBANK = 4
    with ExitStack() as ctx:
        def sb(name, shape, dt):
            return ctx.enter_context(nc.sbuf_tensor(name, shape, dt))

        slot = sb("slot", [P, 2, UB, PW], F32)
        S = sb("S", [P, 2, UB, SRC_W], BF16)
        Dh = sb("Dh", [P, 2, UB, DST_W], BF16)
        eas = sb("eas", [P, 2, UB, 3 * DE], BF16)
        rest = sb("rest", [P, UB, DE], F32)
        sums = sb("sums", [P, STRIP], F32)
        ads = sb("ads", [DST_H, 2, 2 * UD, STRIP], F16)
        asd = sb("asd", [P, 2, US, STRIP], F16)
        easum = sb("easum", [3 * DE, NP], F32)
        bank = [ctx.enter_context(nc.psum_tensor(f"bank{i}", [P, 512], F32)) for i in range(NBANK)]
        accs = [ctx.enter_context(nc.psum_tensor(f"pooled_acc{i}", [P, 512], F32)) for i in range(2)]
        eab = [ctx.enter_context(nc.psum_tensor(f"eab{i}", [P, 512], F32)) for i in range(2)]

        slot_in = [k.sem("slot_in0"), k.sem("slot_in1")]
        hots, split, ea_chain = k.sem("hots"), k.sem("split"), k.sem("ea_chain")
        filled, act_out = k.sem("filled"), k.sem("act_out")
        ads_used, sums_full = k.sem("ads_used"), k.sem("sums_full")
        sums_read, sums_out = k.sem("sums_read"), k.sem("sums_out")
        ea_filled, ea_added, zeroed = k.sem("ea_filled"), k.sem("ea_added"), k.sem("zeroed")
        unit_out = [k.sem("unit_out0"), k.sem("unit_out1")]
        ea_out, turn, turn_sp, turn_act = k.sem("ea_out"), k.sem("turn"), k.sem("turn_sp"), k.sem("turn_act")

        items = []
        for jj in range(UD):
            for h in range(2):
                for lo, hi in ((0, 4), (4, US)):
                    items.append(("ds", 2 * jj + h, lo, hi))
        for ii in range(US):
            for lo, hi in ((0, 2), (2, 4)):
                items.append(("sd", ii, lo, hi))
        NI = len(items)
        DS_ITEMS = 4 * UD

        def target(item, b):
            kind, r, lo, hi = item
            if kind == "ds":
                return ads[:, b, r, lo * SRC_W:hi * SRC_W]
            return asd[:, b, r, lo * DST_W:hi * DST_W]

        def bank_of(v, i):
            return bank[(v * NI + i) % NBANK]

        def source(v, i):
            kind, r, lo, hi = items[i]
            if kind == "ds":
                return bank_of(v, i)[0:DST_H, 0:(hi - lo) * SRC_W]
            return bank_of(v, i)[:, 0:(hi - lo) * DST_W]

        def unit(q, v):
            return q * (2 * NU) + v, v, v % 2, q * NU + v // 2, q * 2 + v // NU

        def units(eng, body):
            for v in range(NU):
                body(0, v)
            with eng.Fori(0, NU // 2) as q:
                for v in range(NU, 3 * NU):
                    body(q, v)

        NUNIT = NU * NU
        assert NU % 2 == 1

        with nc.Block() as block:
            @block.sync
            def _(sp):
                def store_sums(s):
                    sp.wait_ge(sums_read.h, sums_read.at(2 * s + 2))
                    sp.sem_inc(turn_sp.h, 1)
                    sp.dma_start(k.pooled[:, cols(s, STRIP)], sums[:, :]).then_inc(sums_out.h, 16)

                def body(q, v):
                    u, v, b, n, s = unit(q, v)
                    sp.wait_ge(act_out.h, act_out.at(u * NI + DS_ITEMS))
                    sp.sem_inc(turn_sp.h, 1)
                    sp.dma_start(k.counts_ds[bass.ds(u, 1)].rearrange("u p r c -> (u p) (r c)"),
                                 ads[:, b, :, :].rearrange("p r c -> p (r c)")).then_inc(unit_out[b].h, 16)
                    sp.wait_ge(act_out.h, act_out.at((u + 1) * NI))
                    sp.sem_inc(turn_sp.h, 1)
                    sp.dma_start(k.counts_sd[bass.ds(u, 1)].rearrange("u p r c -> (u p) (r c)"),
                                 asd[:, b, :, :].rearrange("p r c -> p (r c)")).then_inc(unit_out[b].h, 16)
                    if v >= NU and v % NU == 0:
                        store_sums(s - 1)

                units(sp, body)
                store_sums(NU - 1)
                sp.wait_ge(ea_added.h, ea_added.at(2 * NUNIT))
                sp.dma_start(k.ea_sums, easum[:, :]).then_inc(ea_out.h, 16)
                sp.wait_ge(ea_out.h, ea_out.at(16))
                sp.wait_ge(sums_out.h, sums_out.at(16 * NU))
                sp.wait_ge(unit_out[0].h, unit_out[0].at(32 * (NUNIT // 2 + 1)))
                sp.wait_ge(unit_out[1].h, unit_out[1].at(32 * (NUNIT // 2)))

            @block.gpsimd
            def _(pool):
                g = nc.gpsimd
                g.memset(easum[:, :], 0.0).then_inc(zeroed.h, 1)

                def body(q, v):
                    u, v, b, n, s = unit(q, v)
                    pool.wait_ge(slot_in[b].h, slot_in[b].at(n * 16 + 16))
                    pool.sem_inc(turn.h, 1)
                    if ea_filled.due(2 * u - 2):
                        pool.wait_ge(ea_filled.h, ea_filled.at(2 * u - 2))
                    pool.sem_inc(turn.h, 1)
                    f = slot[:, b, :, 2:PW]
                    r = rest[:, :, :]
                    hi, mid, lo = (eas[:, b, :, i * DE:(i + 1) * DE] for i in range(3))
                    g.tensor_copy(hi, f).then_inc(ea_chain.h, 1)
                    pool.wait_ge(ea_chain.h, ea_chain.at(u * 3 + 1))
                    pool.sem_inc(turn.h, 1)
                    if split.due(u):
                        pool.wait_ge(split.h, split.at(u))
                        pool.sem_inc(turn.h, 1)
                    g.tensor_tensor(r, f, hi, ALU.subtract).then_inc(ea_chain.h, 1)
                    pool.wait_ge(ea_chain.h, ea_chain.at(u * 3 + 2))
                    pool.sem_inc(turn.h, 1)
                    g.tensor_copy(mid, r).then_inc(ea_chain.h, 1)
                    pool.wait_ge(ea_chain.h, ea_chain.at(u * 3 + 3))
                    pool.sem_inc(turn.h, 1)
                    g.tensor_tensor(lo, r, mid, ALU.subtract).then_inc(split.h, 1)

                units(pool, body)

            @block.vector
            def _(dve):
                V = nc.vector

                def one_hots(u, b, n):
                    dve.wait_ge(slot_in[b].h, slot_in[b].at(n * 16 + 16))
                    if ea_filled.due(2 * u - 2):
                        dve.wait_ge(ea_filled.h, ea_filled.at(2 * u - 2))
                    for i in range(UB):
                        V.tensor_scalar(S[:, b, i, :], k.iota[:, 0:SRC_W], slot[:, b, i, 0:1], None, ALU.is_equal)
                        last = V.tensor_scalar(Dh[:, b, i, :], k.iota[:, 0:DST_W], slot[:, b, i, 1:2], None,
                                               ALU.is_equal)
                    last.then_inc(hots.h, 1)

                def add_ea(u):
                    t = u % NU
                    for h in range(2):
                        dve.wait_ge(ea_filled.h, ea_filled.at(u * 2 + h + 1))
                        at = bass.ds(t * STRIP + h * HALF, HALF)
                        V.tensor_tensor(easum[:, at], easum[:, at], eab[h][0:3 * DE, 0:HALF], ALU.add
                                        ).then_inc(ea_added.h, 1)

                def body(q, v):
                    u, v, b, n, s = unit(q, v)
                    one_hots(u, b, n)
                    if v > 0:
                        add_ea(u - 1)

                dve.wait_ge(zeroed.h, zeroed.at(1))
                units(dve, body)
                add_ea(NUNIT - 1)

            @block.scalar
            def _(act):
                A = nc.scalar

                def load(u, b):
                    act.dma_start(slot[:, b, :, :].rearrange("p a b -> p (a b)"), rows[:, cols(u, UB * PW)]
                                  ).then_inc(slot_in[b].h, 16)

                def read_sums(s):
                    if sums_out.due(16 * s):
                        act.wait_ge(sums_out.h, sums_out.at(16 * s))
                    for h in range(2):
                        if h == 0:
                            act.wait_ge(sums_full.h, sums_full.at(s + 1))
                        else:
                            act.wait_ge(ads_used.h, ads_used.at(s * NU + NU))
                        A.activation(sums[:, h * HALF:(h + 1) * HALF], accs[h][:, 0:HALF], ACT.Copy,
                                     scale=k.span[:, 3:4]).then_inc(sums_read.h, 1)

                def body(q, v):
                    u, v, b, n, s = unit(q, v)
                    if unit_out[b].due(n * 32):
                        act.wait_ge(unit_out[b].h, unit_out[b].at(n * 32))
                    if ads_used.due(u - 1):
                        act.wait_ge(ads_used.h, ads_used.at(u - 1))
                    for i in range(NI):
                        act.wait_ge(filled.h, filled.at(u * NI + i + 1))
                        A.activation(target(items[i], b), source(v, i), ACT.Copy).then_inc(act_out.h, 1)
                        if i == 4:
                            act.wait_ge(hots.h, hots.at(u + 1))
                            act.wait_ge(ea_chain.h, ea_chain.at(3 * u + 2))
                            act.sem_inc(turn_act.h, 1)
                            load((u + 2) % NUNIT, b)
                    if v >= NU and v % NU == 0:
                        read_sums(s - 1)

                rows = k.slots.rearrange("(p r) w -> p (r w)", p=P)
                load(0, 0)
                load(1, 1)
                units(act, body)
                read_sums(NU - 1)
                for b in range(2):
                    act.wait_ge(slot_in[b].h, slot_in[b].at(16 * (NUNIT // 2 + 1 + (1 - b))))

            @block.tensor
            def _(pe):
                T = nc.tensor

                def pooling(v, t, b):
                    for r in range(2 * UD):
                        for part in range(2):
                            for h in range(2):
                                first = t == 0 and r == 0 and part == 0
                                final = r == 2 * UD - 1 and part == 1
                                yield h, first, final, lambda h=h, r=r, part=part, first=first, final=final: T.matmul(
                                    accs[h][:, 0:HALF], k.hs[0:DST_H, t * 2 * UD + r, part, :],
                                    ads[:, b, r, h * HALF:(h + 1) * HALF], start=first,
                                    stop=final and t == NU - 1, skip_group_check=True)

                def pool_some(u, s, steps, t, n):
                    for h, first, final, mm in steps[:n]:
                        if first and sums_read.due(2 * s - 1 + h):
                            pe.wait_ge(sums_read.h, sums_read.at(2 * s - 1 + h))
                        ins = mm()
                        if final and h == 1:
                            ins.then_inc(ads_used.h, 1)
                        elif final and t == NU - 1:
                            ins.then_inc(sums_full.h, 1)
                    del steps[:n]

                def body(q, v):
                    u, v, b, n, s = unit(q, v)
                    steps = []
                    if v > 0:
                        pu, _, pb, _, ps_ = unit(q, v - 1)
                        pt = (v - 1) % NU
                        steps = list(pooling(v - 1, pt, pb))
                    total = len(steps)
                    pe.wait_ge(hots.h, hots.at(u + 1))
                    for i, (kind, r, lo, hi) in enumerate(items):
                        if act_out.due(u * NI + i - NBANK + 1):
                            pe.wait_ge(act_out.h, act_out.at(u * NI + i - NBANK + 1))
                        for a in range(lo, hi):
                            if kind == "ds":
                                jj, h = r // 2, r % 2
                                kk = a * UD + jj
                                mm = T.matmul(bank_of(v, i)[0:DST_H, (a - lo) * SRC_W:(a - lo + 1) * SRC_W],
                                              Dh[:, b, kk, h * DST_H:(h + 1) * DST_H], S[:, b, kk, :],
                                              start=True, stop=True)
                            else:
                                kk = r * UD + a
                                mm = T.matmul(bank_of(v, i)[:, (a - lo) * DST_W:(a - lo + 1) * DST_W],
                                              S[:, b, kk, :], Dh[:, b, kk, :], start=True, stop=True)
                        mm.then_inc(filled.h, 1)
                        if total and i >= 3:
                            if i == 3:
                                pe.wait_ge(act_out.h, act_out.at(u * NI - NI + DS_ITEMS))
                            due = min(total, -(-(i - 2) * total // (NI - 6)))
                            pool_some(pu, ps_, steps, pt, due - (total - len(steps)))
                    pe.wait_ge(split.h, split.at(u + 1))
                    for h in range(2):
                        if ea_added.due(u * 2 + h - 1):
                            pe.wait_ge(ea_added.h, ea_added.at(u * 2 + h - 1))
                        for jj in range(2 * h, 2 * h + 2):
                            for ii in range(US):
                                kk = ii * UD + jj
                                mm = T.matmul(eab[h][0:3 * DE, (jj % 2) * DST_W:(jj % 2 + 1) * DST_W],
                                              eas[:, b, kk, :], Dh[:, b, kk, :],
                                              start=(ii == 0), stop=(ii == US - 1))
                        mm.then_inc(ea_filled.h, 1)

                units(pe, body)
                pe.wait_ge(act_out.h, act_out.at(NUNIT * NI - NI + DS_ITEMS))
                steps = list(pooling(NU - 1, NU - 1, 0))
                pool_some(NUNIT - 1, NU - 1, steps, NU - 1, len(steps))


def start_loads(k, w, x):
    nc = k.nc
    straight = [("a0", w["L0_gnn_l0_W0"]), ("a1", w["L0_gnn_l0_W1"]), ("b0", w["L0_gnn_l1_W0"]),
                ("b1", w["L0_gnn_l1_W1"]), ("g0", w["L3_gnn_W1"]), ("g1", w["L3_gnn_W2"])]
    straight += [(f"self{i}", w["L1_gnn_W_self"][i]) for i in range(4)]
    straight += [(f"neigh{i}", w["L1_gnn_W_neigh"][i]) for i in range(4)]
    turned = [("msg", w["L2_gnn_W_message"][:, 0:D]), ("node", w["L2_gnn_W_node"]),
              ("up_h", w["L2_gnn_W1"][:, 0:D]), ("up_m", w["L2_gnn_W1"][:, D:2 * D]), ("down", w["L2_gnn_W2"])]
    vectors = []
    for i in range(2):
        vectors += [w[f"L0_gnn_l{i}_{n}"] for n in ("b0", "mbn_g", "mbn_b", "b1", "bn_g", "bn_b")]
    vectors += [w["L1_gnn_bias"][i] for i in range(4)]
    vectors += [w[f"L2_gnn_{n}"] for n in ("b1", "ln1_g", "ln1_b", "b2", "ln2_g", "ln2_b", "ln_g", "ln_b")]
    vectors += [w["L3_gnn_b1"], w["L3_gnn_b2"]]
    k.turned = [name for name, _ in turned]
    k.nv = len(vectors)
    k.W = {name: k.weights[:, i, :] for i, (name, _) in enumerate(straight + turned)}
    k.W["msg_e"] = k.weights[0:3 * DE, len(straight) + len(turned), :]
    k.vec = lambda i: k.vectors[:, i:i + 1]
    w_in, v_in, x_in, x_pad = k.sem("w_in"), k.sem("v_in"), k.sem("x_in"), k.sem("x_pad")
    full = NS - 1
    rowsn = k.B[:, :].rearrange("p (b f) -> p b f", f=D)
    with nc.Block() as block:
        @block.vector
        def _(dve):
            nc.vector.memset(k.B[:, full * D:NP], 0.0).then_inc(x_pad.h, 1)

        @block.sync
        def _(sp):
            sp.dma_start(rowsn[:, 0:full, :], x[0:full * P, :].rearrange("(b p) f -> p b f", p=P)).then_inc(x_in.h, 16)
            sp.wait_ge(x_pad.h, x_pad.at(1))
            sp.dma_start(rowsn[0:N - full * P, full, :], x[full * P:N, :]).then_inc(x_in.h, 16)
            for i, (_, a) in enumerate(turned):
                sp.dma_start(k.raw[:, i, :], a).then_inc(w_in.h, 16)
            for i in range(3):
                sp.dma_start(k.raw_e[:, i * DE:(i + 1) * DE], w["L2_gnn_W_message"][:, D:D + DE]
                             ).then_inc(w_in.h, 16)
            for name, a in straight:
                sp.dma_start(k.W[name], a).then_inc(w_in.h, 16)

        @block.scalar
        def _(act):
            for i, a in enumerate(vectors):
                act.dma_start(k.rows[i:i + 1, :], a.rearrange("(a f) -> a f", a=1)).then_inc(v_in.h, 16)
    k.w_in = 16 * (len(turned) + 3 + len(straight))


def finish_loads(k):
    nc = k.nc
    w_in, v_in, w_T, w_out = k.sem("w_in"), k.sem("v_in"), k.sem("w_T"), k.sem("w_out")
    x_in, x_T, x_copied = k.sem("x_in"), k.sem("x_T"), k.sem("x_copied")
    rowsn = k.B[:, :].rearrange("p (b f) -> p b f", f=D)
    NGRP = -(-NS // 4)
    nv, nt = k.nv, len(k.turned)
    jobs = [(k.bank[i % 4][:, 0:D], k.raw[:, i, :], k.idf[:, :], k.W[name]) for i, name in enumerate(k.turned)]
    jobs.append((k.bank[nt % 4][0:3 * DE, 0:D], k.raw_e[:, :], k.idf[:, :], k.W["msg_e"]))
    jobs.append((k.bank[(nt + 1) % 4][:, 0:nv], k.rows[:, :], k.idf[0:nv, 0:nv], k.vectors[:, 0:nv]))
    with nc.Block() as block:
        @block.tensor
        def _(pe):
            pe.wait_ge(x_in.h, x_in.at(32))
            for g in range(NGRP):
                if g >= 4:
                    pe.wait_ge(x_copied.h, x_copied.at(g - 3))
                for i in range(4 * g, min(4 * g + 4, NS)):
                    mm = nc.tensor.transpose(k.bank[4 + g % 4][:, (i % 4) * P:(i % 4 + 1) * P], rowsn[:, i, :],
                                             k.idf[:, :])
                mm.then_inc(x_T.h, 1)
            pe.wait_ge(w_in.h, w_in.at(k.w_in))
            pe.wait_ge(v_in.h, v_in.at(16 * nv))
            for i, (turned, raw, identity, _) in enumerate(jobs):
                if i >= 4:
                    pe.wait_ge(w_out.h, w_out.at(i - 3))
                nc.tensor.transpose(turned, raw, identity).then_inc(w_T.h, 1)

        @block.vector
        def _(dve):
            for g in range(NGRP):
                dve.wait_ge(x_T.h, x_T.at(g + 1))
                n = min(4, NS - 4 * g) * P
                nc.vector.tensor_copy(k.A[:, g * 512:g * 512 + n], k.bank[4 + g % 4][:, 0:n]).then_inc(x_copied.h, 1)

        @block.scalar
        def _(act):
            for i, (turned, _, _, to) in enumerate(jobs):
                act.wait_ge(w_T.h, w_T.at(i + 1))
                nc.scalar.activation(to, turned, ACT.Copy).then_inc(w_out.h, 1)


def residual(k, y):
    nc = k.nc
    with nc.Block() as block:
        @block.vector
        def _(dve):
            with dve.Fori(0, NU) as s:
                at = cols(s, STRIP)
                nc.vector.tensor_tensor(k.A[:, at], k.A[:, at], y[:, at], ALU.add)


def store_out(k, out):
    nc = k.nc
    o_T, o_copied, o_out = k.sem("o_T"), k.sem("o_copied"), k.sem("o_out")
    full = NS - 1
    rowsn = k.B[:, :].rearrange("p (b f) -> p b f", f=D)
    NGRP = -(-NS // 4)
    with nc.Block() as block:
        @block.tensor
        def _(pe):
            for g in range(NGRP):
                if o_copied.due(g - 3):
                    pe.wait_ge(o_copied.h, o_copied.at(g - 3))
                for i in range(4 * g, min(4 * g + 4, NS)):
                    mm = nc.tensor.transpose(k.bank[g % 4][:, (i % 4) * P:(i % 4 + 1) * P],
                                             k.A[:, i * P:(i + 1) * P], k.idf[:, :])
                mm.then_inc(o_T.h, 1)

        @block.scalar
        def _(act):
            for g in range(NGRP):
                act.wait_ge(o_T.h, o_T.at(g + 1))
                n = min(4, NS - 4 * g) * P
                nc.scalar.activation(k.B[:, g * 512:g * 512 + n], k.bank[g % 4][:, 0:n], ACT.Copy
                                     ).then_inc(o_copied.h, 1)

        @block.sync
        def _(sp):
            for g in range(NGRP - 1):
                sp.wait_ge(o_copied.h, o_copied.at(g + 1))
                sp.dma_start(out[g * 512:(g + 1) * 512, :].rearrange("(b p) f -> p b f", p=P),
                             rowsn[:, 4 * g:4 * g + 4, :]).then_inc(o_out.h, 16)
            sp.wait_ge(o_copied.h, o_copied.at(NGRP))
            sp.dma_start(out[full * P:N, :], rowsn[0:N - full * P, full, :]).then_inc(o_out.h, 16)
            sp.wait_ge(o_out.h, o_out.at(16 * NGRP))


def layer_norm(k, src, dst, squares, gain=None, shift=None, add=False):
    nc = k.nc
    mean, centred, squared = k.sem("ln_mean"), k.sem("ln_centred"), k.sem("ln_squared")
    var, rooted, inverse = k.sem("ln_var"), k.sem("ln_rooted"), k.sem("ln_inverse")
    spread, final, added, turn = k.sem("ln_spread"), k.sem("ln_final"), k.sem("ln_added"), k.sem("ln_turn")
    with nc.Block() as block:
        @block.tensor
        def _(pe):
            def means(c, b):
                pe.wait_ge(centred.h, centred.at(c + 1))
                if add:
                    pe.wait_ge(added.h, added.at(c + 1))
                    pe.sem_inc(turn.h, 1)
                nc.tensor.matmul(k.bank[b][:, 0:CH], k.avg[:, :], src[:, cols(c)], start=True, stop=True
                                 ).then_inc(mean.h, 1)

            chunk_pairs(pe, means)
            for c in range(NCH):
                pe.wait_ge(squared.h, squared.at(c + 1))
                nc.tensor.matmul(k.bank[2][0:NCH, 0:CH], k.gather[:, c, :], squares[:, c * CH:(c + 1) * CH],
                                 start=(c == 0), stop=(c == NCH - 1)).then_inc(var.h, 1)
            pe.wait_ge(inverse.h, inverse.at(1))
            for c in range(NCH):
                if c >= 2:
                    pe.wait_ge(final.h, final.at(c - 1))
                nc.tensor.matmul(k.bank[3 + c % 2][:, 0:CH], k.spread[:, c, :], k.rstd[:, :], start=True, stop=True
                                 ).then_inc(spread.h, 1)

        @block.vector
        def _(dve):
            V = nc.vector
            dve.sem_inc(centred.h, 2)

            def centre(c, b):
                dve.wait_ge(mean.h, mean.at(c + 1))
                V.tensor_tensor(dst[:, cols(c)], src[:, cols(c)], k.bank[b][:, 0:CH], ALU.subtract
                                ).then_inc(centred.h, 1)

            def scale(c, b):
                dve.wait_ge(spread.h, spread.at(c + 1))
                at = cols(c)
                if gain is None:
                    V.scalar_tensor_tensor(dst[:, at], dst[:, at], 0.0, k.bank[3 + b][:, 0:CH], ALU.max, ALU.mult
                                           ).then_inc(final.h, 1)
                else:
                    V.scalar_tensor_tensor(dst[:, at], dst[:, at], gain, k.bank[3 + b][:, 0:CH], ALU.mult, ALU.mult
                                           ).then_inc(final.h, 1)

            def residual(c, b):
                V.tensor_tensor(src[:, cols(c)], src[:, cols(c)], dst[:, cols(c)], ALU.add).then_inc(added.h, 1)

            if add:
                chunk_pairs(dve, residual)
                dve.wait_ge(added.h, added.at(NCH))
            chunk_pairs(dve, centre)
            dve.wait_ge(rooted.h, rooted.at(1))
            V.reciprocal(k.rstd[:, :], k.rstd[:, :]).then_inc(inverse.h, 1)
            chunk_pairs(dve, scale)

        @block.scalar
        def _(act):
            A = nc.scalar

            def square(c, b):
                act.wait_ge(centred.h, centred.at(2 + c + 1))
                A.activation(squares[:, cols(c)], dst[:, cols(c)], ACT.Square).then_inc(squared.h, 1)

            def shift_in(c, b):
                act.wait_ge(final.h, final.at(c + 1))
                A.activation(dst[:, cols(c)], dst[:, cols(c)], ACT.Identity, bias=shift)

            chunk_pairs(act, square)
            act.wait_ge(var.h, var.at(NCH))
            A.activation(k.rstd[:, :], k.bank[2][0:NCH, 0:CH], ACT.Sqrt, bias=k.eps[0:NCH, 0:1]
                         ).then_inc(rooted.h, 1)
            if shift is not None:
                chunk_pairs(act, shift_in)
    k.advance(ln_mean=NCH, ln_centred=NCH + 2, ln_squared=NCH, ln_var=NCH, ln_rooted=1, ln_inverse=1,
              ln_spread=NCH, ln_final=NCH, ln_added=NCH if add else 0)


def product(k, terms, dst, func, bias):
    nc = k.nc
    summed, moved = k.sem("summed"), k.sem("moved")
    with nc.Block() as block:
        @block.tensor
        def _(pe):
            def body(c, b):
                pe.wait_ge(moved.h, moved.at(c + 1))
                for i, (w, v) in enumerate(terms):
                    mm = nc.tensor.matmul(k.bank[b][:, 0:CH], w, v[:, cols(c)], start=(i == 0),
                                          stop=(i == len(terms) - 1))
                mm.then_inc(summed.h, 1)

            chunk_pairs(pe, body)

        @block.scalar
        def _(act):
            act.sem_inc(moved.h, 2)

            def body(c, b):
                act.wait_ge(summed.h, summed.at(c + 1))
                nc.scalar.activation(dst[:, cols(c)], k.bank[b][:, 0:CH], func, bias=bias).then_inc(moved.h, 1)

            chunk_pairs(act, body)
    k.advance(summed=NCH, moved=NCH + 2)


def batch_norm_relu(k, v, gain, shift):
    nc = k.nc
    stat, bn_root, bn_scaled = k.sem("bn_stat"), k.sem("bn_root"), k.sem("bn_scaled")
    st, mv = k.bn_stats, k.bn_mv
    with nc.Block() as block:
        @block.vector
        def _(dve):
            V = nc.vector
            for c in range(NCH):
                n = CH if c < NCH - 1 else LASTCH
                V.bn_stats(st[:, c, :], v[:, c * CH:c * CH + n]).then_inc(stat.h, 1)
            dve.wait_ge(stat.h, stat.at(NCH))
            V.bn_aggr(mv[:, 0:2], st[:, :, :].rearrange("p a b -> p (a b)")).then_inc(stat.h, 1)
            dve.wait_ge(bn_root.h, bn_root.at(1))
            V.reciprocal(mv[:, 3:4], mv[:, 2:3]).then_inc(stat.h, 1)
            dve.wait_ge(stat.h, stat.at(NCH + 2))
            V.tensor_tensor(mv[:, 4:5], mv[:, 3:4], gain, ALU.mult).then_inc(stat.h, 1)
            dve.wait_ge(stat.h, stat.at(NCH + 3))
            with dve.Fori(0, NU) as s:
                at = cols(s, STRIP)
                V.tensor_scalar(v[:, at], v[:, at], mv[:, 0:1], mv[:, 4:5], ALU.subtract, ALU.mult
                                ).then_inc(bn_scaled.h, 1)

        @block.scalar
        def _(act):
            act.wait_ge(stat.h, stat.at(NCH + 1))
            nc.scalar.activation(mv[:, 2:3], mv[:, 1:2], ACT.Sqrt, bias=k.eps[:, 0:1]).then_inc(bn_root.h, 1)
            with act.Fori(0, NU) as s:
                act.wait_ge(bn_scaled.h, bn_scaled.at(s + 1))
                at = cols(s, STRIP)
                nc.scalar.activation(v[:, at], v[:, at], ACT.Relu, bias=shift)
    k.advance(bn_stat=NCH + 3, bn_root=1, bn_scaled=NU)


def split_rows(k, v, rows, signed, scaled):
    nc = k.nc
    nb = NP // rows
    top, scaled_ok, turned, hi_ok, lo_ok = k.sem("top"), k.sem("scaled"), k.sem("turned"), k.sem("hi_ok"), k.sem("lo_ok")
    m = k.span
    ng = -(-nb // 4)
    EXP1 = 1 << 23
    from_ = v if scaled is None else scaled
    unit = 2.0 ** LN_SCALE if scaled is None else 1.0
    with nc.Block() as block:
        @block.vector
        def _(dve):
            V = nc.vector
            n = [0]
            k.tops = 0

            def link(ins):
                n[0] += 1
                ins.then_inc(top.h, 1)
                dve.wait_ge(top.h, top.at(n[0]))

            def exponents():
                V.tensor_reduce(m[:, 0:1], v[:, :], AX, ALU.max).then_inc(top.h, 1)
                n[0] += 1
                if signed:
                    link(V.tensor_reduce(m[:, 1:2], v[:, :], AX, ALU.min))
                    link(V.scalar_tensor_tensor(m[:, 0:1], m[:, 1:2], -1.0, m[:, 0:1], ALU.mult, ALU.max))
                else:
                    dve.wait_ge(top.h, top.at(n[0]))
                link(V.tensor_scalar(m[:, 0:1], m[:, 0:1], 2.0 ** -60, None, ALU.max))
                mi = m[:, :].bitcast(I32)
                link(V.tensor_scalar(mi[:, 1:2], mi[:, 0:1], 0x7F800000, None, ALU.bitwise_and))
                V.tensor_scalar(mi[:, 2:3], mi[:, 1:2], -1.0, float((2 * 127 + 14) * EXP1), ALU.mult, ALU.add
                                ).then_inc(top.h, 1)
                V.tensor_scalar(mi[:, 3:4], mi[:, 1:2], float(-14 * EXP1), None, ALU.add).then_inc(top.h, 1)
                n[0] += 2
                k.tops = n[0]

            if scaled is None:
                V.memset(m[:, 3:4], 2.0 ** -LN_SCALE)
            else:
                exponents()
            for g in range(ng):
                w = min(4, nb - 4 * g)
                dve.wait_ge(hi_ok.h, hi_ok.at(g + 1))
                V.scalar_tensor_tensor(k.hs[0:rows, 4 * g:4 * g + w, 1, :],
                                       k.bank[g % 4][0:rows, 0:w * P].rearrange("p (a f) -> p a f", f=P), unit,
                                       k.hs[0:rows, 4 * g:4 * g + w, 0, :], ALU.mult, ALU.subtract
                                       ).then_inc(lo_ok.h, 1)

        tops = k.tops

        @block.scalar
        def _(act):
            if scaled is not None:
                act.wait_ge(top.h, top.at(tops))
                with act.Fori(0, NU) as s:
                    at = cols(s, STRIP)
                    nc.scalar.activation(scaled[:, at], v[:, at], ACT.Copy, scale=m[:, 2:3]).then_inc(scaled_ok.h, 1)
            for g in range(ng):
                w = min(4, nb - 4 * g)
                act.wait_ge(turned.h, turned.at(g + 1))
                nc.scalar.activation(k.hs[0:rows, 4 * g:4 * g + w, 0, :],
                                     k.bank[g % 4][0:rows, 0:w * P].rearrange("p (a f) -> p a f", f=P), ACT.Copy,
                                     scale=unit).then_inc(hi_ok.h, 1)

        @block.tensor
        def _(pe):
            for g in range(ng):
                w = min(4, nb - 4 * g)
                if scaled is not None:
                    pe.wait_ge(scaled_ok.h, scaled_ok.at(min(NU, -(-(4 * g + w) * rows // STRIP))))
                if lo_ok.due(g - 3):
                    pe.wait_ge(lo_ok.h, lo_ok.at(g - 3))
                for i in range(w):
                    j = 4 * g + i
                    mm = nc.tensor.transpose(k.bank[g % 4][0:rows, i * P:(i + 1) * P],
                                             from_[:, j * rows:(j + 1) * rows], k.idf[:, :])
                mm.then_inc(turned.h, 1)
    k.advance(top=tops, scaled=NU if scaled is not None else 0, turned=ng, hi_ok=ng, lo_ok=ng)


def pool_neighbours(k, over_src, dst, factor):
    nc = k.nc
    table = k.counts_sd if over_src else k.counts_ds
    rows, per = (SRC_W, US) if over_src else (DST_H, 2 * UD)
    halves = [(t, lo, hi) for t in range(NU) for lo, hi in ((0, 4), (4, per))]
    NH = len(halves)
    NBUF = 7
    assert NH % NBUF == 0
    a_in = [k.sem(f"table_in{b}") for b in range(NBUF)]
    used, acc_full, acc_read, fac_in = k.sem("table_used"), k.sem("acc_full"), k.sem("acc_read"), k.sem("fac_in")
    turn = k.sem("turn_pool")
    acc = [k.bank[h] for h in range(2)]
    with nc.sbuf_tensor(f"tbuf{k.next()}", [P, NBUF, 4, STRIP], F16) as tbuf, nc.Block() as block:
        @block.sync
        def _(sp):
            with sp.Fori(0, NU) as s:
                for i, (t, lo, hi) in enumerate(halves):
                    sp.wait_ge(used.h, used.at(s * NH + i + 1))
                    sp.sem_inc(turn.h, 1)
                    u = s + t * NU if over_src else s * NU + t
                    sp.dma_start(tbuf[0:rows, i % NBUF, 0:hi - lo, :],
                                 table[bass.ds(u, 1), :, lo:hi, :].rearrange("u p r c -> (u p) r c")
                                 ).then_inc(a_in[i % NBUF].h, 16)

        @block.tensor
        def _(pe):
            pe.sem_inc(used.h, NBUF)
            with pe.Fori(0, NU) as s:
                for i, (t, lo, hi) in enumerate(halves):
                    b = i % NBUF
                    pe.wait_ge(a_in[b].h, a_in[b].at(s * (16 * NH // NBUF) + 16 * (i // NBUF + 1)))
                    for h in range(2):
                        if i == 0:
                            pe.wait_ge(acc_read.h, acc_read.at(s * 2 + h + 1))
                        for r in range(lo, hi):
                            kb = t * per + r
                            for part in range(2):
                                mm = nc.tensor.matmul(
                                    acc[h][:, 0:HALF], k.hs[0:rows, kb, part, :],
                                    tbuf[0:rows, b, r - lo, h * HALF:(h + 1) * HALF],
                                    start=(i == 0 and r == lo and part == 0),
                                    stop=(i == NH - 1 and r == hi - 1 and part == 1))
                        if h == 1:
                            mm.then_inc(used.h, 1)
                        elif i == NH - 1:
                            mm.then_inc(acc_full.h, 1)

        @block.scalar
        def _(act):
            if factor is not None:
                act.dma_start(k.C[:, :], k.factors[factor:factor + 1, :].to_broadcast([P, NP])).then_inc(fac_in.h, 16)

        @block.vector
        def _(dve):
            dve.sem_inc(acc_read.h, 2)
            if factor is not None:
                dve.wait_ge(fac_in.h, fac_in.at(16))
            with dve.Fori(0, NU) as s:
                for h in range(2):
                    if h == 0:
                        dve.wait_ge(acc_full.h, acc_full.at(s + 1))
                    else:
                        dve.wait_ge(used.h, used.at(s * NH + NH + NBUF))
                    at = bass.ds(s * STRIP + h * HALF, HALF)
                    if factor is None:
                        ins = nc.vector.tensor_scalar(dst[:, at], acc[h][:, 0:HALF], k.span[:, 3:4], None, ALU.mult)
                    else:
                        ins = nc.vector.scalar_tensor_tensor(dst[:, at], acc[h][:, 0:HALF], k.span[:, 3:4],
                                                             k.C[:, at], ALU.mult, ALU.mult)
                    ins.then_inc(acc_read.h, 1)
    for b in range(NBUF):
        a_in[b].base += 16 * NU * NH // NBUF
    k.advance(table_used=NU * NH + NBUF, acc_full=NU, acc_read=2 * NU + 2)
    if factor is not None:
        k.advance(fac_in=16)


def overflow(k, table, gather_at, scatter_at, width, values=None, dst=None, factor=False,
             kept=None):
    nc = k.nc
    i = k.next()
    sums = k.spill_sums if width == D else k.spill_sums_e
    nrows = NP if values is not None else E
    NZERO = 16 * NS + (16 if dst is None else 0)
    with ExitStack() as ctx:
        def sb(name, shape, dt):
            return ctx.enter_context(nc.sbuf_tensor(f"{name}{i}", shape, dt))

        gidx = sb("gidx", [P, COLS], I32)
        sidx = sb("sidx", [P, COLS], I32)
        gcol = sb("gcol", [P, 1], I32)
        scol = sb("scol", [P, 1], I32)
        put = sb("put", [P, 1], I32)
        scolf = sb("scolf", [P, 1], F32)
        dup = sb("dup", [P, 2], F32)
        rows = sb("rows_g", [P, width], F32)
        old = sb("old", [P, width], F32)
        new = sb("new", [P, width], F32)
        diag = sb("diag", [P, P], F32)
        same = sb("same", [P, P], F32)
        junk = sb("junk_o", [P, P], F32)
        ones = sb("ones", [P, P], F32)
        turnb = sb("turnb", [P, 4, P], F32)
        bank = k.bank

        o_in, o_zero, o_dve, o_pe = k.sem("o_in"), k.sem("o_zero"), k.sem("o_dve"), k.sem("o_pe")
        o_got, o_put = k.sem(f"o_got{i}"), k.sem(f"o_put{i}")
        o_col, o_rows = k.sem("o_col"), k.sem("o_rows")
        o_kept, o_set, o_back, o_T, o_add = (k.sem(n) for n in ("o_kept", "o_set", "o_back", "o_T2", "o_add"))
        o_load = k.sem("o_load")
        NV = 5
        NKEEP = NS if values is not None else 0

        with nc.Block() as block:
            @block.sync
            def _(sp):
                n = sp.value_load(k.spill_n[0:1, 0:1], min_val=0, max_val=E)
                with sp.If(n > 0):
                    if kept is not None:
                        sp.dma_start(values[:, :], kept).then_inc(o_load.h, 16)
                    if dst is None:
                        sp.dma_start(k.A[0:DE, :], k.ea_sums[0:DE, :]).then_inc(o_zero.h, 16)
                    sp.dma_start(gidx[:, :], gather_at).then_inc(o_in.h, 16)
                    sp.dma_start(sidx[:, :], scatter_at).then_inc(o_in.h, 16)
                    sp.wait_ge(o_set.h, o_set.at(1))
                    for b in range(NS):
                        sp.dma_start(sums[b * P:(b + 1) * P, :], old[:, :]).then_inc(o_zero.h, 16)
                    for b in range(NKEEP):
                        sp.wait_ge(o_rows.h, o_rows.at(b + 1))
                        sp.dma_start(table[b * P:(b + 1) * P, :], turnb[:, b % 4, :]).then_inc(o_kept.h, 16)
                        sp.wait_ge(o_kept.h, o_kept.at(16 * (b + 1)))
                    sp.wait_ge(o_col.h, o_col.at(COLS + 1))
                    for b in range(NS):
                        if o_add.due(b - 1):
                            sp.wait_ge(o_add.h, o_add.at(b - 1))
                        sp.dma_start(turnb[:, b % 2, 0:width], sums[b * P:(b + 1) * P, :]).then_inc(o_back.h, 16)
                        sp.wait_ge(o_back.h, o_back.at(16 * (b + 1)))
                        sp.sem_inc(o_rows.h, 1)
                    sp.wait_ge(o_add.h, o_add.at(NS))
                    if dst is None:
                        sp.dma_start(k.ea_sums[0:DE, :], k.A[0:DE, :]).then_inc(o_back.h, 16)
                        sp.wait_ge(o_back.h, o_back.at(16 * NS + 16))

            @block.gpsimd
            def _(pool):
                n = pool.value_load(k.spill_n[0:1, 0:1], min_val=0, max_val=E)
                with pool.If(n > 0):
                    g = nc.gpsimd
                    gbound = pool.to_reg(nrows - 1)
                    sbound = pool.to_reg(NP - 1)
                    pool.wait_ge(o_zero.h, o_zero.at(NZERO))
                    if o_kept.due(16 * NKEEP):
                        pool.wait_ge(o_kept.h, o_kept.at(16 * NKEEP))
                    pool.sem_inc(o_col.h, 1)
                    with pool.Fori(0, COLS) as c:
                        pool.wait_ge(o_dve.h, o_dve.at(c * NV + 1))
                        pool.sem_inc(k.sem("turn_o").h, 1)
                        g.indirect_dma_start(out=rows[:, :], out_offset=None, in_=table,
                                             in_offset=bass.IndirectOffsetOnAxis(gcol[:, 0:1], 0),
                                             bounds_check=gbound, oob_is_err=False).then_inc(o_got.h, 16)
                        g.indirect_dma_start(out=old[:, :], out_offset=None, in_=sums,
                                             in_offset=bass.IndirectOffsetOnAxis(scol[:, 0:1], 0),
                                             bounds_check=sbound, oob_is_err=False).then_inc(o_got.h, 16)
                        pool.wait_ge(o_dve.h, o_dve.at(c * NV + NV))
                        pool.sem_inc(k.sem("turn_o").h, 1)
                        g.indirect_dma_start(out=sums, in_=new[:, :], in_offset=None,
                                             out_offset=bass.IndirectOffsetOnAxis(put[:, 0:1], 0),
                                             bounds_check=sbound, oob_is_err=False).then_inc(o_put.h, 16)
                        pool.wait_ge(o_put.h, o_put.at(c * 16 + 16))
                        pool.sem_inc(k.sem("turn_o").h, 1)
                        pool.sem_inc(o_col.h, 1)

            @block.vector
            def _(dve):
                n = dve.value_load(k.spill_n[0:1, 0:1], min_val=0, max_val=E)
                with dve.If(n > 0):
                    V = nc.vector
                    chain, step = k.sem("o_chain"), [0]
                    V.memset(rows[:, :], 0.0)
                    V.memset(ones[:, :], 1.0)
                    V.memset(old[:, :], 0.0).then_inc(o_set.h, 1)
                    dve.wait_ge(o_in.h, o_in.at(32))
                    dve.wait_ge(o_zero.h, o_zero.at(NZERO))
                    for b in range(NKEEP):
                        dve.wait_ge(o_T.h, o_T.at(b + 1))
                        if o_kept.due(16 * (b - 3)):
                            dve.wait_ge(o_kept.h, o_kept.at(16 * (b - 3)))
                        V.tensor_copy(turnb[:, b % 4, :], bank[b % 2][:, 0:P]).then_inc(o_rows.h, 1)
                    with dve.Fori(0, COLS) as c:
                        at = bass.ds(c, 1)
                        dve.wait_ge(o_col.h, o_col.at(c + 1))
                        V.tensor_copy(gcol[:, :], gidx[:, at])
                        V.tensor_copy(scolf[:, :], sidx[:, at])
                        V.tensor_copy(scol[:, :], sidx[:, at]).then_inc(o_dve.h, 1)
                        dve.wait_ge(o_dve.h, o_dve.at(c * NV + 1))
                        V.tensor_scalar(diag[:, :], k.idf[:, :], scolf[:, 0:1], None, ALU.mult).then_inc(o_dve.h, 1)
                        dve.wait_ge(o_pe.h, o_pe.at(c * 2 + 1))
                        V.tensor_scalar(same[:, :], bank[2][:, 0:P], scolf[:, 0:1], None, ALU.is_equal
                                        ).then_inc(o_dve.h, 1)
                        dve.wait_ge(o_dve.h, o_dve.at(c * NV + 3))
                        V.scalar_tensor_tensor(junk[:, :], same[:, :], 1.0, k.tri[:, :], ALU.mult, ALU.mult,
                                               accum_out=dup[:, 0:1]).then_inc(chain.h, 1)
                        dve.wait_ge(chain.h, chain.at(c * 2 + 1))
                        V.tensor_scalar(dup[:, 1:2], dup[:, 0:1], 0.5, BIG, ALU.is_gt, ALU.mult).then_inc(chain.h, 1)
                        dve.wait_ge(chain.h, chain.at(c * 2 + 2))
                        V.tensor_tensor(put[:, :], dup[:, 1:2], scolf[:, :], ALU.add).then_inc(o_dve.h, 1)
                        dve.wait_ge(o_pe.h, o_pe.at(c * 2 + 2))
                        V.tensor_tensor(new[:, :], bank[3][:, 0:width], old[:, :], ALU.add).then_inc(o_dve.h, 1)
                    for b in range(NS):
                        dve.wait_ge(o_T.h, o_T.at(NKEEP + b + 1))
                        at = slice(b * P, (b + 1) * P)
                        t = bank[b % 2][0:width, 0:P]
                        if dst is None:
                            V.tensor_tensor(k.A[0:width, at], k.A[0:width, at], t, ALU.add).then_inc(o_add.h, 1)
                            continue
                        if factor:
                            V.tensor_tensor(junk[:, :], t, k.C[:, at], ALU.mult).then_inc(chain.h, 1)
                        else:
                            V.tensor_copy(junk[:, :], t).then_inc(chain.h, 1)
                        dve.wait_ge(chain.h, chain.at(2 * COLS + b + 1))
                        V.tensor_tensor(dst[:, at], dst[:, at], junk[:, :], ALU.add).then_inc(o_add.h, 1)
                        dve.wait_ge(o_add.h, o_add.at(b + 1))

            @block.tensor
            def _(pe):
                n = pe.value_load(k.spill_n[0:1, 0:1], min_val=0, max_val=E)
                with pe.If(n > 0):
                    T = nc.tensor
                    if kept is not None:
                        pe.wait_ge(o_load.h, o_load.at(16))
                    for b in range(NKEEP):
                        if b >= 2:
                            pe.wait_ge(o_rows.h, o_rows.at(b - 1))
                        T.transpose(bank[b % 2][:, 0:P], values[:, b * P:(b + 1) * P], k.idf[:, :]).then_inc(o_T.h, 1)
                    with pe.Fori(0, COLS) as c:
                        pe.wait_ge(o_dve.h, o_dve.at(c * NV + 2))
                        T.matmul(bank[2][:, 0:P], ones[:, :], diag[:, :], start=True, stop=True).then_inc(o_pe.h, 1)
                        pe.wait_ge(o_dve.h, o_dve.at(c * NV + 3))
                        pe.wait_ge(o_got.h, o_got.at(c * 32 + 32))
                        T.matmul(bank[3][:, 0:width], same[:, :], rows[:, :], start=True, stop=True
                                 ).then_inc(o_pe.h, 1)
                    for b in range(NS):
                        pe.wait_ge(o_rows.h, o_rows.at(NKEEP + b + 1))
                        if o_add.due(b - 1):
                            pe.wait_ge(o_add.h, o_add.at(b - 1))
                        T.transpose(bank[b % 2][0:width, 0:P], turnb[:, b % 2, 0:width], k.idf[:, :]
                                    ).then_inc(o_T.h, 1)
    k.sem("turn_o")
    k.advance(o_in=32, o_zero=NZERO, o_dve=NV * COLS, o_pe=2 * COLS,
              o_col=COLS + 1, o_rows=NKEEP + NS, o_kept=16 * NKEEP, o_set=1,
              o_back=16 * NS + (16 if dst is None else 0), o_T2=NKEEP + NS, o_add=NS, o_chain=2 * COLS +
              (0 if dst is None else NS))


def elu_stage(k, pooled, own, factor, bias, dst):
    nc = k.nc
    step, exped = k.sem("elu_step"), k.sem("elu_exp")
    with nc.Block() as block:
        @block.vector
        def _(dve):
            V = nc.vector
            passes = [
                lambda at: V.tensor_tensor(pooled[:, at], pooled[:, at], own[:, at], ALU.add),
                lambda at: V.tensor_tensor(pooled[:, at], pooled[:, at], factor[:, at], ALU.mult),
                lambda at: V.tensor_scalar(pooled[:, at], pooled[:, at], bias, None, ALU.add),
                lambda at: V.tensor_scalar(dst[:, at], pooled[:, at], 0.0, None, ALU.min),
                lambda at: V.scalar_tensor_tensor(dst[:, at], pooled[:, at], 0.0, dst[:, at], ALU.max, ALU.add),
                lambda at: V.tensor_scalar(dst[:, at], dst[:, at], -1.0, None, ALU.add),
            ]
            for i, f in enumerate(passes):
                with dve.Fori(0, NU) as s:
                    if i == 4:
                        dve.wait_ge(exped.h, exped.at(s + 1))
                    elif i:
                        dve.wait_ge(step.h, step.at((i - 1) * NU + s + 1))
                    f(cols(s, STRIP)).then_inc(step.h, 1)

        @block.scalar
        def _(act):
            with act.Fori(0, NU) as s:
                act.wait_ge(step.h, step.at(3 * NU + s + 1))
                at = cols(s, STRIP)
                nc.scalar.activation(dst[:, at], dst[:, at], ACT.Exp).then_inc(exped.h, 1)
    k.advance(elu_step=6 * NU, elu_exp=NU)


def times(k, v, factor_row):
    nc = k.nc
    f_in, multiplied = k.sem("times_in"), k.sem("multiplied")
    with nc.Block() as block:
        @block.sync
        def _(sp):
            sp.dma_start(k.C[:, :], k.factors[factor_row:factor_row + 1, :].to_broadcast([P, NP])).then_inc(f_in.h, 16)

        @block.vector
        def _(dve):
            dve.wait_ge(f_in.h, f_in.at(16))
            with dve.Fori(0, NU) as s:
                at = cols(s, STRIP)
                nc.vector.tensor_tensor(v[:, at], v[:, at], k.C[:, at], ALU.mult).then_inc(multiplied.h, 1)
    k.advance(times_in=16, multiplied=NU)


def load_ea(k, into, wait=False):
    nc = k.nc
    got = k.sem("easum_in")
    with nc.Block() as block:
        @block.sync
        def _(sp):
            if wait:
                sp.wait_ge(got.h, got.at(16))
            else:
                sp.dma_start(into[0:3 * DE, :], k.ea_sums).then_inc(got.h, 16)


def store_start(k, kept, v):
    with k.nc.Block() as block:
        @block.sync
        def _(sp):
            sp.dma_start(kept, v[:, :]).then_inc(k.sem("kept").h, 16)
    k.advance(kept=16)


def wait_kept(k):
    kept = k.sem("kept")
    with k.nc.Block() as block:
        @block.sync
        def _(sp):
            sp.wait_ge(kept.h, kept.at(0))


def load_back(k):
    nc = k.nc
    back, b_in, c_in = k.sem("back"), k.sem("b_in"), k.sem("c_in")
    with nc.Block() as block:
        @block.sync
        def _(sp):
            sp.dma_start(k.B[:, :], k.pooled).then_inc(b_in.h, 16)
            sp.dma_start(k.A[:, :], k.x_kept).then_inc(back.h, 16)
            sp.wait_ge(back.h, back.at(16))

        @block.scalar
        def _(act):
            act.dma_start(k.C[:, :], k.factors[0:1, :].to_broadcast([P, NP])).then_inc(c_in.h, 16)

        @block.vector
        def _(dve):
            dve.wait_ge(b_in.h, b_in.at(16))
            dve.wait_ge(c_in.h, c_in.at(16))
            with dve.Fori(0, NU) as s:
                at = cols(s, STRIP)
                nc.vector.tensor_tensor(k.B[:, at], k.B[:, at], k.C[:, at], ALU.mult)


def program(nc, w, out):
    with ExitStack() as ctx:
        k = Core(nc, ctx)

        def sb(name, shape, dt):
            return ctx.enter_context(nc.sbuf_tensor(name, shape, dt))

        k.iota = sb("iota", [P, 256], BF16)
        k.id16 = sb("id16", [P, P], F16)
        k.idb = sb("idb", [P, P], BF16)
        k.idf = sb("idf", [P, P], F32)
        k.tri = sb("tri", [P, P], F32)
        k.avg = sb("avg", [P, P], F32)
        k.eps = sb("eps", [P, 1], F32)
        k.gather = sb("gather", [P, NCH, NCH], F32)
        k.spread = sb("spread", [NCH, NCH, D], F32)
        k.zero = sb("zero", [P, 1], F32)
        k.slots = nc.dram_tensor("slots", [NBKT * CAP, PW], F32).ap()
        k.factors = nc.dram_tensor("factors", [3, NP], F32).ap()
        k.counts_ds = nc.dram_tensor("counts_ds", [NU * NU, DST_H, 2 * UD, STRIP], F16).ap()
        k.counts_sd = nc.dram_tensor("counts_sd", [NU * NU, P, US, STRIP], F16).ap()
        k.ea_sums = nc.dram_tensor("ea_sums", [3 * DE, NP], F32).ap()
        k.spill_src = nc.dram_tensor("spill_src", [P, COLS], I32).ap()
        k.spill_dst = nc.dram_tensor("spill_dst", [P, COLS], I32).ap()
        k.spill_edge = nc.dram_tensor("spill_edge", [P, COLS], I32).ap()
        k.spill_n = nc.dram_tensor("spill_n", [1, 1], I32).ap()
        k.spill_rows = nc.dram_tensor("spill_rows", [NP, D], F32).ap()
        k.spill_sums = nc.dram_tensor("spill_sums", [NP, D], F32).ap()
        k.spill_sums_e = nc.dram_tensor("spill_sums_e", [NP, DE], F32).ap()
        k.x_kept = nc.dram_tensor("x_kept", [P, NP], F32).ap()
        k.h_kept = nc.dram_tensor("h_kept", [P, NP], F32).ap()
        k.pooled = nc.dram_tensor("pooled", [P, NP], F32).ap()
        constants(k)
        rank_edges(k, w["src"], w["dst"], w["edge_attr_32"])

        k.weights = sb("weights", [P, 20, D], F32)
        k.vectors = sb("vectors", [P, 32], F32)
        k.hs = sb("hs", [P, NP // DST_H, 2, P], F16)
        k.bn_stats = sb("bn_stats", [P, NCH, 6], F32)
        k.bn_mv = sb("bn_mv", [P, 8], F32)
        k.span = sb("span", [P, 4], F32)
        k.rstd = sb("rstd", [NCH, CH], F32)
        with ExitStack() as early:
            k.raw = early.enter_context(nc.sbuf_tensor("raw", [P, 5, D], F32))
            k.raw_e = early.enter_context(nc.sbuf_tensor("raw_e", [P, 3 * DE], F32))
            k.rows = early.enter_context(nc.sbuf_tensor("rows", [26, D], F32))
            k.A, k.B, k.H = (early.enter_context(nc.sbuf_tensor(f"{n}_early", [P, NP], F32)) for n in "ABH")
            k.bank = [early.enter_context(nc.psum_tensor(f"early{i}", [P, 512], F32)) for i in range(8)]
            start_loads(k, w, w["x"])
            finish_loads(k)
            store_start(k, k.x_kept, k.A)
            layer_norm(k, k.A, k.H, k.B)
            store_start(k, k.h_kept, k.H)
            split_rows(k, k.H, DST_H, False, None)
            wait_kept(k)
        build_adjacency(k)

        k.A, k.B, k.C, k.H = (sb(n, [P, NP], F32) for n in "ABCH")
        k.bank = [ctx.enter_context(nc.psum_tensor(f"acc{i}", [P, 512], F32)) for i in range(8)]
        A, B, C, H, W, vec = k.A, k.B, k.C, k.H, k.W, k.vec
        overflow(k, w["edge_attr_32"], k.spill_edge, k.spill_dst, DE)

        load_back(k)
        for l in range(2):
            v0 = 6 * l
            if l:
                split_rows(k, H, DST_H, False, B)
                pool_neighbours(k, False, B, 0)
            overflow(k, k.spill_rows, k.spill_dst, k.spill_src, D, H, B, True, kept=None if l else k.h_kept)
            product(k, [(W["ab"[l] + "0"], B)], B, ACT.Identity, vec(v0))
            batch_norm_relu(k, B, vec(v0 + 1), vec(v0 + 2))
            product(k, [(W["ab"[l] + "1"], B)], H, ACT.Identity, vec(v0 + 3))
            batch_norm_relu(k, H, vec(v0 + 4), vec(v0 + 5))

        layer_norm(k, A, H, B, add=True)
        for l in range(4):
            split_rows(k, H, SRC_W, False, B if l else None)
            pool_neighbours(k, True, B, 1)
            overflow(k, k.spill_rows, k.spill_src, k.spill_dst, D, H, B, True)
            product(k, [(W[f"self{l}"], H), (W[f"neigh{l}"], B)], H, ACT.Relu if l < 3 else ACT.Identity, vec(12 + l))

        layer_norm(k, A, H, B, add=True)
        split_rows(k, H, SRC_W, False, None)
        load_ea(k, C)
        pool_neighbours(k, True, B, None)
        overflow(k, k.spill_rows, k.spill_src, k.spill_dst, D, H, B)
        load_ea(k, C, wait=True)
        product(k, [(W["msg"], B), (W["msg_e"], C[0:3 * DE])], B, ACT.Identity, k.zero[:, 0:1])
        product(k, [(W["up_h"], H), (W["up_m"], B)], C, ACT.Relu, vec(16))
        layer_norm(k, C, B, C, vec(17), vec(18))
        product(k, [(W["down"], B)], C, ACT.Relu, vec(19))
        layer_norm(k, C, B, C, vec(20), vec(21))
        product(k, [(W["node"], H), (k.idf[:, :], B)], C, ACT.Identity, k.zero[:, 0:1])
        layer_norm(k, C, H, C, vec(22), vec(23))

        layer_norm(k, A, H, B, add=True)
        for l in range(2):
            product(k, [(W[f"g{l}"], H)], H, ACT.Identity, k.zero[:, 0:1])
            times(k, H, 2)
            split_rows(k, H, SRC_W, True, B)
            pool_neighbours(k, True, B, None)
            overflow(k, k.spill_rows, k.spill_src, k.spill_dst, D, H, B)
            elu_stage(k, B, H, C, vec(24 + l), H)
        residual(k, H)
        store_out(k, out)


_INS = ['x', 'src', 'dst', 'edge_attr_32',
        'L0_gnn_l0_W0', 'L0_gnn_l0_b0', 'L0_gnn_l0_W1', 'L0_gnn_l0_b1',
        'L0_gnn_l0_mbn_g', 'L0_gnn_l0_mbn_b', 'L0_gnn_l0_bn_g', 'L0_gnn_l0_bn_b',
        'L0_gnn_l1_W0', 'L0_gnn_l1_b0', 'L0_gnn_l1_W1', 'L0_gnn_l1_b1',
        'L0_gnn_l1_mbn_g', 'L0_gnn_l1_mbn_b', 'L0_gnn_l1_bn_g', 'L0_gnn_l1_bn_b',
        'L1_gnn_W_self', 'L1_gnn_W_neigh', 'L1_gnn_bias',
        'L2_gnn_W_message', 'L2_gnn_W_node', 'L2_gnn_W1', 'L2_gnn_b1', 'L2_gnn_ln1_g', 'L2_gnn_ln1_b',
        'L2_gnn_W2', 'L2_gnn_b2', 'L2_gnn_ln2_g', 'L2_gnn_ln2_b', 'L2_gnn_ln_g', 'L2_gnn_ln_b',
        'L3_gnn_W1', 'L3_gnn_b1', 'L3_gnn_W2', 'L3_gnn_b2']


def kernel(**inputs):
    import numpy as _np
    import concourse.bacc as _bacc
    from concourse import mybir as _mybir
    from concourse.bass_utils import run_bass_kernel_spmd as _run

    nc = _bacc.Bacc("TRN2", target_bir_lowering=False, num_devices=1)
    arrays, args = {}, {}
    for name in _INS:
        a = _np.ascontiguousarray(inputs[name])
        arrays[f"in_{name}_dram"] = a
        args[name] = nc.dram_tensor(f"in_{name}_dram", a.shape, _mybir.dt.from_np(a.dtype), kind="ExternalInput").ap()
    out = nc.dram_tensor("out_0_dram", (N, D), _mybir.dt.float32, kind="ExternalOutput").ap()
    program(nc, args, out)
    r = _run(nc, [arrays], core_ids=[0])
    return r.results[0]["out_0_dram"]
```

```python
from contextlib import ExitStack

import concourse.bass as bass
from concourse import mybir

F32 = mybir.dt.float32
F16 = mybir.dt.float16
BF16 = mybir.dt.bfloat16
I32 = mybir.dt.int32
ALU = mybir.AluOpType
ACT = mybir.ActivationFunctionType
AX = mybir.AxisListType.X

P = 128
D = 128
N = 6250
E = 100000
DE = 32
EPS = 1e-5

SRC_W = 128
DST_W = 224
NS = -(-N // SRC_W)
ND = -(-N // DST_W)
NP = NS * SRC_W
DST_H = DST_W // 2
US = 7
UD = 4
UB = US * UD
STRIP = US * SRC_W
NU = NP // STRIP
HALF = STRIP // 2
NBKT = NS * ND
CAP = 128
assert NP == ND * DST_W and STRIP == UD * DST_W and NP == NU * STRIP

COLS = 784
GR = 8
NG = COLS // GR
LASTP = E // COLS
LASTC = E - LASTP * COLS
FULLP = 112
PW = 2 + DE
FAR = 8000
BIG = float(1 << 20)

LN_SCALE = 12
CH = HALF
NCH = NP // CH
LASTCH = N - (NCH - 1) * CH


class Sem:

    def __init__(self, handle):
        self.h = handle
        self.base = 0

    def at(self, value):
        return self.base + value

    def due(self, value):
        return not isinstance(value, int) or self.base + value > 0


def cols(c, w=CH):
    return bass.ds(c * w, w)


def chunk_pairs(eng, body):
    with eng.Fori(0, NCH // 2) as q:
        for b in range(2):
            body(q * 2 + b, b)


class Core:

    def __init__(self, nc, ctx):
        self.nc = nc
        self.ctx = ctx
        self.sems = {}
        self.n = 0

    def sem(self, name):
        if name not in self.sems:
            self.sems[name] = Sem(self.ctx.enter_context(self.nc.semaphore(name)))
        return self.sems[name]

    def next(self):
        self.n += 1
        return self.n

    def advance(self, **totals):
        for name, n in totals.items():
            self.sems[name].base += n


def constants(k):
    nc = k.nc
    fill = k.sem("fill")
    with nc.Block() as block:
        @block.gpsimd
        def _(pool):
            g = nc.gpsimd
            g.iota(k.iota[:, :], [[1, 256]], base=0, channel_multiplier=0, allow_small_or_imprecise_dtypes=True)
            for m in (k.id16, k.idb, k.idf):
                g.memset(m[:, :], 0.0).then_inc(fill.h, 1)
            g.memset(k.tri[:, :], 1.0).then_inc(fill.h, 1)
            g.memset(k.avg[:, :], 1.0 / D)
            g.memset(k.gather[:, :, :], 1.0 / D).then_inc(fill.h, 1)
            g.memset(k.spread[:, :, :], 1.0).then_inc(fill.h, 1)
            g.memset(k.eps[:, :], EPS)
            g.memset(k.zero[:, :], 0.0)
            pool.wait_ge(fill.h, fill.at(6))
            g.affine_select(out=k.gather[:, :, :], in_=k.gather[:, :, :], compare_op=ALU.is_equal, fill=0.0, base=0,
                            pattern=[[-1, NCH], [1, NCH]], channel_multiplier=0)
            g.affine_select(out=k.spread[:, :, :], in_=k.spread[:, :, :], compare_op=ALU.is_equal, fill=0.0, base=0,
                            pattern=[[-1, NCH], [0, D]], channel_multiplier=1)
            for m in (k.id16, k.idb, k.idf):
                g.affine_select(out=m[:, :], in_=m[:, :], compare_op=ALU.not_equal, fill=1.0, base=0,
                                pattern=[[-1, P]], channel_multiplier=1)
            g.affine_select(out=k.tri[:, :], in_=k.tri[:, :], compare_op=ALU.is_gt, fill=0.0, base=0,
                            pattern=[[-1, P]], channel_multiplier=1)


def rank_edges(k, src, dst, ea, small):
    nc = k.nc
    with ExitStack() as ctx:
        def sb(name, shape, dt):
            return ctx.enter_context(nc.sbuf_tensor(name, shape, dt))

        def ps(name, shape, dt):
            return ctx.enter_context(nc.psum_tensor(name, shape, dt))

        pay = sb("pay", [P, COLS, PW], F32)
        ring = sb("ring", [P, 2, GR, PW], F32)
        si = sb("si", [P, COLS], I32)
        di = sb("di", [P, COLS], I32)
        ti = sb("ti", [P, COLS], I32)
        tj = sb("tj", [P, COLS], I32)
        srcb = sb("srcb", [P, COLS], F32)
        dstw = sb("dstw", [P, COLS], F32)
        srcl = sb("srcl", [P, COLS], F32)
        dstl = sb("dstl", [P, COLS], F32)
        keyf = sb("keyf", [P, COLS], F32)
        key16 = sb("key16", [P, COLS], F16)
        rowbase = sb("rowbase", [P, COLS], F32)
        row = sb("row", [P, 2 * GR], I32)
        parts = sb("parts", [P, 2, 2, GR], F32)
        rank = sb("rank", [P, GR], F32)
        hot = sb("hot", [P, 4, 64 + ND + SRC_W + DST_W], BF16)
        dneg = sb("dneg", [P, COLS], F32)
        away = sb("away", [P, 2, DST_W], BF16)
        H_DW, H_SL, H_DL, H_END = 64, 64 + ND, 64 + ND + SRC_W, 64 + ND + SRC_W + DST_W
        blockT = sb("blockT", [64, 2, P], BF16)
        before = sb("before", [64, 2, ND], BF16)
        junk = sb("junk", [P, 2 * GR, P], F32)
        over = sb("over", [P, COLS], F32)
        oven = sb("oven", [P, 2], F32)
        oveni = sb("oveni", [1, 1], I32)
        zeros = sb("zeros", [P, 256], BF16)
        degs = sb("degs", [NS, SRC_W], F32)
        degd = sb("degd", [ND, DST_W], F32)
        t3 = sb("t3", [ND, DST_W], F32)
        cnt_s = ps("cnt_s", [P, 512], F32)
        cnt_d = ps("cnt_d", [P, 512], F32)
        keys = [ps(f"keys{b}", [P, 512], F32) for b in range(2)]
        look = [ps(f"look{b}", [P, 512], F32) for b in range(2)]
        flip = [ps(f"flip{b}", [P, 1024], BF16) for b in range(2)]

        idx_in = k.sem("idx_in")
        ea_in = [k.sem(f"ea_in{i}") for i in range(COLS // FULLP)]
        pads_set, chain = k.sem("pads_set"), k.sem("chain")
        dhot_step = k.sem("dhot_step")
        prepped, hot_ready, keyrow = k.sem("prepped"), k.sem("hot_ready"), k.sem("keyrow")
        flipped, counted, snapped = k.sem("flipped"), k.sem("counted"), k.sem("snapped")
        flip_copied, looked = k.sem("flip_copied"), k.sem("looked")
        within_done, base_done = k.sem("within_done"), k.sem("base_done")
        rows_ready, row_read, ring_full = k.sem("rows_ready"), k.sem("row_read"), k.sem("ring_full")
        scattered = [k.sem("scattered0"), k.sem("scattered1")]
        turn, deg_out, deg_ready, deg_pads = k.sem("turn"), k.sem("deg_out"), k.sem("deg_ready"), k.sem("deg_pads")
        tail, rooted, spill, spill_no = k.sem("tail"), k.sem("rooted"), k.sem("spill"), k.sem("spill_no")

        with nc.Block() as block:
            @block.sync
            def _(sp):
                sp.wait_ge(pads_set.h, pads_set.at(2))
                for a, t in ((src, si), (dst, di)):
                    for p0, p1 in ((0, FULLP), (FULLP, LASTP)):
                        sp.dma_start(t[p0:p1, :], a[p0 * COLS:p1 * COLS].rearrange("(p c) -> p c", c=COLS)
                                     ).then_inc(idx_in.h, 16)
                    sp.dma_start(t[LASTP:P, 0:LASTC], a[LASTP * COLS:E].rearrange("(p c) -> p c", p=1)
                                 ).then_inc(idx_in.h, 16)
                for to, a, loaded in small:
                    sp.dma_start(to, a).then_inc(loaded.h, 16)
                sp.wait_ge(deg_ready.h, deg_ready.at(3))
                sp.dma_start(k.factors[0].rearrange("(p c) -> p c", c=SRC_W), degs[:, :]).then_inc(deg_out.h, 16)
                sp.dma_start(k.factors[1].rearrange("(p c) -> p c", c=DST_W), degd[:, :]).then_inc(deg_out.h, 16)
                sp.dma_start(k.factors[2].rearrange("(p c) -> p c", c=DST_W), t3[:, :]).then_inc(deg_out.h, 16)
                sp.wait_ge(deg_out.h, deg_out.at(48))
                sp.wait_ge(base_done.h, base_done.at(COLS))
                for p0, p1 in ((0, FULLP), (FULLP, LASTP)):
                    sp.dma_start(si[p0:p1, :], src[p0 * COLS:p1 * COLS].rearrange("(p c) -> p c", c=COLS)
                                 ).then_inc(idx_in.h, 16)
                sp.dma_start(si[LASTP:P, 0:LASTC], src[LASTP * COLS:E].rearrange("(p c) -> p c", p=1)
                             ).then_inc(idx_in.h, 16)
                sp.wait_ge(spill.h, spill.at(6))
                sp.dma_start(k.spill_src, si[:, :]).then_inc(deg_out.h, 16)
                sp.dma_start(k.spill_dst, di[:, :]).then_inc(deg_out.h, 16)
                sp.dma_start(k.spill_edge, ti[:, :]).then_inc(deg_out.h, 16)
                sp.dma_start(k.spill_n, oveni[:, :]).then_inc(deg_out.h, 16)
                sp.wait_ge(deg_out.h, deg_out.at(48 + 64))
                for b in range(2):
                    sp.wait_ge(scattered[b].h, scattered[b].at(16 * COLS // 2))

            @block.gpsimd
            def _(pool):
                g = nc.gpsimd
                bound = pool.to_reg(NBKT * CAP - 1)

                with pool.Fori(0, NG // 2) as q:
                    for b in range(2):
                        pool.wait_ge(rows_ready.h, rows_ready.at(q * 2 + b + 1))
                        pool.sem_inc(turn.h, 1)
                        for j in range(GR):
                            g.indirect_dma_start(
                                out=k.slots, in_=ring[:, b, j, :], in_offset=None,
                                out_offset=bass.IndirectOffsetOnAxis(row[:, b * GR + j:b * GR + j + 1], 0),
                                bounds_check=bound, oob_is_err=False, engine_sem=row_read.h,
                            ).then_inc(scattered[b].h, 16)
                pool.wait_ge(deg_pads.h, deg_pads.at(1))
                g.affine_select(out=degs[:, :], in_=degs[:, :], compare_op=ALU.is_ge, fill=1.0, base=N - 1,
                                pattern=[[-1, SRC_W]], channel_multiplier=-SRC_W).then_inc(deg_pads.h, 1)
                pool.wait_ge(prepped.h, prepped.at(1))
                pool.wait_ge(spill.h, spill.at(1))
                g.iota(ti[:, :], [[1, COLS]], base=0, channel_multiplier=COLS).then_inc(spill_no.h, 1)
                g.partition_all_reduce(oven[:, 1:2], oven[:, 0:1], P, bass.bass_isa.ReduceOp.add
                                       ).then_inc(spill_no.h, 1)

            @block.vector
            def _(dve):
                V = nc.vector
                done = [0]

                def link(ins):
                    done[0] += 1
                    ins.then_inc(chain.h, 1)
                    dve.wait_ge(chain.h, chain.at(done[0]))

                V.memset(si[:, :], FAR).then_inc(pads_set.h, 1)
                V.memset(di[:, :], FAR).then_inc(pads_set.h, 1)
                V.memset(zeros[:, :], 0.0)
                V.memset(pay[96:P, LASTC:COLS, :], 0.0).then_inc(pads_set.h, 1)
                dve.wait_ge(idx_in.h, idx_in.at(96))
                V.tensor_scalar(ti[:, :], si[:, :], 7, None, ALU.logical_shift_right)
                V.tensor_scalar(si[:, :], si[:, :], SRC_W - 1, None, ALU.bitwise_and)
                link(V.tensor_scalar(tj[:, :], di[:, :], 5, None, ALU.logical_shift_right))
                V.tensor_copy(srcb[:, :], ti[:, :])
                V.tensor_copy(srcl[:, :], si[:, :])
                link(V.tensor_scalar(tj[:, :], tj[:, :], 9363.0, None, ALU.mult))
                link(V.tensor_scalar(tj[:, :], tj[:, :], 16, None, ALU.logical_shift_right))
                link(V.tensor_copy(dstw[:, :], tj[:, :]))
                V.tensor_copy(dstl[:, :], di[:, :])
                link(V.tensor_scalar(tj[:, :], tj[:, :], 2, None, ALU.logical_shift_right))
                link(V.scalar_tensor_tensor(dstl[:, :], dstw[:, :], -float(DST_W), dstl[:, :], ALU.mult, ALU.add))
                link(V.scalar_tensor_tensor(keyf[:, :], tj[:, :], float(UB - UD), dstw[:, :], ALU.mult, ALU.add))
                link(V.scalar_tensor_tensor(keyf[:, :], srcb[:, :], float(UD), keyf[:, :], ALU.mult, ALU.add))
                link(V.tensor_scalar(ti[:, :], ti[:, :], 9363.0, None, ALU.mult))
                link(V.tensor_scalar(ti[:, :], ti[:, :], 16, None, ALU.logical_shift_right))
                link(V.scalar_tensor_tensor(keyf[:, :], ti[:, :], float(NU * UB - US * UD), keyf[:, :],
                                            ALU.mult, ALU.add))
                V.tensor_copy(key16[:, :], keyf[:, :])
                link(V.tensor_scalar(rowbase[:, :], keyf[:, :], float(NBKT), BIG, ALU.is_ge, ALU.mult))
                link(V.tensor_tensor(rowbase[:, :], rowbase[:, :], keyf[:, :], ALU.add))
                dve.wait_ge(pads_set.h, pads_set.at(3))
                link(V.tensor_copy(pay[:, :, 0], srcl[:, :]))
                link(V.tensor_copy(pay[:, :, 1], dstl[:, :]))
                V.tensor_scalar(dneg[:, :], dstl[:, :], -1.0, None, ALU.mult)
                V.memset(degs[:, :], 0.0).then_inc(prepped.h, 1)
                dve.wait_ge(prepped.h, prepped.at(1))

                def one_hots(c, b):
                    if counted.due(c - 2):
                        dve.wait_ge(counted.h, counted.at(c - 2))
                    if base_done.due(c - 3):
                        dve.wait_ge(base_done.h, base_done.at(c - 3))
                    at = bass.ds(c, 1)
                    V.tensor_scalar(hot[:, b, 0:64], k.iota[:, 0:64], srcb[:, at], None, ALU.is_equal)
                    V.tensor_scalar(hot[:, b, H_DW:H_SL], k.iota[:, 0:ND], dstw[:, at], None, ALU.is_equal)
                    V.tensor_scalar(hot[:, b, H_SL:H_DL], k.iota[:, 0:SRC_W], srcl[:, at], None, ALU.is_equal
                                    ).then_inc(hot_ready.h, 1)

                def within(c, b, j):
                    dve.wait_ge(keyrow.h, keyrow.at(c + 1))
                    V.scalar_tensor_tensor(junk[:, j, :], keys[j % 2][:, 0:P], keyf[:, bass.ds(c, 1)],
                                           k.tri[:, :], ALU.is_equal, ALU.mult,
                                           accum_out=parts[:, b, 0, j:j + 1]).then_inc(within_done.h, 1)

                def base(c, b, j):
                    dve.wait_ge(looked.h, looked.at(c + 1))
                    V.scalar_tensor_tensor(junk[:, GR + j, 0:ND], look[j % 2][:, 0:ND], 1.0,
                                           hot[:, j % 4, H_DW:H_SL], ALU.mult, ALU.mult,
                                           accum_out=parts[:, b, 1, j:j + 1]).then_inc(base_done.h, 1)

                def finish(g, b):
                    dve.wait_ge(base_done.h, base_done.at((g + 1) * GR))
                    V.tensor_tensor(rank[:, :], parts[:, b, 0, :], parts[:, b, 1, :], ALU.add).then_inc(chain.h, 1)
                    dve.wait_ge(chain.h, chain.at(g + done[0] + 1))
                    V.tensor_scalar(over[:, bass.ds(g * GR, GR)], rank[:, :], float(CAP) - 0.5, None, ALU.is_gt)
                    if row_read.due((g - 1) * GR):
                        dve.wait_ge(row_read.h, row_read.at((g - 1) * GR))
                    dve.wait_ge(ring_full.h, ring_full.at(g + 1))
                    V.scalar_tensor_tensor(row[:, b * GR:(b + 1) * GR], rank[:, :], float(NBKT),
                                           rowbase[:, bass.ds(g * GR, GR)], ALU.mult, ALU.add
                                           ).then_inc(rows_ready.h, 1)

                def groups(q, first=False, last=False):
                    for b in range(2):
                        g = q * 2 + b
                        for j in range(GR):
                            c = g * GR + j
                            if not (last and b == 1 and j == GR - 1):
                                one_hots(c + 1, (j + 1) % 4)
                            within(c, b, j)
                            if j:
                                base(c - 1, b, j - 1)
                            elif not (first and b == 0):
                                base(c - 1, 1 - b, GR - 1)
                            if j == 1 and not (first and b == 0):
                                finish(g - 1, 1 - b)

                one_hots(0, 0)
                groups(0, first=True)
                with dve.Fori(1, NG // 2 - 1) as q:
                    groups(q)
                groups(NG // 2 - 1, last=True)
                base(COLS - 1, 1, GR - 1)
                finish(NG - 1, 1)
                dve.wait_ge(counted.h, counted.at(COLS + 1))
                V.tensor_copy(degs[:, :], cnt_s[0:NS, ND:ND + SRC_W]).then_inc(deg_pads.h, 1)
                V.tensor_copy(degd[:, :], cnt_d[0:ND, 0:DST_W]).then_inc(tail.h, 1)
                dve.wait_ge(tail.h, tail.at(1))
                V.tensor_scalar(t3[:, :], degd[:, :], 1.0, None, ALU.add).then_inc(tail.h, 1)
                dve.wait_ge(tail.h, tail.at(2))
                V.tensor_scalar(degd[:, :], degd[:, :], 1.0, None, ALU.max).then_inc(tail.h, 1)
                dve.wait_ge(tail.h, tail.at(3))
                V.reciprocal(degd[:, :], degd[:, :]).then_inc(deg_ready.h, 1)
                dve.wait_ge(deg_pads.h, deg_pads.at(2))
                V.reciprocal(degs[:, :], degs[:, :]).then_inc(deg_ready.h, 1)
                dve.wait_ge(rooted.h, rooted.at(1))
                V.reciprocal(t3[:, :], t3[:, :]).then_inc(deg_ready.h, 1)
                V.tensor_reduce(oven[:, 0:1], over[:, :], AX, ALU.add).then_inc(spill.h, 1)
                dve.wait_ge(spill.h, spill.at(1))
                V.tensor_scalar(over[:, :], over[:, :], -BIG, BIG, ALU.mult, ALU.add).then_inc(spill.h, 1)
                dve.wait_ge(spill.h, spill.at(2))
                dve.wait_ge(idx_in.h, idx_in.at(96 + 48))
                V.tensor_tensor(si[:, :], si[:, :], over[:, :], ALU.add).then_inc(spill.h, 1)
                V.tensor_tensor(di[:, :], di[:, :], over[:, :], ALU.add).then_inc(spill.h, 1)
                dve.wait_ge(spill_no.h, spill_no.at(1))
                V.tensor_tensor(ti[:, :], ti[:, :], over[:, :], ALU.add).then_inc(spill.h, 1)
                dve.wait_ge(spill_no.h, spill_no.at(2))
                V.tensor_copy(oveni[:, :], oven[0:1, 1:2]).then_inc(spill.h, 1)

            @block.scalar
            def _(act):
                A = nc.scalar

                def load_features(i):
                    c0, c1 = i * FULLP, (i + 1) * FULLP
                    m = min(c1, LASTC)
                    if m < c1:
                        act.wait_ge(pads_set.h, pads_set.at(3))
                    for p0, p1 in ((0, FULLP), (FULLP, LASTP)):
                        act.dma_start(pay[p0:p1, c0:c1, 2:PW],
                                      ea[p0 * COLS:p1 * COLS, :].rearrange("(p c) f -> p c f", c=COLS)[:, c0:c1, :]
                                      ).then_inc(ea_in[i].h, 16)
                    if m > c0:
                        act.dma_start(pay[LASTP:P, c0:m, 2:PW],
                                      ea[LASTP * COLS + c0:LASTP * COLS + m, :].rearrange("(p c) f -> p c f", p=1)
                                      ).then_inc(ea_in[i].h, 16)

                load_features(0)
                act.wait_ge(prepped.h, prepped.at(1))

                def square(c, b):
                    A.activation(away[:, b % 2, :], k.iota[:, 0:DST_W], ACT.Square, bias=dneg[:, bass.ds(c, 1)]
                                 ).then_inc(dhot_step.h, 1)

                def one_hot(c, b):
                    act.wait_ge(dhot_step.h, dhot_step.at(2 * c + 1))
                    A.activation(hot[:, b, H_DL:H_END], away[:, b % 2, :], ACT.Relu, bias=1.0, scale=-1.0
                                 ).then_inc(dhot_step.h, 1)

                for c in range(2):
                    square(c, c)
                    one_hot(c, c)

                def groups(q, last=False):
                    for b in range(2):
                        g = q * 2 + b
                        for j in range(GR):
                            c = g * GR + j
                            ahead = not (last and b == 1 and j >= GR - 2)
                            act.wait_ge(counted.h, counted.at(c + 1))
                            if looked.due(c - 1):
                                act.wait_ge(looked.h, looked.at(c - 1))
                            A.activation(before[0:NS, j % 2, :], cnt_s[0:NS, 0:ND], ACT.Copy
                                         ).then_inc(snapped.h, 1)
                            if ahead:
                                square(c + 2, (j + 2) % 4)
                            act.wait_ge(flipped.h, flipped.at(c + 1))
                            A.activation(blockT[0:NS, j % 2, :], flip[j % 2][0:NS, 0:P], ACT.Copy
                                         ).then_inc(flip_copied.h, 1)
                            if ahead:
                                one_hot(c + 2, (j + 2) % 4)
                            if j == GR - 2:
                                if scattered[b].due(q * (16 * GR)):
                                    act.wait_ge(scattered[b].h, scattered[b].at(q * (16 * GR)))
                                A.activation(ring[:, b, :, :], pay[:, cols(g, GR), :], ACT.Copy
                                             ).then_inc(ring_full.h, 1)

                turns = FULLP // (2 * GR)
                for i, loaded in enumerate(ea_in):
                    act.wait_ge(loaded.h, loaded.at(48 if LASTC > i * FULLP else 32))
                    groups(i * turns)
                    if i + 1 < len(ea_in):
                        load_features(i + 1)
                    final = i + 1 == len(ea_in)
                    with act.Fori(i * turns + 1, (i + 1) * turns - final) as q:
                        groups(q)
                groups(NG // 2 - 1, last=True)
                act.wait_ge(tail.h, tail.at(2))
                A.activation(t3[:, :], t3[:, :], ACT.Sqrt).then_inc(rooted.h, 1)

            @block.tensor
            def _(pe):
                T = nc.tensor
                pe.wait_ge(prepped.h, prepped.at(1))
                T.matmul(cnt_s[0:NS, 0:ND + SRC_W], zeros[:, 0:NS], zeros[:, 0:ND + SRC_W], start=True, stop=True)
                T.matmul(cnt_d[0:ND, 0:DST_W], zeros[:, 0:ND], zeros[:, 0:DST_W], start=True, stop=True
                         ).then_inc(counted.h, 1)

                def lookup(c, b):
                    pe.wait_ge(flip_copied.h, flip_copied.at(c + 1))
                    if base_done.due(c - 1):
                        pe.wait_ge(base_done.h, base_done.at(c - 1))
                    T.matmul(look[b][:, 0:ND], blockT[0:NS, b, :], before[0:NS, b, :],
                             start=True, stop=True).then_inc(looked.h, 1)

                def groups(g2, first=False):
                    for b in range(2):
                        g = g2 * 2 + b
                        for j in range(GR):
                            c = g * GR + j
                            o = j % 4
                            if within_done.due(c - 1):
                                pe.wait_ge(within_done.h, within_done.at(c - 1))
                            T.matmul(keys[j % 2][:, 0:P], key16[:, bass.ds(c, 1)].to_broadcast([P, P]),
                                     k.id16[:, :], start=True, stop=True).then_inc(keyrow.h, 1)
                            pe.wait_ge(hot_ready.h, hot_ready.at(c + 1))
                            if flip_copied.due(c - 1):
                                pe.wait_ge(flip_copied.h, flip_copied.at(c - 1))
                            T.transpose(flip[j % 2][:, 0:P], hot[:, o, 0:P], k.idb[:, :]).then_inc(flipped.h, 1)
                            if not (first and b == 0 and j == 0):
                                lookup(c - 1, (j + 1) % 2)
                            pe.wait_ge(snapped.h, snapped.at(c + 1))
                            T.matmul(cnt_s[0:NS, 0:ND + SRC_W], hot[:, o, 0:NS], hot[:, o, H_DW:H_DL],
                                     start=False, stop=True, skip_group_check=True)
                            pe.wait_ge(dhot_step.h, dhot_step.at(2 * c + 2))
                            T.matmul(cnt_d[0:ND, 0:DST_W], hot[:, o, H_DW:H_SL], hot[:, o, H_DL:H_END],
                                     start=False, stop=True, skip_group_check=True).then_inc(counted.h, 1)

                groups(0, first=True)
                with pe.Fori(1, NG // 2) as g2:
                    groups(g2)
                lookup(COLS - 1, 1)


def build_adjacency(k):
    nc = k.nc
    NBANK = 4
    with ExitStack() as ctx:
        def sb(name, shape, dt):
            return ctx.enter_context(nc.sbuf_tensor(name, shape, dt))

        slot = sb("slot", [P, 2, UB, PW], F32)
        S = sb("S", [P, 2, UB, SRC_W], BF16)
        Dh = sb("Dh", [P, 2, UB, DST_W], BF16)
        eas = sb("eas", [P, 2, UB, 3 * DE], BF16)
        rest = sb("rest", [P, UB, DE], F32)
        sums = sb("sums", [P, STRIP], F32)
        ads = sb("ads", [DST_H, 2, 2 * UD, STRIP], F16)
        asd = sb("asd", [P, 2, US, STRIP], F16)
        easum = sb("easum", [3 * DE, NP], F32)
        bank = [ctx.enter_context(nc.psum_tensor(f"bank{i}", [P, 512], F32)) for i in range(NBANK)]
        accs = [ctx.enter_context(nc.psum_tensor(f"pooled_acc{i}", [P, 512], F32)) for i in range(2)]
        eab = [ctx.enter_context(nc.psum_tensor(f"eab{i}", [P, 512], F32)) for i in range(2)]

        slot_in = [k.sem("slot_in0"), k.sem("slot_in1")]
        hots, split, ea_chain = k.sem("hots"), k.sem("split"), k.sem("ea_chain")
        filled, act_out = k.sem("filled"), k.sem("act_out")
        ads_used, sums_full, hs_in = k.sem("ads_used"), k.sem("sums_full"), k.sem("hs_in")
        sums_read, sums_out = k.sem("sums_read"), k.sem("sums_out")
        ea_filled, ea_added, zeroed = k.sem("ea_filled"), k.sem("ea_added"), k.sem("zeroed")
        unit_out = [k.sem("unit_out0"), k.sem("unit_out1")]
        ea_out, turn, turn_sp, turn_act = k.sem("ea_out"), k.sem("turn"), k.sem("turn_sp"), k.sem("turn_act")

        items = []
        for jj in range(UD):
            for h in range(2):
                for lo, hi in ((0, 4), (4, US)):
                    items.append(("ds", 2 * jj + h, lo, hi))
        for ii in range(US):
            for lo, hi in ((0, 2), (2, 4)):
                items.append(("sd", ii, lo, hi))
        NI = len(items)
        DS_ITEMS = 4 * UD

        def target(item, b):
            kind, r, lo, hi = item
            if kind == "ds":
                return ads[:, b, r, lo * SRC_W:hi * SRC_W]
            return asd[:, b, r, lo * DST_W:hi * DST_W]

        def bank_of(v, i):
            return bank[(v * NI + i) % NBANK]

        def source(v, i):
            kind, r, lo, hi = items[i]
            if kind == "ds":
                return bank_of(v, i)[0:DST_H, 0:(hi - lo) * SRC_W]
            return bank_of(v, i)[:, 0:(hi - lo) * DST_W]

        def unit(q, v):
            return q * (2 * NU) + v, v, v % 2, q * NU + v // 2, q * 2 + v // NU

        def units(eng, body):
            for v in range(NU):
                body(0, v)
            with eng.Fori(0, NU // 2) as q:
                for v in range(NU, 3 * NU):
                    body(q, v)

        NUNIT = NU * NU
        assert NU % 2 == 1

        with nc.Block() as block:
            @block.sync
            def _(sp):
                def store_sums(s):
                    sp.wait_ge(sums_read.h, sums_read.at(2 * s + 2))
                    sp.sem_inc(turn_sp.h, 1)
                    sp.dma_start(k.pooled[:, cols(s, STRIP)], sums[:, :]).then_inc(sums_out.h, 16)

                def body(q, v):
                    u, v, b, n, s = unit(q, v)
                    sp.wait_ge(act_out.h, act_out.at(u * NI + DS_ITEMS))
                    sp.sem_inc(turn_sp.h, 1)
                    sp.dma_start(k.counts_ds[bass.ds(u, 1)].rearrange("u p r c -> (u p) (r c)"),
                                 ads[:, b, :, :].rearrange("p r c -> p (r c)")).then_inc(unit_out[b].h, 16)
                    sp.wait_ge(act_out.h, act_out.at((u + 1) * NI))
                    sp.sem_inc(turn_sp.h, 1)
                    sp.dma_start(k.counts_sd[bass.ds(u, 1)].rearrange("u p r c -> (u p) (r c)"),
                                 asd[:, b, :, :].rearrange("p r c -> p (r c)")).then_inc(unit_out[b].h, 16)
                    if v >= NU and v % NU == 0:
                        store_sums(s - 1)

                units(sp, body)
                store_sums(NU - 1)
                sp.wait_ge(ea_added.h, ea_added.at(2 * NUNIT))
                sp.dma_start(k.ea_sums, easum[:, :]).then_inc(ea_out.h, 16)
                sp.wait_ge(ea_out.h, ea_out.at(16))
                sp.wait_ge(sums_out.h, sums_out.at(16 * NU))
                sp.wait_ge(unit_out[0].h, unit_out[0].at(32 * (NUNIT // 2 + 1)))
                sp.wait_ge(unit_out[1].h, unit_out[1].at(32 * (NUNIT // 2)))

            @block.gpsimd
            def _(pool):
                g = nc.gpsimd
                g.memset(easum[:, :], 0.0).then_inc(zeroed.h, 1)

                def body(q, v):
                    u, v, b, n, s = unit(q, v)
                    pool.wait_ge(slot_in[b].h, slot_in[b].at(n * 16 + 16))
                    pool.sem_inc(turn.h, 1)
                    if ea_filled.due(2 * u - 2):
                        pool.wait_ge(ea_filled.h, ea_filled.at(2 * u - 2))
                    pool.sem_inc(turn.h, 1)
                    f = slot[:, b, :, 2:PW]
                    r = rest[:, :, :]
                    hi, mid, lo = (eas[:, b, :, i * DE:(i + 1) * DE] for i in range(3))
                    g.tensor_copy(hi, f).then_inc(ea_chain.h, 1)
                    pool.wait_ge(ea_chain.h, ea_chain.at(u * 3 + 1))
                    pool.sem_inc(turn.h, 1)
                    if split.due(u):
                        pool.wait_ge(split.h, split.at(u))
                        pool.sem_inc(turn.h, 1)
                    g.tensor_tensor(r, f, hi, ALU.subtract).then_inc(ea_chain.h, 1)
                    pool.wait_ge(ea_chain.h, ea_chain.at(u * 3 + 2))
                    pool.sem_inc(turn.h, 1)
                    g.tensor_copy(mid, r).then_inc(ea_chain.h, 1)
                    pool.wait_ge(ea_chain.h, ea_chain.at(u * 3 + 3))
                    pool.sem_inc(turn.h, 1)
                    g.tensor_tensor(lo, r, mid, ALU.subtract).then_inc(split.h, 1)

                units(pool, body)

            @block.vector
            def _(dve):
                V = nc.vector

                def one_hots(u, b, n):
                    dve.wait_ge(slot_in[b].h, slot_in[b].at(n * 16 + 16))
                    if ea_filled.due(2 * u - 2):
                        dve.wait_ge(ea_filled.h, ea_filled.at(2 * u - 2))
                    for i in range(UB):
                        V.tensor_scalar(S[:, b, i, :], k.iota[:, 0:SRC_W], slot[:, b, i, 0:1], None, ALU.is_equal)
                        last = V.tensor_scalar(Dh[:, b, i, :], k.iota[:, 0:DST_W], slot[:, b, i, 1:2], None,
                                               ALU.is_equal)
                    last.then_inc(hots.h, 1)

                def add_ea(u):
                    t = u % NU
                    for h in range(2):
                        dve.wait_ge(ea_filled.h, ea_filled.at(u * 2 + h + 1))
                        at = bass.ds(t * STRIP + h * HALF, HALF)
                        V.tensor_tensor(easum[:, at], easum[:, at], eab[h][0:3 * DE, 0:HALF], ALU.add
                                        ).then_inc(ea_added.h, 1)

                def body(q, v):
                    u, v, b, n, s = unit(q, v)
                    one_hots(u, b, n)
                    if v > 0:
                        add_ea(u - 1)

                dve.wait_ge(zeroed.h, zeroed.at(1))
                units(dve, body)
                add_ea(NUNIT - 1)

            @block.scalar
            def _(act):
                A = nc.scalar

                def load(u, b):
                    act.dma_start(slot[:, b, :, :].rearrange("p a b -> p (a b)"), rows[:, cols(u, UB * PW)]
                                  ).then_inc(slot_in[b].h, 16)

                def read_sums(s):
                    if sums_out.due(16 * s):
                        act.wait_ge(sums_out.h, sums_out.at(16 * s))
                    for h in range(2):
                        if h == 0:
                            act.wait_ge(sums_full.h, sums_full.at(s + 1))
                        else:
                            act.wait_ge(ads_used.h, ads_used.at(s * NU + NU))
                        A.activation(sums[:, h * HALF:(h + 1) * HALF], accs[h][:, 0:HALF], ACT.Copy,
                                     scale=k.span[:, 3:4]).then_inc(sums_read.h, 1)

                def body(q, v):
                    u, v, b, n, s = unit(q, v)
                    if unit_out[b].due(n * 32):
                        act.wait_ge(unit_out[b].h, unit_out[b].at(n * 32))
                    if ads_used.due(u - 1):
                        act.wait_ge(ads_used.h, ads_used.at(u - 1))
                    for i in range(NI):
                        act.wait_ge(filled.h, filled.at(u * NI + i + 1))
                        A.activation(target(items[i], b), source(v, i), ACT.Copy).then_inc(act_out.h, 1)
                        if i == 4:
                            act.wait_ge(hots.h, hots.at(u + 1))
                            act.wait_ge(ea_chain.h, ea_chain.at(3 * u + 2))
                            act.sem_inc(turn_act.h, 1)
                            load((u + 2) % NUNIT, b)
                    if v >= NU and v % NU == 0:
                        read_sums(s - 1)

                rows = k.slots.rearrange("(p r) w -> p (r w)", p=P)
                load(0, 0)
                load(1, 1)
                act.dma_start(k.hs[0:DST_H, :, :, :], k.hs_kept).then_inc(hs_in.h, 16)
                units(act, body)
                read_sums(NU - 1)
                for b in range(2):
                    act.wait_ge(slot_in[b].h, slot_in[b].at(16 * (NUNIT // 2 + 1 + (1 - b))))

            @block.tensor
            def _(pe):
                T = nc.tensor

                def pooling(v, t, b):
                    for r in range(2 * UD):
                        for part in range(2):
                            for h in range(2):
                                first = t == 0 and r == 0 and part == 0
                                final = r == 2 * UD - 1 and part == 1
                                yield h, first, final, lambda h=h, r=r, part=part, first=first, final=final: T.matmul(
                                    accs[h][:, 0:HALF], k.hs[0:DST_H, t * 2 * UD + r, part, :],
                                    ads[:, b, r, h * HALF:(h + 1) * HALF], start=first,
                                    stop=final and t == NU - 1, skip_group_check=True)

                def pool_some(u, s, steps, t, n):
                    for h, first, final, mm in steps[:n]:
                        if first and sums_read.due(2 * s - 1 + h):
                            pe.wait_ge(sums_read.h, sums_read.at(2 * s - 1 + h))
                        ins = mm()
                        if final and h == 1:
                            ins.then_inc(ads_used.h, 1)
                        elif final and t == NU - 1:
                            ins.then_inc(sums_full.h, 1)
                    del steps[:n]

                def body(q, v):
                    u, v, b, n, s = unit(q, v)
                    steps = []
                    if v > 0:
                        pu, _, pb, _, ps_ = unit(q, v - 1)
                        pt = (v - 1) % NU
                        steps = list(pooling(v - 1, pt, pb))
                    total = len(steps)
                    pe.wait_ge(hots.h, hots.at(u + 1))
                    for i, (kind, r, lo, hi) in enumerate(items):
                        if act_out.due(u * NI + i - NBANK + 1):
                            pe.wait_ge(act_out.h, act_out.at(u * NI + i - NBANK + 1))
                        for a in range(lo, hi):
                            if kind == "ds":
                                jj, h = r // 2, r % 2
                                kk = a * UD + jj
                                mm = T.matmul(bank_of(v, i)[0:DST_H, (a - lo) * SRC_W:(a - lo + 1) * SRC_W],
                                              Dh[:, b, kk, h * DST_H:(h + 1) * DST_H], S[:, b, kk, :],
                                              start=True, stop=True)
                            else:
                                kk = r * UD + a
                                mm = T.matmul(bank_of(v, i)[:, (a - lo) * DST_W:(a - lo + 1) * DST_W],
                                              S[:, b, kk, :], Dh[:, b, kk, :], start=True, stop=True)
                        mm.then_inc(filled.h, 1)
                        if total and i >= 3:
                            if i == 3 and v == 1 and isinstance(q, int):
                                pe.wait_ge(hs_in.h, hs_in.at(16))
                            if i == 3:
                                pe.wait_ge(act_out.h, act_out.at(u * NI - NI + DS_ITEMS))
                            due = min(total, -(-(i - 2) * total // (NI - 6)))
                            pool_some(pu, ps_, steps, pt, due - (total - len(steps)))
                    pe.wait_ge(split.h, split.at(u + 1))
                    for h in range(2):
                        if ea_added.due(u * 2 + h - 1):
                            pe.wait_ge(ea_added.h, ea_added.at(u * 2 + h - 1))
                        for jj in range(2 * h, 2 * h + 2):
                            for ii in range(US):
                                kk = ii * UD + jj
                                mm = T.matmul(eab[h][0:3 * DE, (jj % 2) * DST_W:(jj % 2 + 1) * DST_W],
                                              eas[:, b, kk, :], Dh[:, b, kk, :],
                                              start=(ii == 0), stop=(ii == US - 1))
                        mm.then_inc(ea_filled.h, 1)

                units(pe, body)
                pe.wait_ge(act_out.h, act_out.at(NUNIT * NI - NI + DS_ITEMS))
                steps = list(pooling(NU - 1, NU - 1, 0))
                pool_some(NUNIT - 1, NU - 1, steps, NU - 1, len(steps))


def small_loads(k, w):
    straight = [("a0", w["L0_gnn_l0_W0"]), ("a1", w["L0_gnn_l0_W1"]), ("b0", w["L0_gnn_l1_W0"]),
                ("b1", w["L0_gnn_l1_W1"]), ("g0", w["L3_gnn_W1"]), ("g1", w["L3_gnn_W2"])]
    straight += [(f"self{i}", w["L1_gnn_W_self"][i]) for i in range(4)]
    straight += [(f"neigh{i}", w["L1_gnn_W_neigh"][i]) for i in range(4)]
    turned = [("msg", w["L2_gnn_W_message"][:, 0:D]), ("node", w["L2_gnn_W_node"]),
              ("up_h", w["L2_gnn_W1"][:, 0:D]), ("up_m", w["L2_gnn_W1"][:, D:2 * D]), ("down", w["L2_gnn_W2"])]
    vectors = []
    for i in range(2):
        vectors += [w[f"L0_gnn_l{i}_{n}"] for n in ("b0", "mbn_g", "mbn_b", "b1", "bn_g", "bn_b")]
    vectors += [w["L1_gnn_bias"][i] for i in range(4)]
    vectors += [w[f"L2_gnn_{n}"] for n in ("b1", "ln1_g", "ln1_b", "b2", "ln2_g", "ln2_b", "ln_g", "ln_b")]
    vectors += [w["L3_gnn_b1"], w["L3_gnn_b2"]]
    k.turned = [name for name, _ in turned]
    k.nv = len(vectors)
    k.W = {name: k.weights[:, i, :] for i, (name, _) in enumerate(straight + turned)}
    k.W["msg_e"] = k.weights[0:3 * DE, len(straight) + len(turned), :]
    k.vec = lambda i: k.vectors[:, i:i + 1]
    w_in, v_in = k.sem("w_in"), k.sem("v_in")
    loads = [(k.raw[:, i, :], a, w_in) for i, (_, a) in enumerate(turned)]
    loads += [(k.raw_e[:, i * DE:(i + 1) * DE], w["L2_gnn_W_message"][:, D:D + DE], w_in) for i in range(3)]
    loads += [(k.W[name], a, w_in) for name, a in straight]
    k.w_in = 16 * len(loads)
    loads += [(k.rows[i:i + 1, :], a.rearrange("(a f) -> a f", a=1), v_in) for i, a in enumerate(vectors)]
    return loads


X_PART = (NS - 1) // 4


def start_x_and_slots(k, x):
    nc = k.nc
    x_in, x_pad = [k.sem(f"x_in{i}") for i in range(4)], k.sem("x_pad")
    blank, empty_set, slots_init = k.sem("blank"), k.sem("empty_set"), k.sem("slots_init")
    full = NS - 1
    rowsn = k.B[:, :].rearrange("p (b f) -> p b f", f=D)
    flat = k.slots.rearrange("(p r) w -> p r w", p=P)
    with nc.Block() as block:
        @block.vector
        def _(dve):
            nc.vector.memset(k.B[:, full * D:NP], 0.0).then_inc(x_pad.h, 1)
            nc.vector.memset(k.empty[:, :, :], 0.0).then_inc(blank.h, 1)
            dve.wait_ge(blank.h, blank.at(1))
            nc.vector.memset(k.empty[:, :, 0:2], -1.0).then_inc(empty_set.h, 1)

        @block.sync
        def _(sp):
            for i in range(4):
                sp.dma_start(rowsn[:, i * X_PART:(i + 1) * X_PART, :],
                             x[i * X_PART * P:(i + 1) * X_PART * P, :].rearrange("(b p) f -> p b f", p=P)
                             ).then_inc(x_in[i].h, 16)
            sp.wait_ge(x_pad.h, x_pad.at(1))
            sp.dma_start(rowsn[0:N - full * P, full, :], x[full * P:N, :]).then_inc(x_in[3].h, 16)
            sp.wait_ge(empty_set.h, empty_set.at(1))
            for q in range(NBKT // 98):
                sp.dma_start(flat[:, q * 98:(q + 1) * 98, :], k.empty[:, :, :]).then_inc(slots_init.h, 16)


def turn_x(k):
    nc = k.nc
    x_T, x_copied, x_in = k.sem("x_T"), k.sem("x_copied"), [k.sem(f"x_in{i}") for i in range(4)]
    rowsn = k.B[:, :].rearrange("p (b f) -> p b f", f=D)
    NGRP = -(-NS // 4)
    with nc.Block() as block:
        @block.tensor
        def _(pe):
            for g in range(NGRP):
                if 4 * g % X_PART == 0 and 4 * g < NS - 1:
                    part = 4 * g // X_PART
                    pe.wait_ge(x_in[part].h, x_in[part].at(32 if part == 3 else 16))
                if g >= 4:
                    pe.wait_ge(x_copied.h, x_copied.at(g - 3))
                for i in range(4 * g, min(4 * g + 4, NS)):
                    mm = nc.tensor.transpose(k.bank[4 + g % 4][:, (i % 4) * P:(i % 4 + 1) * P], rowsn[:, i, :],
                                             k.idf[:, :])
                mm.then_inc(x_T.h, 1)

        @block.vector
        def _(dve):
            for g in range(NGRP):
                dve.wait_ge(x_T.h, x_T.at(g + 1))
                n = min(4, NS - 4 * g) * P
                nc.vector.tensor_copy(k.A[:, g * 512:g * 512 + n], k.bank[4 + g % 4][:, 0:n]).then_inc(x_copied.h, 1)


def turn_weights(k):
    nc = k.nc
    w_in, v_in, w_T, w_out = k.sem("w_in"), k.sem("v_in"), k.sem("w_T"), k.sem("w_out")
    nv, nt = k.nv, len(k.turned)
    jobs = [(k.bank[i % 4][:, 0:D], k.raw[:, i, :], k.idf[:, :], k.W[name]) for i, name in enumerate(k.turned)]
    jobs.append((k.bank[nt % 4][0:3 * DE, 0:D], k.raw_e[:, :], k.idf[:, :], k.W["msg_e"]))
    jobs.append((k.bank[(nt + 1) % 4][:, 0:nv], k.rows[:, :], k.idf[0:nv, 0:nv], k.vectors[:, 0:nv]))
    with nc.Block() as block:
        @block.tensor
        def _(pe):
            pe.wait_ge(w_in.h, w_in.at(k.w_in))
            pe.wait_ge(v_in.h, v_in.at(16 * nv))
            for i, (turned, raw, identity, _) in enumerate(jobs):
                if i >= 4:
                    pe.wait_ge(w_out.h, w_out.at(i - 3))
                nc.tensor.transpose(turned, raw, identity).then_inc(w_T.h, 1)

        @block.scalar
        def _(act):
            for i, (turned, _, _, to) in enumerate(jobs):
                act.wait_ge(w_T.h, w_T.at(i + 1))
                nc.scalar.activation(to, turned, ACT.Copy).then_inc(w_out.h, 1)


def residual(k, y):
    nc = k.nc
    with nc.Block() as block:
        @block.vector
        def _(dve):
            with dve.Fori(0, NU) as s:
                at = cols(s, STRIP)
                nc.vector.tensor_tensor(k.A[:, at], k.A[:, at], y[:, at], ALU.add)


def store_out(k, out):
    nc = k.nc
    o_T, o_copied, o_out = k.sem("o_T"), k.sem("o_copied"), k.sem("o_out")
    full = NS - 1
    rowsn = k.B[:, :].rearrange("p (b f) -> p b f", f=D)
    NGRP = -(-NS // 4)
    with nc.Block() as block:
        @block.tensor
        def _(pe):
            for g in range(NGRP):
                if o_copied.due(g - 3):
                    pe.wait_ge(o_copied.h, o_copied.at(g - 3))
                for i in range(4 * g, min(4 * g + 4, NS)):
                    mm = nc.tensor.transpose(k.bank[g % 4][:, (i % 4) * P:(i % 4 + 1) * P],
                                             k.A[:, i * P:(i + 1) * P], k.idf[:, :])
                mm.then_inc(o_T.h, 1)

        @block.scalar
        def _(act):
            for g in range(NGRP):
                act.wait_ge(o_T.h, o_T.at(g + 1))
                n = min(4, NS - 4 * g) * P
                nc.scalar.activation(k.B[:, g * 512:g * 512 + n], k.bank[g % 4][:, 0:n], ACT.Copy
                                     ).then_inc(o_copied.h, 1)

        @block.sync
        def _(sp):
            for g in range(NGRP - 1):
                sp.wait_ge(o_copied.h, o_copied.at(g + 1))
                sp.dma_start(out[g * 512:(g + 1) * 512, :].rearrange("(b p) f -> p b f", p=P),
                             rowsn[:, 4 * g:4 * g + 4, :]).then_inc(o_out.h, 16)
            sp.wait_ge(o_copied.h, o_copied.at(NGRP))
            sp.dma_start(out[full * P:N, :], rowsn[0:N - full * P, full, :]).then_inc(o_out.h, 16)
            sp.wait_ge(o_out.h, o_out.at(16 * NGRP))


def layer_norm(k, src, dst, squares, gain=None, shift=None, add=False):
    nc = k.nc
    mean, centred, squared = k.sem("ln_mean"), k.sem("ln_centred"), k.sem("ln_squared")
    var, rooted, inverse = k.sem("ln_var"), k.sem("ln_rooted"), k.sem("ln_inverse")
    spread, final, added, turn = k.sem("ln_spread"), k.sem("ln_final"), k.sem("ln_added"), k.sem("ln_turn")
    with nc.Block() as block:
        @block.tensor
        def _(pe):
            def means(c, b):
                pe.wait_ge(centred.h, centred.at(c + 1))
                if add:
                    pe.wait_ge(added.h, added.at(c + 1))
                    pe.sem_inc(turn.h, 1)
                nc.tensor.matmul(k.bank[b][:, 0:CH], k.avg[:, :], src[:, cols(c)], start=True, stop=True
                                 ).then_inc(mean.h, 1)

            chunk_pairs(pe, means)
            for c in range(NCH):
                pe.wait_ge(squared.h, squared.at(c + 1))
                nc.tensor.matmul(k.bank[2][0:NCH, 0:CH], k.gather[:, c, :], squares[:, c * CH:(c + 1) * CH],
                                 start=(c == 0), stop=(c == NCH - 1)).then_inc(var.h, 1)
            pe.wait_ge(inverse.h, inverse.at(1))
            for c in range(NCH):
                if c >= 2:
                    pe.wait_ge(final.h, final.at(c - 1))
                nc.tensor.matmul(k.bank[3 + c % 2][:, 0:CH], k.spread[:, c, :], k.rstd[:, :], start=True, stop=True
                                 ).then_inc(spread.h, 1)

        @block.vector
        def _(dve):
            V = nc.vector
            dve.sem_inc(centred.h, 2)

            def centre(c, b):
                dve.wait_ge(mean.h, mean.at(c + 1))
                V.tensor_tensor(dst[:, cols(c)], src[:, cols(c)], k.bank[b][:, 0:CH], ALU.subtract
                                ).then_inc(centred.h, 1)

            def scale(c, b):
                dve.wait_ge(spread.h, spread.at(c + 1))
                at = cols(c)
                if gain is None:
                    V.scalar_tensor_tensor(dst[:, at], dst[:, at], 0.0, k.bank[3 + b][:, 0:CH], ALU.max, ALU.mult
                                           ).then_inc(final.h, 1)
                else:
                    V.scalar_tensor_tensor(dst[:, at], dst[:, at], gain, k.bank[3 + b][:, 0:CH], ALU.mult, ALU.mult
                                           ).then_inc(final.h, 1)

            def residual(c, b):
                V.tensor_tensor(src[:, cols(c)], src[:, cols(c)], dst[:, cols(c)], ALU.add).then_inc(added.h, 1)

            if add:
                chunk_pairs(dve, residual)
                dve.wait_ge(added.h, added.at(NCH))
            chunk_pairs(dve, centre)
            dve.wait_ge(rooted.h, rooted.at(1))
            V.reciprocal(k.rstd[:, :], k.rstd[:, :]).then_inc(inverse.h, 1)
            chunk_pairs(dve, scale)

        @block.scalar
        def _(act):
            A = nc.scalar

            def square(c, b):
                act.wait_ge(centred.h, centred.at(2 + c + 1))
                A.activation(squares[:, cols(c)], dst[:, cols(c)], ACT.Square).then_inc(squared.h, 1)

            def shift_in(c, b):
                act.wait_ge(final.h, final.at(c + 1))
                A.activation(dst[:, cols(c)], dst[:, cols(c)], ACT.Identity, bias=shift)

            chunk_pairs(act, square)
            act.wait_ge(var.h, var.at(NCH))
            A.activation(k.rstd[:, :], k.bank[2][0:NCH, 0:CH], ACT.Sqrt, bias=k.eps[0:NCH, 0:1]
                         ).then_inc(rooted.h, 1)
            if shift is not None:
                chunk_pairs(act, shift_in)
    k.advance(ln_mean=NCH, ln_centred=NCH + 2, ln_squared=NCH, ln_var=NCH, ln_rooted=1, ln_inverse=1,
              ln_spread=NCH, ln_final=NCH, ln_added=NCH if add else 0)


def product_times(k, weight, v, factor):
    nc = k.nc
    summed, moved, row_in = k.sem("p_summed"), k.sem("p_moved"), k.sem("row_in")
    with nc.Block() as block:
        @block.tensor
        def _(pe):
            def body(c, b):
                pe.wait_ge(moved.h, moved.at(c + 1))
                nc.tensor.matmul(k.bank[b][:, 0:CH], weight, v[:, cols(c)], start=True, stop=True
                                 ).then_inc(summed.h, 1)

            chunk_pairs(pe, body)

        @block.vector
        def _(dve):
            dve.sem_inc(moved.h, 2)
            dve.wait_ge(row_in.h, row_in.at(0))

            def body(c, b):
                dve.wait_ge(summed.h, summed.at(c + 1))
                nc.vector.tensor_tensor(v[:, cols(c)], k.bank[b][:, 0:CH], factor[:, cols(c)], ALU.mult
                                        ).then_inc(moved.h, 1)

            chunk_pairs(dve, body)
    k.advance(p_summed=NCH, p_moved=NCH + 2)


def product(k, terms, dst, func, bias, stats=False):
    nc = k.nc
    summed, moved = k.sem("summed"), k.sem("moved")
    with nc.Block() as block:
        @block.tensor
        def _(pe):
            def body(c, b):
                pe.wait_ge(moved.h, moved.at(c + 1))
                for i, (w, v) in enumerate(terms):
                    mm = nc.tensor.matmul(k.bank[b][:, 0:CH], w, v[:, cols(c)], start=(i == 0),
                                          stop=(i == len(terms) - 1))
                mm.then_inc(summed.h, 1)

            chunk_pairs(pe, body)

        @block.scalar
        def _(act):
            act.sem_inc(moved.h, 2)

            def body(c, b):
                act.wait_ge(summed.h, summed.at(c + 1))
                nc.scalar.activation(dst[:, cols(c)], k.bank[b][:, 0:CH], func, bias=bias).then_inc(moved.h, 1)

            chunk_pairs(act, body)

        @block.vector
        def _(dve):
            if stats:
                for c in range(NCH):
                    n = CH if c < NCH - 1 else LASTCH
                    dve.wait_ge(moved.h, moved.at(2 + c + 1))
                    nc.vector.bn_stats(k.bn_stats[:, c, :], dst[:, c * CH:c * CH + n])

    k.advance(summed=NCH, moved=NCH + 2)


def batch_norm_relu(k, v, gain, shift):
    nc = k.nc
    stat, bn_root, bn_scaled = k.sem("bn_stat"), k.sem("bn_root"), k.sem("bn_scaled")
    st, mv = k.bn_stats, k.bn_mv
    with nc.Block() as block:
        @block.vector
        def _(dve):
            V = nc.vector
            V.bn_aggr(mv[:, 0:2], st[:, :, :].rearrange("p a b -> p (a b)")).then_inc(stat.h, 1)
            dve.wait_ge(bn_root.h, bn_root.at(1))
            V.reciprocal(mv[:, 3:4], mv[:, 2:3]).then_inc(stat.h, 1)
            dve.wait_ge(stat.h, stat.at(2))
            V.tensor_tensor(mv[:, 4:5], mv[:, 3:4], gain, ALU.mult).then_inc(stat.h, 1)
            dve.wait_ge(stat.h, stat.at(3))
            with dve.Fori(0, NU) as s:
                at = cols(s, STRIP)
                V.tensor_scalar(v[:, at], v[:, at], mv[:, 0:1], mv[:, 4:5], ALU.subtract, ALU.mult
                                ).then_inc(bn_scaled.h, 1)

        @block.scalar
        def _(act):
            act.wait_ge(stat.h, stat.at(1))
            nc.scalar.activation(mv[:, 2:3], mv[:, 1:2], ACT.Sqrt, bias=k.eps[:, 0:1]).then_inc(bn_root.h, 1)
            with act.Fori(0, NU) as s:
                act.wait_ge(bn_scaled.h, bn_scaled.at(s + 1))
                at = cols(s, STRIP)
                nc.scalar.activation(v[:, at], v[:, at], ACT.Relu, bias=shift)
    k.advance(bn_stat=3, bn_root=1, bn_scaled=NU)


NBUF = 7


def table_pieces(k, over_src):
    table = k.counts_sd if over_src else k.counts_ds
    rows, per = (SRC_W, US) if over_src else (DST_H, 2 * UD)
    return table, rows, per, [(t, lo, hi) for t in range(NU) for lo, hi in ((0, 4), (4, per))]


def load_piece(k, sp, over_src, tbuf, s, i):
    table, rows, _, pieces = table_pieces(k, over_src)
    t, lo, hi = pieces[i]
    u = s + t * NU if over_src else s * NU + t
    sp.dma_start(tbuf[0:rows, i % NBUF, 0:hi - lo, :],
                 table[bass.ds(u, 1), :, lo:hi, :].rearrange("u p r c -> (u p) r c")
                 ).then_inc(k.sem(f"table_in{i % NBUF}").h, 16)


def split_and_pool(k, v, over_src, scaled, dst, factor, own=None, signed=False, load_factor=True,
                   peaks=False, layer=None):
    with k.nc.sbuf_tensor(f"tbuf{k.next()}", [P, NBUF, 4, STRIP], F16) as tbuf:
        split_rows(k, v, over_src, signed, scaled, tbuf, k.peaks if peaks else v, layer is not None)
        pool_neighbours(k, over_src, dst, factor, own, tbuf, load_factor, v, layer)


def split_rows(k, v, over_src, signed, scaled, tbuf=None, tops_of=None, keep=False):
    nc = k.nc
    rows = SRC_W if over_src else DST_H
    nb = NP // rows
    top, scaled_ok, turned, hi_ok, lo_ok = k.sem("top"), k.sem("scaled"), k.sem("turned"), k.sem("hi_ok"), k.sem("lo_ok")
    m = k.span
    ng = -(-nb // 4)
    EXP1 = 1 << 23
    from_ = v if scaled is None else scaled
    unit = 2.0 ** LN_SCALE if scaled is None else 1.0
    with nc.Block() as block:
        if tbuf is not None:
            @block.sync
            def _(sp):
                for i in range(NBUF):
                    load_piece(k, sp, over_src, tbuf, 0, i)
                if keep:
                    sp.dma_start(k.h_kept, v[:, :]).then_inc(k.sem("v_kept").h, 16)

        @block.vector
        def _(dve):
            V = nc.vector
            n = [0]
            k.tops = 0

            def link(ins):
                n[0] += 1
                ins.then_inc(top.h, 1)
                dve.wait_ge(top.h, top.at(n[0]))

            def exponents():
                V.tensor_reduce(m[:, 0:1], tops_of[:, :], AX, ALU.max).then_inc(top.h, 1)
                n[0] += 1
                if signed:
                    link(V.tensor_reduce(m[:, 1:2], v[:, :], AX, ALU.min))
                    link(V.scalar_tensor_tensor(m[:, 0:1], m[:, 1:2], -1.0, m[:, 0:1], ALU.mult, ALU.max))
                else:
                    dve.wait_ge(top.h, top.at(n[0]))
                link(V.tensor_scalar(m[:, 0:1], m[:, 0:1], 2.0 ** -60, None, ALU.max))
                mi = m[:, :].bitcast(I32)
                link(V.tensor_scalar(mi[:, 1:2], mi[:, 0:1], 0x7F800000, None, ALU.bitwise_and))
                V.tensor_scalar(mi[:, 2:3], mi[:, 1:2], -1.0, float((2 * 127 + 14) * EXP1), ALU.mult, ALU.add
                                ).then_inc(top.h, 1)
                V.tensor_scalar(mi[:, 3:4], mi[:, 1:2], float(-14 * EXP1), None, ALU.add).then_inc(top.h, 1)
                n[0] += 2
                k.tops = n[0]

            if scaled is None:
                V.memset(m[:, 3:4], 2.0 ** -LN_SCALE)
            else:
                exponents()
            for g in range(ng):
                w = min(4, nb - 4 * g)
                dve.wait_ge(hi_ok.h, hi_ok.at(g + 1))
                V.scalar_tensor_tensor(k.hs[0:rows, 4 * g:4 * g + w, 1, :],
                                       k.bank[g % 4][0:rows, 0:w * P].rearrange("p (a f) -> p a f", f=P), unit,
                                       k.hs[0:rows, 4 * g:4 * g + w, 0, :], ALU.mult, ALU.subtract
                                       ).then_inc(lo_ok.h, 1)

        tops = k.tops

        @block.scalar
        def _(act):
            if scaled is not None:
                act.wait_ge(top.h, top.at(tops))
                with act.Fori(0, NU) as s:
                    at = cols(s, STRIP)
                    nc.scalar.activation(scaled[:, at], v[:, at], ACT.Copy, scale=m[:, 2:3]).then_inc(scaled_ok.h, 1)
            for g in range(ng):
                w = min(4, nb - 4 * g)
                act.wait_ge(turned.h, turned.at(g + 1))
                nc.scalar.activation(k.hs[0:rows, 4 * g:4 * g + w, 0, :],
                                     k.bank[g % 4][0:rows, 0:w * P].rearrange("p (a f) -> p a f", f=P), ACT.Copy,
                                     scale=unit).then_inc(hi_ok.h, 1)

        @block.tensor
        def _(pe):
            for g in range(ng):
                w = min(4, nb - 4 * g)
                if scaled is not None:
                    pe.wait_ge(scaled_ok.h, scaled_ok.at(min(NU, -(-(4 * g + w) * rows // STRIP))))
                if lo_ok.due(g - 3):
                    pe.wait_ge(lo_ok.h, lo_ok.at(g - 3))
                for i in range(w):
                    j = 4 * g + i
                    mm = nc.tensor.transpose(k.bank[g % 4][0:rows, i * P:(i + 1) * P],
                                             from_[:, j * rows:(j + 1) * rows], k.idf[:, :])
                mm.then_inc(turned.h, 1)
    k.advance(top=tops, scaled=NU if scaled is not None else 0, turned=ng, hi_ok=ng, lo_ok=ng)


def pool_neighbours(k, over_src, dst, factor, own, tbuf, load_factor, v, layer):
    nc = k.nc
    _, rows, per, halves = table_pieces(k, over_src)
    NH = len(halves)
    assert NH % NBUF == 0
    a_in = [k.sem(f"table_in{b}") for b in range(NBUF)]
    used, acc_full, acc_read, fac_in = k.sem("table_used"), k.sem("acc_full"), k.sem("acc_read"), k.sem("fac_in")
    summed, moved, v_kept = k.sem("layer_summed"), k.sem("layer_moved"), k.sem("v_kept")
    turn = k.sem("turn_pool")
    acc = [k.bank[h] for h in range(2)]
    load_factor = load_factor and factor is not None
    with nc.Block() as block:
        @block.sync
        def _(sp):
            def piece(s, i):
                sp.wait_ge(used.h, used.at(s * NH + i + 1))
                sp.sem_inc(turn.h, 1)
                load_piece(k, sp, over_src, tbuf, s, i)

            for i in range(NBUF, NH):
                piece(0, i)
            with sp.Fori(1, NU) as s:
                for i in range(NH):
                    piece(s, i)

        @block.tensor
        def _(pe):
            def transform(s):
                for h in range(2):
                    pe.wait_ge(moved.h, moved.at(2 * s + h + 1))
                    at = bass.ds(s * STRIP + h * HALF, HALF)
                    nc.tensor.matmul(k.bank[2 + h][:, 0:HALF], layer[0], v[:, at], start=True, stop=False)
                    nc.tensor.matmul(k.bank[2 + h][:, 0:HALF], layer[1], dst[:, at], start=False, stop=True
                                     ).then_inc(summed.h, 1)

            def strip(s, first):
                for i, (t, lo, hi) in enumerate(halves):
                    b = i % NBUF
                    pe.wait_ge(a_in[b].h, a_in[b].at(s * (16 * NH // NBUF) + 16 * (i // NBUF + 1)))
                    for h in range(2):
                        if i == 0:
                            pe.wait_ge(acc_read.h, acc_read.at(s * 2 + h + 1))
                        for r in range(lo, hi):
                            kb = t * per + r
                            for part in range(2):
                                mm = nc.tensor.matmul(
                                    acc[h][:, 0:HALF], k.hs[0:rows, kb, part, :],
                                    tbuf[0:rows, b, r - lo, h * HALF:(h + 1) * HALF],
                                    start=(i == 0 and r == lo and part == 0),
                                    stop=(i == NH - 1 and r == hi - 1 and part == 1))
                        if h == 1:
                            mm.then_inc(used.h, 1)
                        elif i == NH - 1:
                            mm.then_inc(acc_full.h, 1)
                    if i == 1 and layer is not None and not first:
                        transform(s - 1)

            pe.sem_inc(used.h, NBUF)
            if layer is None:
                with pe.Fori(0, NU) as s:
                    strip(s, False)
            else:
                strip(0, True)
                with pe.Fori(1, NU) as s:
                    strip(s, False)
                pe.wait_ge(acc_read.h, acc_read.at(2 * NU + 2))
                transform(NU - 1)

        @block.scalar
        def _(act):
            if load_factor:
                act.wait_ge(used.h, used.at(2 * NBUF))
                act.dma_start(k.C[:, :], k.factors[factor:factor + 1, :].to_broadcast([P, NP])).then_inc(fac_in.h, 16)
            if layer is not None:
                act.sem_inc(moved.h, 2)
                act.wait_ge(v_kept.h, v_kept.at(16))

                def replace(c, b):
                    act.wait_ge(summed.h, summed.at(c + 1))
                    nc.scalar.activation(v[:, cols(c)], k.bank[2 + b][:, 0:CH], layer[2], bias=layer[3]
                                         ).then_inc(moved.h, 1)

                chunk_pairs(act, replace)

        @block.vector
        def _(dve):
            dve.sem_inc(acc_read.h, 2)
            if load_factor:
                dve.wait_ge(fac_in.h, fac_in.at(16))

            def note_peaks(s):
                for h in range(2):
                    dve.wait_ge(moved.h, moved.at(2 * s + h + 3))
                    nc.vector.tensor_reduce(k.peaks[:, bass.ds(2 * s + h, 1)],
                                            v[:, bass.ds(s * STRIP + h * HALF, HALF)], AX, ALU.max)

            def strip(s, first):
                if layer is not None and not first:
                    note_peaks(s - 1)
                for h in range(2):
                    if h == 0:
                        dve.wait_ge(acc_full.h, acc_full.at(s + 1))
                    else:
                        dve.wait_ge(used.h, used.at(s * NH + NH + NBUF))
                    at = bass.ds(s * STRIP + h * HALF, HALF)
                    if own is not None:
                        ins = nc.vector.scalar_tensor_tensor(dst[:, at], acc[h][:, 0:HALF], k.span[:, 3:4],
                                                             own[:, at], ALU.mult, ALU.add)
                    elif factor is None:
                        ins = nc.vector.tensor_scalar(dst[:, at], acc[h][:, 0:HALF], k.span[:, 3:4], None, ALU.mult)
                    else:
                        ins = nc.vector.scalar_tensor_tensor(dst[:, at], acc[h][:, 0:HALF], k.span[:, 3:4],
                                                             k.C[:, at], ALU.mult, ALU.mult)
                    ins.then_inc(acc_read.h, 1)

            strip(0, True)
            with dve.Fori(1, NU) as s:
                strip(s, False)
            if layer is not None:
                note_peaks(NU - 1)

    for b in range(NBUF):
        a_in[b].base += 16 * NU * NH // NBUF
    k.advance(table_used=NU * NH + NBUF, acc_full=NU, acc_read=2 * NU + 2)
    if load_factor:
        k.advance(fac_in=16)
    if layer is not None:
        k.advance(layer_summed=NCH, layer_moved=NCH + 2, v_kept=16)


def overflow(k, table, gather_at, scatter_at, width, values=None, dst=None, factor=False,
             kept=None, layer=None):
    nc = k.nc
    i = k.next()
    sums = k.spill_sums if width == D else k.spill_sums_e
    nrows = NP if values is not None else E
    NZERO = 16 * NS + (16 if dst is None else 0)
    with ExitStack() as ctx:
        def sb(name, shape, dt):
            return ctx.enter_context(nc.sbuf_tensor(f"{name}{i}", shape, dt))

        gidx = sb("gidx", [P, COLS], I32)
        sidx = sb("sidx", [P, COLS], I32)
        gcol = sb("gcol", [P, 1], I32)
        scol = sb("scol", [P, 1], I32)
        put = sb("put", [P, 1], I32)
        scolf = sb("scolf", [P, 1], F32)
        dup = sb("dup", [P, 2], F32)
        rows = sb("rows_g", [P, width], F32)
        old = sb("old", [P, width], F32)
        new = sb("new", [P, width], F32)
        diag = sb("diag", [P, P], F32)
        same = sb("same", [P, P], F32)
        junk = sb("junk_o", [P, P], F32)
        ones = sb("ones", [P, P], F32)
        turnb = sb("turnb", [P, 4, P], F32)
        bank = k.bank

        o_in, o_zero, o_dve, o_pe = k.sem("o_in"), k.sem("o_zero"), k.sem("o_dve"), k.sem("o_pe")
        o_got, o_put = k.sem(f"o_got{i}"), k.sem(f"o_put{i}")
        o_col, o_rows = k.sem("o_col"), k.sem("o_rows")
        o_kept, o_set, o_back, o_T, o_add = (k.sem(n) for n in ("o_kept", "o_set", "o_back", "o_T2", "o_add"))
        o_load, o_summed, o_moved = k.sem("o_load"), k.sem("o_summed"), k.sem("o_moved")
        NV = 5
        NKEEP = NS if values is not None else 0

        with nc.Block() as block:
            @block.sync
            def _(sp):
                n = sp.value_load(k.spill_n[0:1, 0:1], min_val=0, max_val=E)
                with sp.If(n > 0):
                    if kept is not None:
                        sp.dma_start(values[:, :], kept).then_inc(o_load.h, 16)
                    if dst is None:
                        sp.dma_start(k.A[0:DE, :], k.ea_sums[0:DE, :]).then_inc(o_zero.h, 16)
                    sp.dma_start(gidx[:, :], gather_at).then_inc(o_in.h, 16)
                    sp.dma_start(sidx[:, :], scatter_at).then_inc(o_in.h, 16)
                    sp.wait_ge(o_set.h, o_set.at(1))
                    for b in range(NS):
                        sp.dma_start(sums[b * P:(b + 1) * P, :], old[:, :]).then_inc(o_zero.h, 16)
                    for b in range(NKEEP):
                        sp.wait_ge(o_rows.h, o_rows.at(b + 1))
                        sp.dma_start(table[b * P:(b + 1) * P, :], turnb[:, b % 4, :]).then_inc(o_kept.h, 16)
                        sp.wait_ge(o_kept.h, o_kept.at(16 * (b + 1)))
                    sp.wait_ge(o_col.h, o_col.at(COLS + 1))
                    for b in range(NS):
                        if o_add.due(b - 1):
                            sp.wait_ge(o_add.h, o_add.at(b - 1))
                        sp.dma_start(turnb[:, b % 2, 0:width], sums[b * P:(b + 1) * P, :]).then_inc(o_back.h, 16)
                        sp.wait_ge(o_back.h, o_back.at(16 * (b + 1)))
                        sp.sem_inc(o_rows.h, 1)
                    sp.wait_ge(o_add.h, o_add.at(NS))
                    if dst is None:
                        sp.dma_start(k.ea_sums[0:DE, :], k.A[0:DE, :]).then_inc(o_back.h, 16)
                        sp.wait_ge(o_back.h, o_back.at(16 * NS + 16))

            @block.gpsimd
            def _(pool):
                n = pool.value_load(k.spill_n[0:1, 0:1], min_val=0, max_val=E)
                with pool.If(n > 0):
                    g = nc.gpsimd
                    gbound = pool.to_reg(nrows - 1)
                    sbound = pool.to_reg(NP - 1)
                    pool.wait_ge(o_zero.h, o_zero.at(NZERO))
                    if o_kept.due(16 * NKEEP):
                        pool.wait_ge(o_kept.h, o_kept.at(16 * NKEEP))
                    pool.sem_inc(o_col.h, 1)
                    with pool.Fori(0, COLS) as c:
                        pool.wait_ge(o_dve.h, o_dve.at(c * NV + 1))
                        pool.sem_inc(k.sem("turn_o").h, 1)
                        g.indirect_dma_start(out=rows[:, :], out_offset=None, in_=table,
                                             in_offset=bass.IndirectOffsetOnAxis(gcol[:, 0:1], 0),
                                             bounds_check=gbound, oob_is_err=False).then_inc(o_got.h, 16)
                        g.indirect_dma_start(out=old[:, :], out_offset=None, in_=sums,
                                             in_offset=bass.IndirectOffsetOnAxis(scol[:, 0:1], 0),
                                             bounds_check=sbound, oob_is_err=False).then_inc(o_got.h, 16)
                        pool.wait_ge(o_dve.h, o_dve.at(c * NV + NV))
                        pool.sem_inc(k.sem("turn_o").h, 1)
                        g.indirect_dma_start(out=sums, in_=new[:, :], in_offset=None,
                                             out_offset=bass.IndirectOffsetOnAxis(put[:, 0:1], 0),
                                             bounds_check=sbound, oob_is_err=False).then_inc(o_put.h, 16)
                        pool.wait_ge(o_put.h, o_put.at(c * 16 + 16))
                        pool.sem_inc(k.sem("turn_o").h, 1)
                        pool.sem_inc(o_col.h, 1)

            @block.vector
            def _(dve):
                n = dve.value_load(k.spill_n[0:1, 0:1], min_val=0, max_val=E)
                with dve.If(n > 0):
                    V = nc.vector
                    chain, step = k.sem("o_chain"), [0]
                    V.memset(rows[:, :], 0.0)
                    V.memset(ones[:, :], 1.0)
                    V.memset(old[:, :], 0.0).then_inc(o_set.h, 1)
                    dve.wait_ge(o_in.h, o_in.at(32))
                    dve.wait_ge(o_zero.h, o_zero.at(NZERO))
                    for b in range(NKEEP):
                        dve.wait_ge(o_T.h, o_T.at(b + 1))
                        if o_kept.due(16 * (b - 3)):
                            dve.wait_ge(o_kept.h, o_kept.at(16 * (b - 3)))
                        V.tensor_copy(turnb[:, b % 4, :], bank[b % 2][:, 0:P]).then_inc(o_rows.h, 1)
                    with dve.Fori(0, COLS) as c:
                        at = bass.ds(c, 1)
                        dve.wait_ge(o_col.h, o_col.at(c + 1))
                        V.tensor_copy(gcol[:, :], gidx[:, at])
                        V.tensor_copy(scolf[:, :], sidx[:, at])
                        V.tensor_copy(scol[:, :], sidx[:, at]).then_inc(o_dve.h, 1)
                        dve.wait_ge(o_dve.h, o_dve.at(c * NV + 1))
                        V.tensor_scalar(diag[:, :], k.idf[:, :], scolf[:, 0:1], None, ALU.mult).then_inc(o_dve.h, 1)
                        dve.wait_ge(o_pe.h, o_pe.at(c * 2 + 1))
                        V.tensor_scalar(same[:, :], bank[2][:, 0:P], scolf[:, 0:1], None, ALU.is_equal
                                        ).then_inc(o_dve.h, 1)
                        dve.wait_ge(o_dve.h, o_dve.at(c * NV + 3))
                        V.scalar_tensor_tensor(junk[:, :], same[:, :], 1.0, k.tri[:, :], ALU.mult, ALU.mult,
                                               accum_out=dup[:, 0:1]).then_inc(chain.h, 1)
                        dve.wait_ge(chain.h, chain.at(c * 2 + 1))
                        V.tensor_scalar(dup[:, 1:2], dup[:, 0:1], 0.5, BIG, ALU.is_gt, ALU.mult).then_inc(chain.h, 1)
                        dve.wait_ge(chain.h, chain.at(c * 2 + 2))
                        V.tensor_tensor(put[:, :], dup[:, 1:2], scolf[:, :], ALU.add).then_inc(o_dve.h, 1)
                        dve.wait_ge(o_pe.h, o_pe.at(c * 2 + 2))
                        V.tensor_tensor(new[:, :], bank[3][:, 0:width], old[:, :], ALU.add).then_inc(o_dve.h, 1)
                    for b in range(NS):
                        dve.wait_ge(o_T.h, o_T.at(NKEEP + b + 1))
                        at = slice(b * P, (b + 1) * P)
                        t = bank[b % 2][0:width, 0:P]
                        if dst is None:
                            V.tensor_tensor(k.A[0:width, at], k.A[0:width, at], t, ALU.add).then_inc(o_add.h, 1)
                            continue
                        if factor:
                            V.tensor_tensor(junk[:, :], t, k.C[:, at], ALU.mult).then_inc(chain.h, 1)
                        else:
                            V.tensor_copy(junk[:, :], t).then_inc(chain.h, 1)
                        dve.wait_ge(chain.h, chain.at(2 * COLS + b + 1))
                        V.tensor_tensor(dst[:, at], dst[:, at], junk[:, :], ALU.add).then_inc(o_add.h, 1)
                        dve.wait_ge(o_add.h, o_add.at(b + 1))
                    for c in range(NCH if layer is not None else 0):
                        at = slice(c * CH, (c + 1) * CH)
                        dve.wait_ge(o_summed.h, o_summed.at(c + 1))
                        if layer[2] is ACT.Relu:
                            V.tensor_scalar(values[:, at], bank[4 + c % 2][:, 0:CH], layer[3], 0.0, ALU.add, ALU.max
                                            ).then_inc(o_moved.h, 1)
                        else:
                            V.tensor_scalar(values[:, at], bank[4 + c % 2][:, 0:CH], layer[3], None, ALU.add
                                            ).then_inc(o_moved.h, 1)
                        dve.wait_ge(o_moved.h, o_moved.at(c + 1))
                        V.tensor_reduce(k.peaks[:, c:c + 1], values[:, at], AX, ALU.max)

            @block.tensor
            def _(pe):
                n = pe.value_load(k.spill_n[0:1, 0:1], min_val=0, max_val=E)
                with pe.If(n > 0):
                    T = nc.tensor
                    if kept is not None:
                        pe.wait_ge(o_load.h, o_load.at(16))
                    for b in range(NKEEP):
                        if b >= 2:
                            pe.wait_ge(o_rows.h, o_rows.at(b - 1))
                        T.transpose(bank[b % 2][:, 0:P], values[:, b * P:(b + 1) * P], k.idf[:, :]).then_inc(o_T.h, 1)
                    with pe.Fori(0, COLS) as c:
                        pe.wait_ge(o_dve.h, o_dve.at(c * NV + 2))
                        T.matmul(bank[2][:, 0:P], ones[:, :], diag[:, :], start=True, stop=True).then_inc(o_pe.h, 1)
                        pe.wait_ge(o_dve.h, o_dve.at(c * NV + 3))
                        pe.wait_ge(o_got.h, o_got.at(c * 32 + 32))
                        T.matmul(bank[3][:, 0:width], same[:, :], rows[:, :], start=True, stop=True
                                 ).then_inc(o_pe.h, 1)
                    for b in range(NS):
                        pe.wait_ge(o_rows.h, o_rows.at(NKEEP + b + 1))
                        if o_add.due(b - 1):
                            pe.wait_ge(o_add.h, o_add.at(b - 1))
                        T.transpose(bank[b % 2][0:width, 0:P], turnb[:, b % 2, 0:width], k.idf[:, :]
                                    ).then_inc(o_T.h, 1)
                    if layer is not None:
                        pe.wait_ge(o_add.h, o_add.at(NS))
                    for c in range(NCH if layer is not None else 0):
                        at = slice(c * CH, (c + 1) * CH)
                        if c >= 2:
                            pe.wait_ge(o_moved.h, o_moved.at(c - 1))
                        T.matmul(bank[4 + c % 2][:, 0:CH], layer[0], values[:, at], start=True, stop=False)
                        T.matmul(bank[4 + c % 2][:, 0:CH], layer[1], dst[:, at], start=False, stop=True
                                 ).then_inc(o_summed.h, 1)
    k.sem("turn_o")
    k.advance(o_load=16 if kept is not None else 0, o_summed=NCH if layer is not None else 0,
              o_moved=NCH if layer is not None else 0, o_in=32, o_zero=NZERO, o_dve=NV * COLS, o_pe=2 * COLS,
              o_col=COLS + 1, o_rows=NKEEP + NS, o_kept=16 * NKEEP, o_set=1,
              o_back=16 * NS + (16 if dst is None else 0), o_T2=NKEEP + NS, o_add=NS, o_chain=2 * COLS +
              (0 if dst is None else NS))


def elu_stage(k, sums, factor, bias, dst):
    nc = k.nc
    scaled, low, exped = k.sem("elu_scaled"), k.sem("elu_low"), k.sem("elu_exp")
    with nc.Block() as block:
        @block.vector
        def _(dve):
            V = nc.vector
            with dve.Fori(0, NU) as s:
                at = cols(s, STRIP)
                V.tensor_tensor(sums[:, at], sums[:, at], factor[:, at], ALU.mult).then_inc(scaled.h, 1)
            with dve.Fori(0, NU) as s:
                at = cols(s, STRIP)
                dve.wait_ge(scaled.h, scaled.at(s + 1))
                V.tensor_scalar(dst[:, at], sums[:, at], bias, 0.0, ALU.add, ALU.min).then_inc(low.h, 1)
            with dve.Fori(0, NU) as s:
                at = cols(s, STRIP)
                dve.wait_ge(exped.h, exped.at(s + 1))
                V.scalar_tensor_tensor(dst[:, at], dst[:, at], -1.0, sums[:, at], ALU.add, ALU.add)

        @block.scalar
        def _(act):
            with act.Fori(0, NU) as s:
                at = cols(s, STRIP)
                act.wait_ge(low.h, low.at(s + 1))
                nc.scalar.activation(sums[:, at], sums[:, at], ACT.Relu, bias=bias)
                nc.scalar.activation(dst[:, at], dst[:, at], ACT.Exp).then_inc(exped.h, 1)
    k.advance(elu_scaled=NU, elu_low=NU, elu_exp=NU)


def load_factor_row(k, row):
    with k.nc.Block() as block:
        @block.sync
        def _(sp):
            sp.dma_start(k.C[:, :], k.factors[row:row + 1, :].to_broadcast([P, NP])).then_inc(k.sem("row_in").h, 16)
    k.advance(row_in=16)


def load_ea(k, into, wait=False):
    nc = k.nc
    got = k.sem("easum_in")
    with nc.Block() as block:
        @block.sync
        def _(sp):
            if wait:
                sp.wait_ge(got.h, got.at(16))
            else:
                sp.dma_start(into[0:3 * DE, :], k.ea_sums).then_inc(got.h, 16)


def store_start(k, kept, v):
    with k.nc.Block() as block:
        @block.sync
        def _(sp):
            sp.dma_start(kept, v).then_inc(k.sem("kept").h, 16)
    k.advance(kept=16)


def wait_kept(k):
    kept, slots_init = k.sem("kept"), k.sem("slots_init")
    with k.nc.Block() as block:
        @block.sync
        def _(sp):
            sp.wait_ge(slots_init.h, slots_init.at(16 * (NBKT // 98)))
            sp.wait_ge(kept.h, kept.at(0))


def start_back(k):
    with k.nc.Block() as block:
        @block.sync
        def _(sp):
            sp.dma_start(k.B[:, :], k.pooled).then_inc(k.sem("b_in").h, 16)

        @block.scalar
        def _(act):
            act.dma_start(k.C[:, :], k.factors[0:1, :].to_broadcast([P, NP])).then_inc(k.sem("c_in").h, 16)


def load_back(k):
    nc = k.nc
    b_in, c_in = k.sem("b_in"), k.sem("c_in")
    with nc.Block() as block:
        @block.sync
        def _(sp):
            sp.dma_start(k.A[:, :], k.x_kept).then_inc(k.sem("back").h, 16)

        @block.vector
        def _(dve):
            dve.wait_ge(b_in.h, b_in.at(16))
            dve.wait_ge(c_in.h, c_in.at(16))
            with dve.Fori(0, NU) as s:
                at = cols(s, STRIP)
                nc.vector.tensor_tensor(k.B[:, at], k.B[:, at], k.C[:, at], ALU.mult)


def wait_back(k):
    back = k.sem("back")
    with k.nc.Block() as block:
        @block.sync
        def _(sp):
            sp.wait_ge(back.h, back.at(16))


def program(nc, w, out):
    with ExitStack() as ctx:
        k = Core(nc, ctx)

        def sb(name, shape, dt):
            return ctx.enter_context(nc.sbuf_tensor(name, shape, dt))

        k.iota = sb("iota", [P, 256], BF16)
        k.id16 = sb("id16", [P, P], F16)
        k.idb = sb("idb", [P, P], BF16)
        k.idf = sb("idf", [P, P], F32)
        k.tri = sb("tri", [P, P], F32)
        k.avg = sb("avg", [P, P], F32)
        k.eps = sb("eps", [P, 1], F32)
        k.gather = sb("gather", [P, NCH, NCH], F32)
        k.spread = sb("spread", [NCH, NCH, D], F32)
        k.zero = sb("zero", [P, 1], F32)
        k.slots = nc.dram_tensor("slots", [NBKT * CAP, PW], F32).ap()
        k.factors = nc.dram_tensor("factors", [3, NP], F32).ap()
        k.counts_ds = nc.dram_tensor("counts_ds", [NU * NU, DST_H, 2 * UD, STRIP], F16).ap()
        k.counts_sd = nc.dram_tensor("counts_sd", [NU * NU, P, US, STRIP], F16).ap()
        k.ea_sums = nc.dram_tensor("ea_sums", [3 * DE, NP], F32).ap()
        k.spill_src = nc.dram_tensor("spill_src", [P, COLS], I32).ap()
        k.spill_dst = nc.dram_tensor("spill_dst", [P, COLS], I32).ap()
        k.spill_edge = nc.dram_tensor("spill_edge", [P, COLS], I32).ap()
        k.spill_n = nc.dram_tensor("spill_n", [1, 1], I32).ap()
        k.spill_rows = nc.dram_tensor("spill_rows", [NP, D], F32).ap()
        k.spill_sums = nc.dram_tensor("spill_sums", [NP, D], F32).ap()
        k.spill_sums_e = nc.dram_tensor("spill_sums_e", [NP, DE], F32).ap()
        k.x_kept = nc.dram_tensor("x_kept", [P, NP], F32).ap()
        k.h_kept = nc.dram_tensor("h_kept", [P, NP], F32).ap()
        k.hs_kept = nc.dram_tensor("hs_kept", [DST_H, NP // DST_H, 2, P], F16).ap()
        k.pooled = nc.dram_tensor("pooled", [P, NP], F32).ap()
        constants(k)
        k.weights = sb("weights", [P, 20, D], F32)
        k.vectors = sb("vectors", [P, 32], F32)
        k.raw = sb("raw", [P, 5, D], F32)
        k.raw_e = sb("raw_e", [P, 3 * DE], F32)
        k.rows = sb("rows", [26, D], F32)
        k.span = sb("span", [P, 4], F32)
        k.rstd = sb("rstd", [NCH, CH], F32)
        with ExitStack() as early:
            k.A, k.B, k.H = (early.enter_context(nc.sbuf_tensor(f"{n}_early", [P, NP], F32)) for n in "ABH")
            k.hs = early.enter_context(nc.sbuf_tensor("hs_early", [P, NP // DST_H, 2, P], F16))
            k.empty = early.enter_context(nc.sbuf_tensor("empty", [P, 98, PW], F32))
            k.bank = [early.enter_context(nc.psum_tensor(f"early{i}", [P, 512], F32)) for i in range(8)]
            start_x_and_slots(k, w["x"])
            turn_x(k)
            store_start(k, k.x_kept, k.A[:, :])
            layer_norm(k, k.A, k.H, k.B)
            store_start(k, k.h_kept, k.H[:, :])
            split_rows(k, k.H, False, False, None)
            store_start(k, k.hs_kept, k.hs[0:DST_H, :, :, :])
            wait_kept(k)
        rank_edges(k, w["src"], w["dst"], w["edge_attr_32"], small_loads(k, w))

        k.hs = sb("hs", [P, NP // DST_H, 2, P], F16)
        k.bn_stats = sb("bn_stats", [P, NCH, 6], F32)
        k.bn_mv = sb("bn_mv", [P, 8], F32)
        k.peaks = sb("peaks", [P, NCH], F32)
        build_adjacency(k)

        k.A, k.B, k.C, k.H = (sb(n, [P, NP], F32) for n in "ABCH")
        k.bank = [ctx.enter_context(nc.psum_tensor(f"acc{i}", [P, 512], F32)) for i in range(8)]
        A, B, C, H, W, vec = k.A, k.B, k.C, k.H, k.W, k.vec
        start_back(k)
        overflow(k, w["edge_attr_32"], k.spill_edge, k.spill_dst, DE)

        turn_weights(k)

        load_back(k)
        for l in range(2):
            v0 = 6 * l
            if l:
                split_and_pool(k, H, False, B, B, 0, load_factor=False)
            overflow(k, k.spill_rows, k.spill_dst, k.spill_src, D, H, B, True, kept=None if l else k.h_kept)
            product(k, [(W["ab"[l] + "0"], B)], B, ACT.Identity, vec(v0), stats=True)
            batch_norm_relu(k, B, vec(v0 + 1), vec(v0 + 2))
            product(k, [(W["ab"[l] + "1"], B)], H, ACT.Identity, vec(v0 + 3), stats=True)
            batch_norm_relu(k, H, vec(v0 + 4), vec(v0 + 5))

        wait_back(k)
        layer_norm(k, A, H, B, add=True)
        for l in range(4):
            layer = (W[f"self{l}"], W[f"neigh{l}"], ACT.Relu if l < 3 else ACT.Identity, vec(12 + l))
            split_and_pool(k, H, True, B if l else None, B, 1, load_factor=(l == 0), peaks=True, layer=layer)
            overflow(k, k.spill_rows, k.spill_src, k.spill_dst, D, H, B, True, kept=k.h_kept, layer=layer)

        layer_norm(k, A, H, B, add=True)
        load_ea(k, C)
        split_and_pool(k, H, True, None, B, None)
        overflow(k, k.spill_rows, k.spill_src, k.spill_dst, D, H, B)
        load_ea(k, C, wait=True)
        product(k, [(W["msg"], B), (W["msg_e"], C[0:3 * DE])], B, ACT.Identity, k.zero[:, 0:1])
        product(k, [(W["up_h"], H), (W["up_m"], B)], C, ACT.Relu, vec(16))
        layer_norm(k, C, B, C, vec(17), vec(18))
        product(k, [(W["down"], B)], C, ACT.Relu, vec(19))
        layer_norm(k, C, B, C, vec(20), vec(21))
        product(k, [(W["node"], H), (k.idf[:, :], B)], C, ACT.Identity, k.zero[:, 0:1])
        layer_norm(k, C, H, C, vec(22), vec(23))

        load_factor_row(k, 2)
        layer_norm(k, A, H, B, add=True)
        for l in range(2):
            product_times(k, W[f"g{l}"], H, C)
            split_and_pool(k, H, True, B, B, None, own=H, signed=True)
            overflow(k, k.spill_rows, k.spill_src, k.spill_dst, D, H, B)
            elu_stage(k, B, C, vec(24 + l), H)
        residual(k, H)
        store_out(k, out)


_INS = ['x', 'src', 'dst', 'edge_attr_32',
        'L0_gnn_l0_W0', 'L0_gnn_l0_b0', 'L0_gnn_l0_W1', 'L0_gnn_l0_b1',
        'L0_gnn_l0_mbn_g', 'L0_gnn_l0_mbn_b', 'L0_gnn_l0_bn_g', 'L0_gnn_l0_bn_b',
        'L0_gnn_l1_W0', 'L0_gnn_l1_b0', 'L0_gnn_l1_W1', 'L0_gnn_l1_b1',
        'L0_gnn_l1_mbn_g', 'L0_gnn_l1_mbn_b', 'L0_gnn_l1_bn_g', 'L0_gnn_l1_bn_b',
        'L1_gnn_W_self', 'L1_gnn_W_neigh', 'L1_gnn_bias',
        'L2_gnn_W_message', 'L2_gnn_W_node', 'L2_gnn_W1', 'L2_gnn_b1', 'L2_gnn_ln1_g', 'L2_gnn_ln1_b',
        'L2_gnn_W2', 'L2_gnn_b2', 'L2_gnn_ln2_g', 'L2_gnn_ln2_b', 'L2_gnn_ln_g', 'L2_gnn_ln_b',
        'L3_gnn_W1', 'L3_gnn_b1', 'L3_gnn_W2', 'L3_gnn_b2']


def kernel(**inputs):
    import numpy as _np
    import concourse.bacc as _bacc
    from concourse import mybir as _mybir
    from concourse.bass_utils import run_bass_kernel_spmd as _run

    nc = _bacc.Bacc("TRN2", target_bir_lowering=False, num_devices=1)
    arrays, args = {}, {}
    for name in _INS:
        a = _np.ascontiguousarray(inputs[name])
        arrays[f"in_{name}_dram"] = a
        args[name] = nc.dram_tensor(f"in_{name}_dram", a.shape, _mybir.dt.from_np(a.dtype), kind="ExternalInput").ap()
    out = nc.dram_tensor("out_0_dram", (N, D), _mybir.dt.float32, kind="ExternalOutput").ap()
    program(nc, args, out)
    r = _run(nc, [arrays], core_ids=[0])
    return r.results[0]["out_0_dram"]
```
